# Optimizing a Trainium2 kernel written in Bass

```python
import numpy as np
import jax
import jax.numpy as jnp

def _softmax(x, axis=-1):
    return jax.nn.softmax(x, axis=axis)

def _gelu(x):
    return jax.nn.gelu(x, approximate=True)

def _silu(x):
    return jax.nn.silu(x)

def _sigmoid(x):
    return jax.nn.sigmoid(x)

def _layernorm(x, axis=-1, eps=1e-05):
    m = jnp.mean(x, axis=axis, keepdims=True)
    v = jnp.var(x, axis=axis, keepdims=True)
    return (x - m) / jnp.sqrt(v + eps)

def _scatter_add(tgt, idx, src, axis=0):
    return tgt.at[idx].add(src)

def _segment_sum(src, seg, n):
    return jax.ops.segment_sum(src, seg, n)
kernel_name = 'mk_lm_tower_d1_tok_ids1024_r4_c5c45f'

def setup_inputs(seed: int=0):
    np.random.seed(seed)
    _w = jnp.asarray

    def _rec_inputs():
        import jax
        import jax.numpy as jnp
        _rk = jax.random.key(seed)
        x = jax.random.randint(jax.random.fold_in(_rk, 1), (64, 128), 0, 12500, jnp.int32)
        return x
    x = _rec_inputs()

    def _L0_tok_setup():
        import jax, jax.numpy as jnp
        import numpy as np
        VOCAB = 12500
        EMBED_DIM = 256
        HALF = EMBED_DIM // 2
        BATCH, SEQ = (32, 512)
        key = jax.random.key(seed)
        ks = jax.random.split(key, 7)
        token_ids = jax.random.randint(ks[0], (BATCH, SEQ), 0, VOCAB)
        token_table = jax.random.normal(ks[1], (VOCAB, HALF), dtype=jnp.float32)
        op_table = jax.random.normal(ks[2], (10, HALF), dtype=jnp.float32)
        var_table = jax.random.normal(ks[3], (10, HALF), dtype=jnp.float32)
        const_table = jax.random.normal(ks[4], (10, HALF), dtype=jnp.float32)
        struct_table = jax.random.normal(ks[5], (10, HALF), dtype=jnp.float32)
        special_table = jax.random.normal(ks[6], (VOCAB - 40, HALF), dtype=jnp.float32)
        return {'token_ids': token_ids, 'token_table': token_table, 'op_table': op_table, 'var_table': var_table, 'const_table': const_table, 'struct_table': struct_table, 'special_table': special_table}
    _L0_tok_all = _L0_tok_setup()
    _L0_tok_in = {k: v for k, v in _L0_tok_all.items() if k in ('token_table', 'op_table', 'var_table', 'const_table', 'struct_table', 'special_table')}
    del _L0_tok_all

    def _L0_attn_setup():
        import jax, jax.numpy as jnp
        import numpy as np
        B, S, E, H = (4, 1024, 256, 16)
        D = E // H

        def _phi(x):
            return jax.nn.elu(x) + 1.0
        key = jax.random.key(seed)
        k1, k2, k3 = jax.random.split(key, 3)
        x = jax.random.normal(k1, (B, S, E), dtype=jnp.float32)
        W_qkv = jax.random.normal(k2, (E, 3 * E), dtype=jnp.float32) * E ** (-0.5)
        b_qkv = jnp.zeros((3 * E,), dtype=jnp.float32)
        W_proj = jax.random.normal(k3, (E, E), dtype=jnp.float32) * E ** (-0.5)
        b_proj = jnp.zeros((E,), dtype=jnp.float32)
        return {'x': x, 'W_qkv': W_qkv, 'b_qkv': b_qkv, 'W_proj': W_proj, 'b_proj': b_proj}
    _L0_attn_all = _L0_attn_setup()
    _L0_attn_in = {k: v for k, v in _L0_attn_all.items() if k in ('W_qkv', 'b_qkv', 'W_proj', 'b_proj')}
    del _L0_attn_all

    def _L0_ffn_setup():
        import jax, jax.numpy as jnp
        import numpy as np
        import math
        HID, HD, E, MIN_E = (256, 128, 16, 2)
        B, T = (4, 512)
        IS_CAUSAL = True

        def _l2norm(x, axis):
            return x / jnp.sqrt(jnp.sum(x * x, axis=axis, keepdims=True) + 1e-12)

        def _gating(hidden_states, sim_matrix, gates):
            b, t, c = hidden_states.shape
            flat = hidden_states.reshape(b * t, c)
            logits = _l2norm(flat, -1) @ _l2norm(sim_matrix, 0) - jax.nn.sigmoid(gates)
            gated = jax.nn.relu(logits)
            mask = (gated > 0).astype(gated.dtype)
            inactive = jnp.sum(mask, axis=1) == 0
            _, top_idx = jax.lax.top_k(logits, MIN_E)
            fb = jnp.sum(jax.nn.one_hot(top_idx, E, dtype=mask.dtype), axis=1)
            mask = mask + inactive[:, None].astype(mask.dtype) * fb
            masked = jnp.where(mask > 0, gated, -jnp.inf)
            probs = jax.nn.softmax(masked, axis=-1)
            return probs
        key = jax.random.key(seed)
        ks = jax.random.split(key, 6)
        a_qkv = math.sqrt(6.0 / (HID + HD))
        a_o = math.sqrt(6.0 / (HD + HID))
        return {'hidden_states': jax.random.normal(ks[0], (B, T, HID), jnp.float32), 'sim_matrix': jax.random.normal(ks[1], (HID, E), jnp.float32), 'gates': jnp.zeros((E,), jnp.float32), 'q_proj': jax.random.uniform(ks[2], (E, HID, HD), jnp.float32, -a_qkv, a_qkv), 'k_proj': jax.random.uniform(ks[3], (E, HID, HD), jnp.float32, -a_qkv, a_qkv), 'v_proj': jax.random.uniform(ks[4], (E, HID, HD), jnp.float32, -a_qkv, a_qkv), 'o_proj': jax.random.uniform(ks[5], (E, HD, HID), jnp.float32, -a_o, a_o)}
    _L0_ffn_all = _L0_ffn_setup()
    _L0_ffn_in = {k: v for k, v in _L0_ffn_all.items() if k in ('sim_matrix', 'gates', 'q_proj', 'k_proj', 'v_proj', 'o_proj')}
    del _L0_ffn_all
    return {'x': x, 'L0_tok_token_table': _L0_tok_in['token_table'], 'L0_tok_op_table': _L0_tok_in['op_table'], 'L0_tok_var_table': _L0_tok_in['var_table'], 'L0_tok_const_table': _L0_tok_in['const_table'], 'L0_tok_struct_table': _L0_tok_in['struct_table'], 'L0_tok_special_table': _L0_tok_in['special_table'], 'L0_attn_W_qkv': _L0_attn_in['W_qkv'], 'L0_attn_b_qkv': _L0_attn_in['b_qkv'], 'L0_attn_W_proj': _L0_attn_in['W_proj'], 'L0_attn_b_proj': _L0_attn_in['b_proj'], 'L0_ffn_sim_matrix': _L0_ffn_in['sim_matrix'], 'L0_ffn_gates': _L0_ffn_in['gates'], 'L0_ffn_q_proj': _L0_ffn_in['q_proj'], 'L0_ffn_k_proj': _L0_ffn_in['k_proj'], 'L0_ffn_v_proj': _L0_ffn_in['v_proj'], 'L0_ffn_o_proj': _L0_ffn_in['o_proj']}

def reference(x, L0_tok_token_table, L0_tok_op_table, L0_tok_var_table, L0_tok_const_table, L0_tok_struct_table, L0_tok_special_table, L0_attn_W_qkv, L0_attn_b_qkv, L0_attn_W_proj, L0_attn_b_proj, L0_ffn_sim_matrix, L0_ffn_gates, L0_ffn_q_proj, L0_ffn_k_proj, L0_ffn_v_proj, L0_ffn_o_proj):
    import jax
    import jax.numpy as jnp

    def _L0_tok_ref(token_ids, token_table, op_table, var_table, const_table, struct_table, special_table):
        import jax, jax.numpy as jnp
        import numpy as np
        VOCAB = 12500
        EMBED_DIM = 256
        HALF = EMBED_DIM // 2
        BATCH, SEQ = (32, 512)
        token_embeds = token_table[token_ids]
        cat_table = jnp.concatenate([op_table, var_table, const_table, struct_table, special_table], axis=0)
        category_embeds = cat_table[token_ids]
        return jnp.concatenate([token_embeds, category_embeds], axis=-1)

    def _L0_attn_ref(x, W_qkv, b_qkv, W_proj, b_proj):
        import jax, jax.numpy as jnp
        import numpy as np
        B, S, E, H = (4, 1024, 256, 16)
        D = E // H

        def _phi(x):
            return jax.nn.elu(x) + 1.0
        b, s, _ = x.shape
        qkv = (x @ W_qkv + b_qkv).reshape(b, s, 3, H, D)
        q, k, v = (qkv[:, :, 0], qkv[:, :, 1], qkv[:, :, 2])
        pq, pk = (_phi(q), _phi(k))
        kv = jnp.einsum('bshd,bshm->bhmd', pk, v)
        z = 1.0 / (jnp.einsum('bshd,bhd->bsh', pq, pk.sum(axis=1)) + 1e-06)
        attn = jnp.einsum('bshd,bhmd,bsh->bshm', pq, kv, z)
        attn = attn.reshape(b, s, H * D)
        _proj = attn @ W_proj + b_proj
        return attn

    def _L0_ffn_ref(hidden_states, sim_matrix, gates, q_proj, k_proj, v_proj, o_proj):
        import jax, jax.numpy as jnp
        import numpy as np
        import math
        HID, HD, E, MIN_E = (256, 128, 16, 2)
        B, T = (4, 512)
        IS_CAUSAL = True

        def _l2norm(x, axis):
            return x / jnp.sqrt(jnp.sum(x * x, axis=axis, keepdims=True) + 1e-12)

        def _gating(hidden_states, sim_matrix, gates):
            b, t, c = hidden_states.shape
            flat = hidden_states.reshape(b * t, c)
            logits = _l2norm(flat, -1) @ _l2norm(sim_matrix, 0) - jax.nn.sigmoid(gates)
            gated = jax.nn.relu(logits)
            mask = (gated > 0).astype(gated.dtype)
            inactive = jnp.sum(mask, axis=1) == 0
            _, top_idx = jax.lax.top_k(logits, MIN_E)
            fb = jnp.sum(jax.nn.one_hot(top_idx, E, dtype=mask.dtype), axis=1)
            mask = mask + inactive[:, None].astype(mask.dtype) * fb
            masked = jnp.where(mask > 0, gated, -jnp.inf)
            probs = jax.nn.softmax(masked, axis=-1)
            return probs
        b, t, c = hidden_states.shape
        rw = _gating(hidden_states, sim_matrix, gates).reshape(b, t, E)
        q = jnp.einsum('btc,ech,bte->bth', hidden_states, q_proj, rw)
        k = jnp.einsum('btc,ech,bte->bth', hidden_states, k_proj, rw)
        v = jnp.einsum('btc,ech,bte->bth', hidden_states, v_proj, rw)
        scale = 1.0 / math.sqrt(HD)
        scores = jnp.einsum('bqh,bkh->bqk', q, k) * scale
        if IS_CAUSAL:
            causal = jnp.tril(jnp.ones((t, t), dtype=bool))
            scores = jnp.where(causal[None], scores, -jnp.inf)
        attn = jax.nn.softmax(scores, axis=-1)
        ao = jnp.einsum('bqk,bkh->bqh', attn, v)
        out = jnp.einsum('bth,ehc,bte->btc', ao, o_proj, rw)
        return out
    h = _L0_tok_ref(x, L0_tok_token_table, L0_tok_op_table, L0_tok_var_table, L0_tok_const_table, L0_tok_struct_table, L0_tok_special_table)
    h = h + _L0_attn_ref(_layernorm(h, axis=-1), L0_attn_W_qkv, L0_attn_b_qkv, L0_attn_W_proj, L0_attn_b_proj)
    h = h + _L0_ffn_ref(_layernorm(h, axis=-1), L0_ffn_sim_matrix, L0_ffn_gates, L0_ffn_q_proj, L0_ffn_k_proj, L0_ffn_v_proj, L0_ffn_o_proj)
    return h

_drawn_inputs = setup_inputs


def setup_inputs(seed=0):
    import zlib

    import numpy as np

    out = dict(_drawn_inputs(seed))
    spreads = {'L0_attn_b_qkv': (0.0, 0.1), 'L0_attn_b_proj': (0.0, 0.1), 'L0_ffn_gates': (0.0, 0.1)}
    factors = {'L0_tok_op_table': 3.738,
     'L0_tok_var_table': 4.105,
     'L0_tok_const_table': 2.805,
     'L0_tok_struct_table': 3.463}
    for name, (base, spread) in spreads.items():
        noise = np.random.default_rng([zlib.crc32(name.encode()), seed]).standard_normal(out[name].shape)
        drawn = base * np.exp(spread * noise) if base else spread * noise
        out[name] = jnp.asarray(drawn.astype(out[name].dtype))
    for name, factor in factors.items():
        out[name] = (out[name] * factor).astype(out[name].dtype)
    return out
```

```python
from contextlib import ExitStack

import concourse.bass as bass
from concourse import mybir

F32 = mybir.dt.float32
F32R = mybir.dt.float32r
I32 = mybir.dt.int32
U32 = mybir.dt.uint32
ALU = mybir.AluOpType
ACT = mybir.ActivationFunctionType
AX_X = mybir.AxisListType.X

P = 128
FIRST = 3
LN_EPS = 1e-5
NORM_EPS = 1e-12
DEN_EPS = 1e-6
MASKED = -1.0e30

A_STEPS = ["ids_picked", "ln1_stats", "ln1_moments", "ln1_var_eps", "ln1_rstd", "x1_normed", "x1_turned",
           "x1T_hi", "x1T_lo", "qk_product", "v_product", "qk_biased", "v_biased", "qk_negative", "qk_exp",
           "phi", "phi_q_turned", "kv_product", "phi_q_T", "kv_masked", "attn_sums", "attn_den", "attn_z",
           "attn", "h2", "ln2_stats", "ln2_moments", "ln2_var_eps", "ln2_rstd", "x2_normed", "x2_energy",
           "x2_energy_eps", "x2_inverse_norm", "x2_turned", "x2T_hi", "x2T_lo", "logits_product", "logits",
           "top_values", "top_indices", "is_first", "top_two", "gate_flags", "gate_mask", "gate_negmax",
           "gate_exp", "gate_sum", "gate_rsum", "routing"]
C_STEPS = ["heads_turned", "heads_T", "scores", "scores_masked", "scores_negmax", "probs", "probs_rsum",
           "o_weights", "probs_turned", "probs_T", "ao_product", "aoT_hi", "aoT_lo", "out_sum"]


class Tile:

    def __init__(self, t, half, parity):
        self.t, self.half, self.p = t, half, parity

    def shift(self, k):
        q = self.p + k
        return Tile(self.t + k, self.half + q // 2, q % 2)

    def ahead(self, j):
        return Tile(j * 2 + self.t, j + self.half, self.p)

    @property
    def exists(self):
        return not (isinstance(self.t, int) and self.t < 0)


def tile_at(t):
    return Tile(t, t // 2, t % 2)


def build(nc, x, token_table, op_table, var_table, const_table, struct_table, special_table,
          W_qkv, b_qkv, W_proj, b_proj, sim_matrix, gates, q_proj, k_proj, v_proj, o_proj, out):
    B, T = x.shape
    HALF = token_table.shape[1]
    C = 2 * HALF
    CH = C // P
    E = gates.shape[0]
    HD = q_proj.shape[2]
    D = 16
    HG = P // D
    G = C // P
    KVW = P + 2
    NUMW = P + HG
    N_SMALL = sum(t.shape[0] for t in (op_table, var_table, const_table, struct_table))
    N_SPECIAL = special_table.shape[0]
    SCALE = float(HD) ** -0.5
    OSLOT = E // 2
    assert T == P and HD == P and C == 2 * P and E == 16

    NSTAGE = 3
    STAGE = CH * 3 * C
    QKV_E, O_E = 2, 4
    NQ, NO = E // QKV_E, E // O_E
    ROUNDS = [("attn", 0)] + [("qkv", r) for r in range(NQ)] + [("o", r) for r in range(NO)]
    EBANK = [e % 3 for e in range(E - 1)] + [1]

    def bank_before(e):
        for back in range(1, E + 1):
            if EBANK[(e - back) % E] == EBANK[e]:
                return (e - back) % E, 0 if back <= e else 1

    small = nc.dram_tensor("small_table", [N_SMALL, HALF], F32, kind="Internal").ap()

    with ExitStack() as ctx:
        def sb(name, shape, dt=F32):
            return ctx.enter_context(nc.sbuf_tensor(name, shape, dt))

        def sem(name):
            return ctx.enter_context(nc.semaphore(name))

        ident = sb("ident", [P, P])
        causal = sb("causal", [P, P])
        head_mask = sb("head_mask", [P, P])
        head_of_row = sb("head_of_row", [P, HG])
        ones = sb("ones", [P, P])
        minus_half = sb("minus_half", [P, E])
        expert_no = sb("expert_no", [P, E])
        eps = sb("eps", [P, 2])
        bias = sb("bias", [P, 3 * C])
        gate_bias = sb("gate_bias", [P, E])
        gate_tmp = sb("gate_tmp", [P, E])
        ids_rows = sb("ids_rows", [B, T], I32)
        ids_rows_f = sb("ids_rows_f", [B, T])
        ids_f = sb("ids_f", [P, B])
        ids_low = sb("ids_low", [P, B])
        ids = sb("ids", [P, B, 2], U32)
        ids_now = [sb(f"ids_now{p}", [P, 2], U32) for p in range(2)]
        stage = [sb(f"stage{s}", [P, STAGE]) for s in range(NSTAGE)]
        wa = [sb(f"wa_{n}", [P, CH, 3 * C], F32R) for n in ("hi", "lo")]
        wq = [sb(f"wq_{n}", [P, E, CH, 3 * HD], F32R) for n in ("hi", "lo")]
        wo = [sb(f"wo_{n}", [P, E, C], F32R) for n in ("hi", "lo")]
        sim = sb("sim", [P, CH, E])
        sim_sq = sb("sim_sq", [P, CH, E])
        sim_norm = sb("sim_norm", [P, E])
        sim_inv = sb("sim_inv", [P, E])
        simn = sb("simn", [P, CH, E])
        ws = [sb(f"ws_{n}", [P, CH, E], F32R) for n in ("hi", "lo")]
        h = [sb(f"h{p}", [P, C]) for p in range(2)]
        h2 = [sb(f"h2_{p}", [P, C]) for p in range(2)]
        stats = sb("stats", [P, 2, 6])
        mv = sb("mv", [P, 2, 2])
        var_eps = sb("var_eps", [P, 2])
        rstd = sb("rstd", [P, 2])
        x1 = sb("x1", [P, C])
        x2 = sb("x2", [P, C])
        x1T = [sb(f"x1T_{n}", [P, CH, P], F32R) for n in ("hi", "lo")]
        x2T = [[sb(f"x2T_{n}{p}", [P, CH, P], F32R) for n in ("hi", "lo")] for p in range(2)]
        qk = sb("qk", [P, 2 * C])
        qk_neg = sb("qk_neg", [P, 2 * C])
        qk_e = sb("qk_e", [P, 2 * C])
        phi = sb("phi", [P, 2 * C])
        vx = sb("vx", [P, G, KVW])
        pqT = sb("pqT", [P, G, P])
        kvm = sb("kvm", [P, G, NUMW])
        den = sb("den", [P, G, HG])
        zden = sb("zden", [P, G, HG])
        attn = sb("attn", [P, C])
        squares = sb("squares", [P, C])
        energy = sb("energy", [P, 2])
        inv_norm = sb("inv_norm", [P, 1])
        logits = sb("logits", [P, E])
        top = sb("top", [P, 8])
        top_at = sb("top_at", [P, 8], U32)
        is_first = sb("is_first", [P, E])
        top_two = sb("top_two", [P, E])
        idle = sb("idle", [P, 1])
        active = sb("active", [P, E])
        gated = sb("gated", [P, E])
        gmask = sb("gmask", [P, E])
        gneg = sb("gneg", [P, 1])
        gexp = sb("gexp", [P, E])
        gsel = sb("gsel", [P, E])
        gsum = sb("gsum", [P, 2])
        rw = [sb(f"rw{p}", [P, E]) for p in range(2)]
        qkv = [sb(f"qkv{p}", [P, 3 * HD]) for p in range(2)]
        headsT = sb("headsT", [P, 2, P])
        sc = sb("sc", [P, P])
        sneg = sb("sneg", [P, 1])
        pr = sb("pr", [P, P])
        psumm = sb("psumm", [P, 2])
        prT = sb("prT", [P, P])
        aoT = [sb(f"aoT_{n}", [P, P], F32R) for n in ("hi", "lo")]
        rwo = [sb(f"rwo{p}", [P, E]) for p in range(2)]
        o_part = [sb(f"o_part{b}", [P, 2, C]) for b in range(2)]
        acc_v = sb("acc_v", [P, C])
        acc_p = sb("acc_p", [P, C])
        result = [sb(f"result{p}", [P, C]) for p in range(2)]

        banks = [ctx.enter_context(nc.psum_tensor(f"bank{b}", [P, 512], F32)) for b in range(8)]
        ps_e = banks[0:3]
        ps_o = banks[3:5]
        ps_a, ps_b, ps_c = banks[5:8]
        ps_sums = ps_a[:, 0:G * NUMW].rearrange("p (g n) -> p g n", g=G)
        ps_kv = ps_b[:, 0:G * KVW].rearrange("p (g n) -> p g n", g=G)

        done = {s: sem(s) for s in A_STEPS + C_STEPS}
        expert_product = [sem(f"expert_product{e}") for e in range(E)]
        expert_added = [sem(f"expert_added{e}") for e in range(E)]
        o_product = [sem(f"o_product{s}") for s in range(OSLOT)]
        o_scaled = {s: sem(f"o_scaled{s}") for s in range(0, OSLOT, 2)}
        o_pooled = {s: [sem(f"o_pooled{s}_{j}") for j in range(2)] for s in range(0, OSLOT, 2)}
        o_added = {s: [sem(f"o_added{s}_{j}") for j in range(2)] for s in range(1, OSLOT, 2)}
        rows_gathered = [sem(f"rows_gathered{p}") for p in range(2)]
        special_gathered = [sem(f"special_gathered{p}") for p in range(2)]
        stored = [sem(f"stored{p}") for p in range(2)]
        stage_loaded = [sem(f"stage_loaded{s}") for s in range(NSTAGE)]
        split_hi = sem("split_hi")
        split_lo = sem("split_lo")
        small_loaded = sem("small_loaded")
        inputs_loaded = sem("inputs_loaded")
        consts_base = sem("consts_base")
        consts_ready = sem("consts_ready")
        setup_v = sem("setup_v")
        setup_p = sem("setup_p")
        setup_own = sem("setup_own")
        setup_a = sem("setup_a")
        setup_t = sem("setup_t")

        def after(eng, step, tile):
            if tile.exists:
                eng.wait_ge(done[step] if isinstance(step, str) else step, tile.t + 1)

        def gathered(eng, tile):
            eng.wait_ge(rows_gathered[tile.p], tile.half * 32 + 32)

        def loaded(eng, r):
            count = sum(16 if ROUNDS[k][0] != "qkv" else 48 for k in range(r % NSTAGE, r + 1, NSTAGE))
            eng.wait_ge(stage_loaded[r % NSTAGE], count)

        def round_views(r):
            kind, n = ROUNDS[r]
            s = stage[r % NSTAGE]
            if kind == "attn":
                v = s[:, :].rearrange("p (c n) -> p c n", c=CH)
                return v, wa[0][:, :, :], wa[1][:, :, :]
            if kind == "qkv":
                v = s[:, :].rearrange("p (e c n) -> p e c n", e=QKV_E, c=CH)
                return v, *[w[:, n * QKV_E:(n + 1) * QKV_E] for w in wq]
            v = s[:, 0:O_E * C].rearrange("p (e n) -> p e n", e=O_E)
            return v, *[w[:, n * O_E:(n + 1) * O_E] for w in wo]

        block = ctx.enter_context(nc.Block())

        @block.sync
        def _(sp):
            row = 0
            for tab in (op_table, var_table, const_table, struct_table):
                sp.dma_start(small[row:row + tab.shape[0], :], tab).then_inc(small_loaded, 16)
                row += tab.shape[0]
            sp.dma_start(ids_rows[:, :], x).then_inc(inputs_loaded, 16)
            sp.dma_start(bias[:, :], b_qkv.partition_broadcast(P)).then_inc(inputs_loaded, 16)
            sp.dma_start(gate_tmp[:, :], gates.partition_broadcast(P)).then_inc(inputs_loaded, 16)
            sp.dma_start(sim[:, :, :], sim_matrix.rearrange("(c p) e -> p c e", p=P)).then_inc(inputs_loaded, 16)
            for r, (kind, n) in enumerate(ROUNDS):
                if r >= NSTAGE:
                    sp.wait_ge(split_hi, r - NSTAGE + 1)
                    sp.wait_ge(split_lo, r - NSTAGE + 1)
                s, landed = stage[r % NSTAGE], stage_loaded[r % NSTAGE]
                if kind == "attn":
                    sp.dma_start(s[:, :].rearrange("p (c n) -> p c n", c=CH),
                                 W_qkv.rearrange("(c p) n -> p c n", p=P)).then_inc(landed, 16)
                elif kind == "qkv":
                    v = s[:, :].rearrange("p (e c m h) -> p (e c) m h", e=QKV_E, c=CH, m=3)
                    for m, w in enumerate((q_proj, k_proj, v_proj)):
                        src = w[n * QKV_E:(n + 1) * QKV_E].rearrange("e (c p) h -> p (e c) h", p=P)
                        sp.dma_start(v[:, :, m, :], src).then_inc(landed, 16)
                else:
                    sp.dma_start(s[:, 0:O_E * C].rearrange("p (e n) -> p e n", e=O_E),
                                 o_proj[n * O_E:(n + 1) * O_E].rearrange("e h c -> h e c")).then_inc(landed, 16)

            def store(tile):
                after(sp, "out_sum", tile)
                sp.dma_start(out[tile.t], result[tile.p][:, :]).then_inc(stored[tile.p], 16)

            for t in range(FIRST):
                store(tile_at(t))
            with sp.Fori(0, (B - 1 - FIRST) // 2) as j:
                for k in range(2):
                    store(tile_at(FIRST + k).ahead(j))
            store(tile_at(B - 1))
            for p in range(2):
                sp.wait_ge(stored[p], 16 * (B // 2))

        @block.gpsimd
        def _(pool):
            pool.memset(ident[:, :], 0.0).then_inc(consts_base, 1)
            pool.memset(causal[:, :], 0.0).then_inc(consts_base, 1)
            pool.memset(head_mask[:, :], 1.0).then_inc(consts_base, 1)
            pool.memset(head_of_row[:, :], 1.0).then_inc(consts_base, 1)
            pool.memset(ones[:, :], 1.0).then_inc(consts_ready, 1)
            pool.memset(minus_half[:, :], -0.5).then_inc(consts_ready, 1)
            pool.memset(vx[:, :, :], 1.0).then_inc(consts_ready, 1)
            pool.memset(eps[:, 0:1], LN_EPS).then_inc(consts_ready, 1)
            pool.memset(eps[:, 1:2], NORM_EPS).then_inc(consts_ready, 1)
            pool.iota(expert_no[:, :], pattern=[[1, E]], base=0, channel_multiplier=0,
                      allow_small_or_imprecise_dtypes=True).then_inc(consts_ready, 1)
            pool.wait_ge(consts_base, 4)
            pool.affine_select(out=ident[:, :], in_=ident[:, :], compare_op=ALU.not_equal, fill=1.0, base=0,
                               pattern=[[-1, P]], channel_multiplier=1).then_inc(consts_ready, 1)
            pool.affine_select(out=causal[:, :], in_=causal[:, :], compare_op=ALU.is_ge, fill=MASKED, base=0,
                               pattern=[[-1, P]], channel_multiplier=1).then_inc(consts_ready, 1)
            hm = head_mask[:, :].rearrange("p (h d) -> p h d", d=D)
            pool.affine_select(out=hm, in_=hm, compare_op=ALU.is_ge, fill=0.0, base=0,
                               pattern=[[-D, HG], [0, D]], channel_multiplier=1).then_inc(consts_base, 1)
            pool.affine_select(out=head_of_row[:, :], in_=head_of_row[:, :], compare_op=ALU.is_ge, fill=0.0,
                               base=0, pattern=[[-D, HG]], channel_multiplier=1).then_inc(consts_base, 1)
            pool.wait_ge(consts_base, 6)
            pool.affine_select(out=hm, in_=hm, compare_op=ALU.is_ge, fill=0.0, base=D - 1,
                               pattern=[[D, HG], [0, D]], channel_multiplier=-1).then_inc(consts_ready, 1)
            pool.affine_select(out=head_of_row[:, :], in_=head_of_row[:, :], compare_op=ALU.is_ge, fill=0.0,
                               base=D - 1, pattern=[[D, HG]], channel_multiplier=-1).then_inc(consts_ready, 1)

            def pick_ids(tile):
                pool.tensor_copy(ids_now[tile.p][:, :], ids[:, bass.ds(tile.t, 1), :].rearrange("p o n -> p (o n)")
                                 ).then_inc(done["ids_picked"], 1)
                after(pool, "ids_picked", tile)

            def gather(tile):
                hp = h[tile.p]
                tok = bass.IndirectOffsetOnAxis(ap=ids_now[tile.p][:, 0:1], axis=0)
                low = bass.IndirectOffsetOnAxis(ap=ids_now[tile.p][:, 1:2], axis=0)
                pool.indirect_dma_start(out=hp[:, 0:HALF], out_offset=None, in_=token_table, in_offset=tok
                                        ).then_inc(rows_gathered[tile.p], 16)
                pool.indirect_dma_start(out=hp[:, HALF:C], out_offset=None, in_=special_table, in_offset=low,
                                        bounds_check=N_SPECIAL - 1, oob_is_err=False
                                        ).then_inc(special_gathered[tile.p], 16)

            def gather_small(tile):
                hp = h[tile.p]
                tok = bass.IndirectOffsetOnAxis(ap=ids_now[tile.p][:, 0:1], axis=0)
                pool.indirect_dma_start(out=hp[:, HALF:C], out_offset=None, in_=small, in_offset=tok,
                                        bounds_check=N_SMALL - 1, oob_is_err=False
                                        ).then_inc(rows_gathered[tile.p], 16)

            def ln_rstd(tile, n):
                name = f"ln{n + 1}"
                after(pool, f"{name}_moments", tile)
                pool.tensor_tensor(var_eps[:, n:n + 1], mv[:, n, 1:2], eps[:, 0:1], ALU.add
                                   ).then_inc(done[f"{name}_var_eps"], 1)
                after(pool, f"{name}_var_eps", tile)
                pool.tensor_tensor(rstd[:, n:n + 1], var_eps[:, n:n + 1], minus_half[:, 0:1], ALU.pow
                                   ).then_inc(done[f"{name}_rstd"], 1)

            def residual(tile):
                after(pool, "attn", tile)
                pool.tensor_tensor(h2[tile.p][:, :], h[tile.p][:, :], attn[:, :], ALU.add
                                   ).then_inc(done["h2"], 1)

            def inverse_norm(tile):
                after(pool, "x2_energy", tile)
                pool.tensor_tensor(energy[:, 1:2], energy[:, 0:1], eps[:, 1:2], ALU.add
                                   ).then_inc(done["x2_energy_eps"], 1)
                after(pool, "x2_energy_eps", tile)
                pool.tensor_tensor(inv_norm[:, :], energy[:, 1:2], minus_half[:, 0:1], ALU.pow
                                   ).then_inc(done["x2_inverse_norm"], 1)

            def pool_sum(tile, s):
                after(pool, o_scaled[s], tile)
                part = o_part[(s // 2) % 2]
                if s:
                    after(pool, o_pooled[s - 2][1], tile)
                else:
                    after(pool, "out_sum", tile.shift(-1))
                pool.tensor_tensor(acc_p[:, :], part[:, 0, :], acc_p[:, :] if s else h2[tile.p][:, :], ALU.add
                                   ).then_inc(o_pooled[s][0], 1)
                after(pool, o_pooled[s][0], tile)
                pool.tensor_tensor(acc_p[:, :], part[:, 1, :], acc_p[:, :], ALU.add
                                   ).then_inc(o_pooled[s][1], 1)

            def final_sum(tile):
                after(pool, o_pooled[OSLOT - 2][1], tile)
                after(pool, o_added[OSLOT - 1][1], tile)
                before = tile.shift(-2)
                if before.exists:
                    pool.wait_ge(stored[tile.p], before.half * 16 + 16)
                pool.tensor_tensor(result[tile.p][:, :], acc_p[:, :], acc_v[:, :], ALU.add
                                   ).then_inc(done["out_sum"], 1)

            def step(tile, a=True, c=True, g=True):
                nxt, prev = tile.shift(1), tile.shift(-1)
                if g:
                    pick_ids(tile.shift(2))
                if a:
                    ln_rstd(nxt, 0)
                if g:
                    gather(tile.shift(2))
                if c:
                    pool_sum(prev, 0)
                if g:
                    ahead = tile.shift(2)
                    pool.wait_ge(special_gathered[ahead.p], ahead.half * 16 + 16)
                if a:
                    residual(nxt)
                if g:
                    gather_small(tile.shift(2))
                if a:
                    ln_rstd(nxt, 1)
                if c:
                    pool_sum(prev, 2)
                if a:
                    inverse_norm(nxt)
                if c:
                    pool_sum(prev, 4)
                    pool_sum(prev, 6)
                    final_sum(prev)

            pool.wait_ge(consts_ready, 10)
            pool.wait_ge(setup_v, 3)
            pool.wait_ge(small_loaded, 64)
            for t in range(2):
                pick_ids(tile_at(t))
                gather(tile_at(t))
                pool.wait_ge(special_gathered[t], 16)
                gather_small(tile_at(t))
            pool.wait_ge(setup_v, 4)
            pool.tensor_tensor(sim_inv[:, :], sim_norm[:, :], minus_half[:, :], ALU.pow).then_inc(setup_p, 1)
            first = tile_at(0)
            ln_rstd(first, 0)
            residual(first)
            ln_rstd(first, 1)
            inverse_norm(first)
            step(tile_at(0), c=False)
            for t in range(1, FIRST):
                step(tile_at(t))
            with pool.Fori(0, (B - 3 - FIRST) // 2) as j:
                for k in range(2):
                    step(tile_at(FIRST + k).ahead(j))
            step(tile_at(B - 3))
            step(tile_at(B - 2), g=False)
            step(tile_at(B - 1), a=False, g=False)
            step(tile_at(B), a=False, g=False)

        @block.scalar
        def _(act):
            def turned_hi(ps, dst, product, signal, tile):
                after(act, product, tile)
                act.copy(dst, ps).then_inc(done[signal], 1)

            def x1_hi(tile):
                turned_hi(ps_a[:, 0:C], x1T[0][:, :, :].rearrange("p c t -> p (c t)"), "x1_turned", "x1T_hi", tile)

            def x2_hi(tile):
                turned_hi(ps_b[:, 0:C], x2T[tile.p][0][:, :, :].rearrange("p c t -> p (c t)"),
                          "x2_turned", "x2T_hi", tile)

            def qk_exp(tile):
                after(act, "qk_biased", tile)
                act.activation(qk_neg[:, :], qk[:, :], ACT.Relu, scale=-1.0).then_inc(done["qk_negative"], 1)
                after(act, "qk_negative", tile)
                act.activation(qk_e[:, :], qk_neg[:, :], ACT.Exp, scale=-1.0).then_inc(done["qk_exp"], 1)

            def phi_q(tile):
                after(act, "phi_q_turned", tile)
                act.copy(pqT[:, :, :].rearrange("p g t -> p (g t)"), ps_a[:, 0:C]).then_inc(done["phi_q_T"], 1)

            def x2_energy(tile):
                after(act, "x2_normed", tile)
                act.activation(squares[:, :], x2[:, :], ACT.Square, accum_out=energy[:, 0:1]
                               ).then_inc(done["x2_energy"], 1)

            def gate_exp(tile):
                after(act, "gate_negmax", tile)
                act.activation(gexp[:, :], gated[:, :], ACT.Exp, bias=gneg[:, 0:1]).then_inc(done["gate_exp"], 1)

            def heads(tile):
                after(act, "heads_turned", tile)
                act.copy(headsT[:, :, :].rearrange("p a t -> p (a t)"), ps_c[:, 0:2 * P]
                         ).then_inc(done["heads_T"], 1)

            def probs(tile):
                after(act, "scores_negmax", tile)
                act.activation(pr[:, :], sc[:, :], ACT.Exp, bias=sneg[:, 0:1], accum_out=psumm[:, 0:1]
                               ).then_inc(done["probs"], 1)

            def probs_T(tile):
                after(act, "probs_turned", tile)
                act.copy(prT[:, :], ps_c[:, 0:P]).then_inc(done["probs_T"], 1)

            def ao_hi(tile):
                after(act, o_product[OSLOT - 1], tile.shift(-1))
                after(act, "ao_product", tile)
                act.copy(aoT[0][:, :], ps_c[:, P:2 * P]).then_inc(done["aoT_hi"], 1)

            def o_scale(tile, s):
                if s == 0:
                    after(act, "o_weights", tile)
                after(act, o_product[s], tile)
                after(act, o_pooled[(s - 4) % OSLOT][1], tile if s >= 4 else tile.shift(-1))
                part = o_part[(s // 2) % 2]
                act.mul(part[:, 0, :], ps_o[0][:, 0:C], rwo[tile.p][:, 2 * s:2 * s + 1])
                act.mul(part[:, 1, :], ps_o[0][:, C:2 * C], rwo[tile.p][:, 2 * s + 1:2 * s + 2]
                        ).then_inc(o_scaled[s], 1)

            def weights_hi(r):
                loaded(act, r)
                raw, hi, _ = round_views(r)
                act.copy(hi, raw).then_inc(split_hi, 1)

            def step(tile, a=True, c=True, weights=False):
                nxt, prev = tile.shift(1), tile.shift(-1)
                if weights:
                    for r in range(1, 4):
                        weights_hi(r)
                if c:
                    heads(prev)
                if a:
                    x1_hi(nxt)
                if c:
                    probs(prev)
                    probs_T(prev)
                    ao_hi(prev)
                if weights:
                    for r in range(4, 6):
                        weights_hi(r)
                if a:
                    qk_exp(nxt)
                if weights:
                    weights_hi(6)
                if a:
                    phi_q(nxt)
                if weights:
                    weights_hi(7)
                if c:
                    o_scale(prev, 0)
                    o_scale(prev, 2)
                if a:
                    x2_energy(nxt)
                    x2_hi(nxt)
                if weights:
                    weights_hi(8)
                if c:
                    o_scale(prev, 4)
                if a:
                    gate_exp(nxt)
                if weights:
                    for r in range(9, len(ROUNDS)):
                        weights_hi(r)
                if c:
                    o_scale(prev, 6)

            act.wait_ge(inputs_loaded, 64)
            act.activation(gate_bias[:, :], gate_tmp[:, :], ACT.Exp, scale=-1.0).then_inc(setup_a, 1)
            weights_hi(0)
            act.wait_ge(setup_v, 5)
            act.copy(ws[0][:, :, :], simn[:, :, :]).then_inc(setup_a, 1)
            first = tile_at(0)
            x1_hi(first)
            qk_exp(first)
            phi_q(first)
            x2_energy(first)
            x2_hi(first)
            gate_exp(first)
            step(tile_at(0), c=False, weights=True)
            for t in range(1, FIRST):
                step(tile_at(t))
            with act.Fori(0, (B - 1 - FIRST) // 2) as j:
                for k in range(2):
                    step(tile_at(FIRST + k).ahead(j))
            step(tile_at(B - 1), a=False)
            step(tile_at(B), a=False)

        @block.vector
        def _(dve):
            def ln_stats(tile, n):
                src = (h, h2)[n][tile.p]
                name = f"ln{n + 1}"
                if n == 0:
                    gathered(dve, tile)
                else:
                    after(dve, "h2", tile)
                dve.bn_stats(stats[:, n, :], src[:, :]).then_inc(done[f"{name}_stats"], 1)
                after(dve, f"{name}_stats", tile)

            def ln_moments(tile, n):
                name = f"ln{n + 1}"
                dve.bn_aggr(mv[:, n, :], stats[:, n, :]).then_inc(done[f"{name}_moments"], 1)

            def ln_apply(tile, n):
                src, dst = (h, h2)[n][tile.p], (x1, x2)[n]
                after(dve, f"ln{n + 1}_rstd", tile)
                dve.tensor_scalar(dst[:, :], src[:, :], mv[:, n, 0:1], rstd[:, n:n + 1], ALU.subtract, ALU.mult
                                  ).then_inc(done[("x1_normed", "x2_normed")[n]], 1)

            def turned_lo(ps, pair, hi_step, lo_step, tile):
                after(dve, hi_step, tile)
                dve.tensor_tensor(pair[1], ps, pair[0].bitcast(F32), ALU.subtract).then_inc(done[lo_step], 1)

            def x1_lo(tile):
                turned_lo(ps_a[:, 0:C], [v[:, :, :].rearrange("p c t -> p (c t)") for v in x1T],
                          "x1T_hi", "x1T_lo", tile)

            def x2_lo(tile):
                turned_lo(ps_b[:, 0:C], [v[:, :, :].rearrange("p c t -> p (c t)") for v in x2T[tile.p]],
                          "x2T_hi", "x2T_lo", tile)

            def ao_lo(tile):
                turned_lo(ps_c[:, P:2 * P], [v[:, :] for v in aoT], "aoT_hi", "aoT_lo", tile)

            def qkv_bias(tile):
                after(dve, "qk_product", tile)
                dve.tensor_tensor(qk[:, :], ps_b[:, :], bias[:, 0:2 * C], ALU.add).then_inc(done["qk_biased"], 1)
                after(dve, "v_product", tile)
                dve.tensor_tensor(vx[:, :, 0:P], ps_a[:, 0:C].rearrange("p (g n) -> p g n", g=G),
                                  bias[:, 2 * C:3 * C].rearrange("p (g n) -> p g n", g=G), ALU.add
                                  ).then_inc(done["v_biased"], 1)

            def phi_sum(tile):
                after(dve, "qk_exp", tile)
                dve.scalar_tensor_tensor(phi[:, :], qk[:, :], 0.0, qk_e[:, :], ALU.max, ALU.add
                                         ).then_inc(done["phi"], 1)

            def kv_mask(tile):
                after(dve, "kv_product", tile)
                dve.tensor_tensor(kvm[:, :, 0:P], ps_kv[:, :, 0:P],
                                  head_mask[:, :].unsqueeze(1).broadcast_to([P, G, P]), ALU.mult)
                dve.tensor_tensor(kvm[:, :, P:NUMW], ps_kv[:, :, P:P + 1].broadcast_to([P, G, HG]),
                                  head_of_row[:, :].unsqueeze(1).broadcast_to([P, G, HG]), ALU.mult
                                  ).then_inc(done["kv_masked"], 1)

            def attend(tile):
                after(dve, "attn_sums", tile)
                dve.tensor_scalar(den[:, :, :], ps_sums[:, :, P:NUMW], DEN_EPS, None, ALU.add
                                  ).then_inc(done["attn_den"], 1)
                after(dve, "attn_den", tile)
                dve.reciprocal(zden[:, :, :], den[:, :, :]).then_inc(done["attn_z"], 1)
                after(dve, "attn_z", tile)
                dve.tensor_tensor(attn[:, :].rearrange("p (g h d) -> p g h d", g=G, d=D),
                                  ps_sums[:, :, 0:P].rearrange("p g (h d) -> p g h d", d=D),
                                  zden[:, :, :].unsqueeze(3).broadcast_to([P, G, HG, D]), ALU.mult
                                  ).then_inc(done["attn"], 1)

            def gate_pick(tile):
                after(dve, "x2_inverse_norm", tile)
                after(dve, "logits_product", tile)
                dve.scalar_tensor_tensor(logits[:, :], ps_b[:, 0:E], inv_norm[:, 0:1], gate_bias[:, :],
                                         ALU.mult, ALU.subtract).then_inc(done["logits"], 1)
                after(dve, "logits", tile)
                dve.tensor_scalar(gated[:, :], logits[:, :], 0.0, None, ALU.max)
                dve.max(top[:, :], logits[:, :]).then_inc(done["top_values"], 1)
                dve.tensor_scalar(active[:, :], logits[:, :], 0.0, None, ALU.is_gt)
                after(dve, "top_values", tile)
                dve.tensor_scalar(gneg[:, :], top[:, 0:1], 0.0, -1.0, ALU.max, ALU.mult
                                  ).then_inc(done["gate_negmax"], 1)
                dve.max_index(top_at[:, :], top[:, :], logits[:, :]).then_inc(done["top_indices"], 1)
                dve.tensor_scalar(idle[:, :], top[:, 0:1], 0.0, None, ALU.is_le)
                after(dve, "top_indices", tile)
                dve.tensor_scalar(is_first[:, :], expert_no[:, :], top_at[:, 0:1], None, ALU.is_equal
                                  ).then_inc(done["is_first"], 1)
                after(dve, "is_first", tile)
                dve.scalar_tensor_tensor(top_two[:, :], expert_no[:, :], top_at[:, 1:2], is_first[:, :],
                                         ALU.is_equal, ALU.add).then_inc(done["top_two"], 1)
                after(dve, "top_two", tile)
                dve.scalar_tensor_tensor(gmask[:, :], top_two[:, :], idle[:, 0:1], active[:, :],
                                         ALU.mult, ALU.add).then_inc(done["gate_mask"], 1)

            def gate_softmax(tile):
                after(dve, "gate_mask", tile)
                after(dve, "gate_exp", tile)
                dve.scalar_tensor_tensor(gsel[:, :], gexp[:, :], 1.0, gmask[:, :], ALU.mult, ALU.mult,
                                         accum_out=gsum[:, 0:1]).then_inc(done["gate_sum"], 1)
                after(dve, "gate_sum", tile)
                dve.reciprocal(gsum[:, 1:2], gsum[:, 0:1]).then_inc(done["gate_rsum"], 1)
                after(dve, "gate_rsum", tile)
                dve.tensor_scalar(rw[tile.p][:, :], gsel[:, :], gsum[:, 1:2], None, ALU.mult
                                  ).then_inc(done["routing"], 1)

            def expert_add(tile, e):
                acc, w = qkv[tile.p], rw[tile.p][:, e:e + 1]
                if e == 0:
                    after(dve, "routing", tile)
                    after(dve, "ao_product", tile.shift(-2))
                else:
                    after(dve, expert_added[e - 1], tile)
                after(dve, expert_product[e], tile)
                src = ps_e[EBANK[e]][:, 0:3 * HD]
                if e == 0:
                    ins = dve.tensor_scalar(acc[:, :], src, w, None, ALU.mult)
                else:
                    ins = dve.scalar_tensor_tensor(acc[:, :], src, w, acc[:, :], ALU.mult, ALU.add)
                ins.then_inc(expert_added[e], 1)

            def mask_scores(tile):
                after(dve, "scores", tile)
                dve.scalar_tensor_tensor(sc[:, :], ps_c[:, 2 * P:3 * P], SCALE, causal[:, :], ALU.mult, ALU.add
                                         ).then_inc(done["scores_masked"], 1)
                after(dve, "scores_masked", tile)
                dve.tensor_reduce(sneg[:, :], sc[:, :], AX_X, ALU.max, negate=True
                                  ).then_inc(done["scores_negmax"], 1)

            def o_weights(tile):
                after(dve, "probs", tile)
                dve.reciprocal(psumm[:, 1:2], psumm[:, 0:1]).then_inc(done["probs_rsum"], 1)
                after(dve, "probs_rsum", tile)
                dve.tensor_scalar(rwo[tile.p][:, :], rw[tile.p][:, :], psumm[:, 1:2], None, ALU.mult
                                  ).then_inc(done["o_weights"], 1)

            def o_add(tile, s):
                if s == 1:
                    after(dve, "o_weights", tile)
                    after(dve, "out_sum", tile.shift(-1))
                after(dve, o_product[s], tile)
                for j in range(2):
                    src, w = ps_o[1][:, j * C:(j + 1) * C], rwo[tile.p][:, 2 * s + j:2 * s + j + 1]
                    if s == 1 and j == 0:
                        ins = dve.tensor_scalar(acc_v[:, :], src, w, None, ALU.mult)
                    else:
                        after(dve, o_added[s][0] if j else o_added[s - 2][1], tile)
                        ins = dve.scalar_tensor_tensor(acc_v[:, :], src, w, acc_v[:, :], ALU.mult, ALU.add)
                    ins.then_inc(o_added[s][j], 1)

            def weights_lo(r):
                loaded(dve, r)
                dve.wait_ge(split_hi, r + 1)
                raw, hi, lo = round_views(r)
                dve.tensor_tensor(lo, raw, hi.bitcast(F32), ALU.subtract).then_inc(split_lo, 1)

            def step(tile, m=True, a=True, c=True, weights=False):
                nxt, prev = tile.shift(1), tile.shift(-1)

                def add(e):
                    if weights:
                        if e % QKV_E == 0:
                            weights_lo(1 + e // QKV_E)
                        if e == E - 1:
                            for r in range(1 + NQ, len(ROUNDS)):
                                weights_lo(r)
                    if m:
                        expert_add(tile, e)

                if a:
                    ln_stats(nxt, 0)
                add(0)
                if a:
                    ln_moments(nxt, 0)
                add(1)
                if a:
                    ln_apply(nxt, 0)
                add(2)
                if a:
                    x1_lo(nxt)
                if c:
                    mask_scores(prev)
                add(3)
                if c:
                    o_weights(prev)
                add(4)
                if a:
                    qkv_bias(nxt)
                add(5)
                if c:
                    ao_lo(prev)
                add(6)
                if a:
                    phi_sum(nxt)
                add(7)
                add(8)
                if a:
                    kv_mask(nxt)
                add(9)
                if a:
                    attend(nxt)
                if c:
                    o_add(prev, 1)
                add(10)
                if a:
                    ln_stats(nxt, 1)
                add(11)
                if a:
                    ln_moments(nxt, 1)
                if c:
                    o_add(prev, 3)
                if a:
                    ln_apply(nxt, 1)
                add(12)
                if a:
                    x2_lo(nxt)
                add(13)
                if c:
                    o_add(prev, 5)
                if a:
                    gate_pick(nxt)
                add(14)
                if a:
                    gate_softmax(nxt)
                add(15)
                if c:
                    o_add(prev, 7)

            dve.wait_ge(inputs_loaded, 64)
            dve.tensor_copy(ids_rows_f[:, :], ids_rows[:, :]).then_inc(setup_v, 1)
            dve.tensor_tensor(sim_sq[:, :, :], sim[:, :, :], sim[:, :, :], ALU.mult).then_inc(setup_v, 1)
            dve.wait_ge(setup_t, 1)
            dve.tensor_copy(ids_f[:, :], ps_a[:, 0:B]).then_inc(setup_own, 1)
            dve.wait_ge(setup_own, 1)
            dve.tensor_scalar(ids_low[:, :], ids_f[:, :], float(N_SMALL), float(2 ** 22), ALU.is_lt, ALU.mult
                              ).then_inc(setup_own, 1)
            dve.wait_ge(setup_own, 2)
            dve.tensor_copy(ids[:, :, 0], ids_f[:, :])
            dve.scalar_tensor_tensor(ids[:, :, 1], ids_f[:, :], float(N_SMALL), ids_low[:, :],
                                     ALU.subtract, ALU.add).then_inc(setup_v, 1)
            dve.wait_ge(setup_t, 2)
            dve.tensor_scalar(sim_norm[:, :], ps_c[:, 0:E], NORM_EPS, None, ALU.add).then_inc(setup_v, 1)
            dve.wait_ge(setup_a, 1)
            dve.tensor_scalar(gate_tmp[:, :], gate_bias[:, :], 1.0, None, ALU.add).then_inc(setup_own, 1)
            dve.wait_ge(setup_own, 3)
            dve.reciprocal(gate_bias[:, :], gate_tmp[:, :])
            dve.wait_ge(setup_p, 1)
            dve.tensor_tensor(simn[:, :, :], sim[:, :, :], sim_inv[:, :].unsqueeze(1).broadcast_to([P, CH, E]),
                              ALU.mult).then_inc(setup_v, 1)
            dve.wait_ge(setup_a, 2)
            dve.tensor_tensor(ws[1][:, :, :], simn[:, :, :], ws[0][:, :, :].bitcast(F32), ALU.subtract
                              ).then_inc(setup_v, 1)
            weights_lo(0)
            dve.wait_ge(consts_ready, 10)
            first = tile_at(0)
            ln_stats(first, 0)
            ln_moments(first, 0)
            ln_apply(first, 0)
            x1_lo(first)
            qkv_bias(first)
            phi_sum(first)
            kv_mask(first)
            attend(first)
            ln_stats(first, 1)
            ln_moments(first, 1)
            ln_apply(first, 1)
            x2_lo(first)
            gate_pick(first)
            gate_softmax(first)
            step(tile_at(0), c=False, weights=True)
            for t in range(1, FIRST):
                step(tile_at(t))
            with dve.Fori(0, (B - 1 - FIRST) // 2) as j:
                for k in range(2):
                    step(tile_at(FIRST + k).ahead(j))
            step(tile_at(B - 1), a=False)
            step(tile_at(B), m=False, a=False)

        @block.tensor
        def _(pe):
            def product(ps, left, right):
                n = len(left[0])
                for c in range(n):
                    pe.matmul(ps, left[1][c], right[0][c], start=(c == 0), stop=False)
                    pe.matmul(ps, left[0][c], right[1][c], start=False, stop=False)
                    last = pe.matmul(ps, left[0][c], right[0][c], start=False, stop=(c == n - 1))
                return last

            def chunks(pair, *where):
                return [[w[(slice(None), c, *where)] for c in range(CH)] for w in pair]

            def turn_x1(tile):
                after(pe, "x1_normed", tile)
                after(pe, "attn", tile.shift(-1))
                for c in range(CH):
                    last = pe.transpose(ps_a[:, c * P:(c + 1) * P], x1[:, c * P:(c + 1) * P], ident[:, :])
                last.then_inc(done["x1_turned"], 1)

            def qkv_products(tile):
                after(pe, "x1T_lo", tile)
                after(pe, "logits", tile.shift(-1))
                x1p = chunks(x1T, slice(None))
                product(ps_b[:, :], x1p, chunks(wa, slice(0, 2 * C))).then_inc(done["qk_product"], 1)
                product(ps_a[:, 0:C], x1p, chunks(wa, slice(2 * C, 3 * C))).then_inc(done["v_product"], 1)

            def kv_products(tile):
                after(pe, "phi", tile)
                for g in range(G):
                    last = pe.transpose(ps_a[:, g * P:(g + 1) * P], phi[:, g * P:(g + 1) * P], ident[:, :])
                last.then_inc(done["phi_q_turned"], 1)
                for g in range(G):
                    last = pe.matmul(ps_kv[:, g, :], phi[:, C + g * P:C + (g + 1) * P], vx[:, g, :],
                                     start=True, stop=True)
                last.then_inc(done["kv_product"], 1)

            def attn_sums(tile):
                after(pe, "phi_q_T", tile)
                after(pe, "kv_masked", tile)
                for g in range(G):
                    last = pe.matmul(ps_sums[:, g, :], pqT[:, g, :], kvm[:, g, :], start=True, stop=True)
                last.then_inc(done["attn_sums"], 1)

            def turn_x2(tile):
                after(pe, "x2_normed", tile)
                for c in range(CH):
                    last = pe.transpose(ps_b[:, c * P:(c + 1) * P], x2[:, c * P:(c + 1) * P], ident[:, :])
                last.then_inc(done["x2_turned"], 1)

            def gate_product(tile):
                after(pe, "x2T_lo", tile)
                product(ps_b[:, 0:E], chunks(x2T[tile.p], slice(None)), chunks(ws, slice(None))
                        ).then_inc(done["logits_product"], 1)

            def expert(tile, e, weights):
                if weights and e % QKV_E == 0:
                    pe.wait_ge(split_lo, 2 + e // QKV_E)
                if e == 0:
                    after(pe, "x2T_lo", tile)
                user, back = bank_before(e)
                after(pe, expert_added[user], tile.shift(-back))
                product(ps_e[EBANK[e]][:, 0:3 * HD], chunks(x2T[tile.p], slice(None)),
                        [[w[:, e, c, :] for c in range(CH)] for w in wq]).then_inc(expert_product[e], 1)

            def turn_heads(tile):
                after(pe, expert_added[E - 1], tile)
                after(pe, "aoT_lo", tile.shift(-1))
                for m in range(2):
                    last = pe.transpose(ps_c[:, m * P:(m + 1) * P], qkv[tile.p][:, m * HD:(m + 1) * HD], ident[:, :])
                last.then_inc(done["heads_turned"], 1)

            def score(tile):
                after(pe, "heads_T", tile)
                pe.matmul(ps_c[:, 2 * P:3 * P], headsT[:, 0, :], headsT[:, 1, :], start=True, stop=True
                          ).then_inc(done["scores"], 1)

            def turn_probs(tile):
                after(pe, "probs", tile)
                pe.transpose(ps_c[:, 0:P], pr[:, :], ident[:, :]).then_inc(done["probs_turned"], 1)

            def attend_v(tile):
                after(pe, "probs_T", tile)
                pe.matmul(ps_c[:, P:2 * P], qkv[tile.p][:, 2 * HD:3 * HD], prT[:, :], start=True, stop=True
                          ).then_inc(done["ao_product"], 1)

            def o_slot(tile, s):
                if s == 0:
                    after(pe, "aoT_lo", tile)
                user, t = (s - 2, tile) if s >= 2 else (s + OSLOT - 2, tile.shift(-1))
                after(pe, o_added[user][1] if s % 2 else o_scaled[user], t)
                for j in range(2):
                    last = product(ps_o[s % 2][:, j * C:(j + 1) * C], [[a[:, :]] for a in aoT],
                                   [[w[:, 2 * s + j, :]] for w in wo])
                last.then_inc(o_product[s], 1)

            def step(tile, m=True, a=True, c=True, weights=False):
                nxt, prev = tile.shift(1), tile.shift(-1)

                def experts(*es):
                    if m:
                        for e in es:
                            expert(tile, e, weights)

                experts(0)
                if c:
                    turn_heads(prev)
                experts(1)
                if a:
                    turn_x1(nxt)
                experts(2)
                if c:
                    score(prev)
                experts(3)
                if a:
                    qkv_products(nxt)
                experts(4)
                if c:
                    turn_probs(prev)
                experts(5)
                if c:
                    attend_v(prev)
                experts(6, 7)
                if a:
                    kv_products(nxt)
                experts(8)
                if c:
                    o_slot(prev, 0)
                experts(9)
                if a:
                    attn_sums(nxt)
                if c:
                    o_slot(prev, 1)
                experts(10)
                if c:
                    o_slot(prev, 2)
                experts(11)
                if c:
                    o_slot(prev, 3)
                if a:
                    turn_x2(nxt)
                experts(12)
                if c:
                    o_slot(prev, 4)
                experts(13)
                if c:
                    o_slot(prev, 5)
                if a:
                    gate_product(nxt)
                experts(14)
                if c:
                    o_slot(prev, 6)
                experts(15)
                if c:
                    o_slot(prev, 7)

            pe.wait_ge(consts_ready, 10)
            pe.wait_ge(setup_v, 1)
            pe.transpose(ps_a[:, 0:B], ids_rows_f[:, :], ident[0:B, 0:B]).then_inc(setup_t, 1)
            pe.wait_ge(setup_v, 2)
            for c in range(CH):
                last = pe.matmul(ps_c[:, 0:E], ones[:, :], sim_sq[:, c, :], start=(c == 0), stop=(c == CH - 1))
            last.then_inc(setup_t, 1)
            first = tile_at(0)
            pe.wait_ge(setup_v, 6)
            turn_x1(first)
            pe.wait_ge(split_lo, 1)
            qkv_products(first)
            kv_products(first)
            attn_sums(first)
            turn_x2(first)
            gate_product(first)
            step(tile_at(0), c=False, weights=True)
            pe.wait_ge(split_lo, len(ROUNDS))
            for t in range(1, FIRST):
                step(tile_at(t))
            with pe.Fori(0, (B - 1 - FIRST) // 2) as j:
                for k in range(2):
                    step(tile_at(FIRST + k).ahead(j))
            step(tile_at(B - 1), a=False)
            step(tile_at(B), m=False, a=False)


_INS = ["x", "L0_tok_token_table", "L0_tok_op_table", "L0_tok_var_table", "L0_tok_const_table",
        "L0_tok_struct_table", "L0_tok_special_table", "L0_attn_W_qkv", "L0_attn_b_qkv", "L0_attn_W_proj",
        "L0_attn_b_proj", "L0_ffn_sim_matrix", "L0_ffn_gates", "L0_ffn_q_proj", "L0_ffn_k_proj",
        "L0_ffn_v_proj", "L0_ffn_o_proj"]


def kernel(**inputs):
    import numpy as _np
    import concourse.bacc as _bacc
    from concourse import mybir as _mybir
    from concourse.bass_utils import run_bass_kernel_spmd as _run

    nc = _bacc.Bacc("TRN2", target_bir_lowering=False, num_devices=1)
    arrays, args = {}, []
    for name in _INS:
        a = _np.ascontiguousarray(inputs[name])
        arrays[f"in_{name}"] = a
        args.append(nc.dram_tensor(f"in_{name}", a.shape, _mybir.dt.from_np(a.dtype), kind="ExternalInput").ap())
    b, t = inputs["x"].shape
    c = 2 * inputs["L0_tok_token_table"].shape[1]
    args.append(nc.dram_tensor("out_h", (b, t, c), _mybir.dt.float32, kind="ExternalOutput").ap())
    build(nc, *args)
    r = _run(nc, [arrays], core_ids=[0])
    return r.results[0]["out_h"]
```

```python
from contextlib import ExitStack

import concourse.bass as bass
from concourse import mybir

F32 = mybir.dt.float32
F32R = mybir.dt.float32r
I32 = mybir.dt.int32
U32 = mybir.dt.uint32
ALU = mybir.AluOpType
ACT = mybir.ActivationFunctionType
AX_X = mybir.AxisListType.X

P = 128
LN_EPS = 1e-5
NORM_EPS = 1e-12
DEN_EPS = 1e-6
MASKED = -1.0e30

P1_STEPS = ["ids_picked", "ln1_stats", "ln1_moments", "ln2_stats", "ln2_moments", "roots_eps", "roots",
            "x1_normed", "x1_turned", "x1_T", "qk_product", "v_product", "qk_negative", "qk_exp", "v_copied",
            "phi", "phi_q_turned", "kv_product", "phi_q_T", "kv_masked", "attn_sums", "attn_den", "attn_z",
            "attn", "h2", "x2_normed", "x2_energy", "x2_turned", "x2_T", "logits_product", "logits",
            "top_values", "top_indices", "is_two", "top_two", "gate_mask", "gate_negmax", "gate_exp",
            "gate_sum", "gate_rsum", "routing", "pair_weights", "rank_product", "ranks", "position",
            "position_index", "position_kept", "count"]
P2_STEPS = ["pair_turned", "pair_hi", "pair_lo", "pair_product", "pair_copied"]
DENSE_STEPS = ["dense_stats", "dense_moments", "dense_eps", "dense_root", "dense_x2", "dense_turned", "dense_hi", "dense_lo"]
P3_STEPS = ["pair_picked", "first_row", "qkv_sum", "heads_turned", "heads_T", "scores", "scores_masked",
            "scores_negmax", "probs", "probs_rsum", "o_weights", "probs_turned", "probs_T", "ao_product",
            "aoT_hi", "aoT_lo", "out_sum"]


class Tile:

    def __init__(self, c, j=None):
        self.c, self.j = c, j
        self.p, self.q = c % 2, c % 4
        self.t = c if j is None else j * 4 + c
        self.half = c // 2 if j is None else j * 2 + c // 2
        self.quarter = c // 4 if j is None else j + c // 4

    def shift(self, k):
        return Tile(self.c + k, self.j)

    @property
    def exists(self):
        return self.j is not None or self.c >= 0

    def inside(self, n):
        return self.j is not None or 0 <= self.c < n


def run(eng, step, first, last, low, high):
    for c in range(first, low):
        step(Tile(c))
    with eng.Fori(0, (high + 1 - low) // 4) as j:
        for k in range(4):
            step(Tile(low + k, j))
    for c in range(high + 1, last + 1):
        step(Tile(c))


def build(nc, x, token_table, op_table, var_table, const_table, struct_table, special_table,
          W_qkv, b_qkv, W_proj, b_proj, sim_matrix, gates, q_proj, k_proj, v_proj, o_proj, out):
    B, T = x.shape
    HALF = token_table.shape[1]
    C = 2 * HALF
    CH = C // P
    E = gates.shape[0]
    HD = q_proj.shape[2]
    Y = 3 * HD
    D = 16
    HG = P // D
    G = C // P
    KVW = P + 2
    NUMW = P + HG
    N_SMALL = sum(t.shape[0] for t in (op_table, var_table, const_table, struct_table))
    N_SPECIAL = special_table.shape[0]
    SCALE = float(HD) ** -0.5
    REGION = (B + 1) * T
    PAIR_TILES = 2 * B + E
    OSLOT = E // 2
    POOL_SLOTS = (0, 3, 6)
    DVE_SLOTS = [s for s in range(OSLOT) if s not in POOL_SLOTS]
    assert T == P and HD == P and C == 2 * P and E == 16 and B // 4 == E and PAIR_TILES % 4 == 0

    small = nc.dram_tensor("small_table", [N_SMALL, HALF], F32, kind="Internal").ap()
    sorted_x = nc.dram_tensor("sorted_x", [E * REGION + E * P, C], F32, kind="Internal").ap()
    sorted_y = nc.dram_tensor("sorted_y", [PAIR_TILES * P, Y], F32, kind="Internal").ap()
    h2_rows = nc.dram_tensor("h2_rows", [B, T, C], F32, kind="Internal").ap()

    with ExitStack() as ctx:
        def sb(name, shape, dt=F32):
            return ctx.enter_context(nc.sbuf_tensor(name, shape, dt))

        def sem(name):
            return ctx.enter_context(nc.semaphore(name))

        def sems(name, n):
            return [sem(f"{name}{i}") for i in range(n)]

        ident = sb("ident", [P, P])
        causal = sb("causal", [P, P])
        head_mask = sb("head_mask", [P, P])
        head_of_row = sb("head_of_row", [P, HG])
        earlier = sb("earlier", [P, P])
        ones = sb("ones", [P, P])
        ones_r = sb("ones_r", [1, P], F32R)
        zeros = sb("zeros", [P, C])
        minus_half = sb("minus_half", [P, E])
        eps = sb("eps", [P, 3])
        expert_no = sb("expert_no", [P, E])
        region_start = sb("region_start", [P, E])
        partition_no = sb("partition_no", [P, 1])
        waiter = sb("waiter", [P, 8])
        bias = [sb(f"bias_{n}", [1, 3 * C], F32R) for n in ("hi", "lo")]
        gate_bias = sb("gate_bias", [P, E])
        gate_tmp = sb("gate_tmp", [P, E])
        ids_rows = sb("ids_rows", [B, T], I32)
        ids_rows_f = sb("ids_rows_f", [B, T])
        ids_f = sb("ids_f", [P, B])
        ids_low = sb("ids_low", [P, B])
        ids = sb("ids", [P, B, 2], U32)
        ids_now = [sb(f"ids_now{q}", [P, 2], U32) for q in range(4)]
        w_attn = sb("w_attn", [P, CH, 3 * C])
        raw_qkv = sb("raw_qkv", [P, CH, Y])
        raw_o = sb("raw_o", [P, C])
        bias_raw = raw_qkv[0:1, :, :].rearrange("p c n -> p (c n)")
        wq = [sb(f"wq_{n}", [P, E, CH, Y], F32R) for n in ("hi", "lo")]
        wo = [sb(f"wo_{n}", [P, E, C], F32R) for n in ("hi", "lo")]
        sim = sb("sim", [P, CH, E])
        sim_sq = sb("sim_sq", [P, CH, E])
        sim_norm = sb("sim_norm", [P, E])
        sim_inv = sb("sim_inv", [P, E])
        simn = sb("simn", [P, CH, E])
        h4 = sb("h4", [P, 4, C])
        h2 = [sb(f"h2_{p}", [P, C]) for p in range(2)]
        stats = sb("stats", [P, 2, 6])
        moments = [sb(f"moments{p}", [P, 3, 2]) for p in range(2)]
        roots_eps = [sb(f"roots_eps{p}", [P, 3]) for p in range(2)]
        roots = [sb(f"roots{p}", [P, 3]) for p in range(2)]
        x1 = sb("x1", [P, C])
        x1T = sb("x1T", [P, C])
        x2 = [sb(f"x2_{q}", [P, C]) for q in range(4)]
        x2T = sb("x2T", [P, C])
        qk_neg = sb("qk_neg", [P, 2 * C])
        qk_e = sb("qk_e", [P, 2 * C])
        phi = sb("phi", [P, 2 * C])
        vx = sb("vx", [P, G, KVW])
        pqT = sb("pqT", [P, G, P])
        kvm = sb("kvm", [P, G, NUMW])
        den = sb("den", [P, G, HG])
        zden = sb("zden", [P, G, HG])
        attn = sb("attn", [P, C])
        squares = sb("squares", [P, C])
        logits = sb("logits", [P, E])
        top = sb("top", [P, 8])
        top_at = sb("top_at", [P, 8], U32)
        is_one = sb("is_one", [P, E])
        is_two = sb("is_two", [P, E])
        top_two = sb("top_two", [P, E])
        idle = sb("idle", [P, 1])
        active = sb("active", [P, E])
        gated = sb("gated", [P, E])
        gmask = sb("gmask", [P, E])
        gneg = sb("gneg", [P, 1])
        gexp = sb("gexp", [P, E])
        gsel = sb("gsel", [P, E])
        gsum = sb("gsum", [P, 2])
        picked = sb("picked", [P, 4, E])
        ranks = sb("ranks", [P, E])
        next_row = sb("next_row", [P, E])
        third = sb("third", [P, 1])
        position = sb("position", [P, 2])
        position_u = [sb(f"position_u{q}", [P, 2], U32) for q in range(4)]
        routing = sb("routing", [P, B, E])
        pair_w = sb("pair_w", [P, B, 2])
        pair_in_x = sb("pair_in_x", [P, B, 2])
        pair_at = sb("pair_at", [P, B, 2], U32)
        tab = sb("tab", [P, 2, 2])
        tiles_i = sb("tiles_i", [P, E], I32)
        tiles_f = sb("tiles_f", [P, E])
        tiles_cum = sb("tiles_cum", [P, E])
        before = sb("before", [P, E])
        y_shift = sb("y_shift", [P, E])
        y_step = sb("y_step", [P, E])
        tab_tmp = sb("tab_tmp", [P, 4])
        tab_i = sb("tab_i", [1, 2, 2 * P], I32)
        fill_i = sb("fill_i", [1, E], I32)
        flag_f = sb("flag_f", [1, 1])
        flag_i = sb("flag_i", [1, 1], I32)
        row_x = sb("row_x", [P, 4, C])
        row_y = sb("row_y", [P, 4, Y])
        split = [[sb(f"split_{n}{q}", [P, CH, P], F32R) for n in ("hi", "lo")] for q in range(4)]
        qkv = [phi[:, 0:Y], qk_e[:, 0:Y]]
        pair_now = [sb(f"pair_now{p}", [P, 2], U32) for p in range(2)]
        headsT = x1T[:, :].rearrange("p (a t) -> p a t", a=2)
        sc, pr = attn[:, 0:P], attn[:, P:2 * P]
        prT = squares[:, 0:P]
        acc_v, acc_p = x1, x2T
        sneg = sb("sneg", [P, 1])
        psumm = sb("psumm", [P, 2])
        rwo = [sb(f"rwo{p}", [P, E]) for p in range(2)]
        o_part = [h4[:, 2 * b:2 * b + 2, :] for b in range(2)]
        aoT = [[w[:, 0, :] for w in split[p]] for p in range(2)]

        banks = [ctx.enter_context(nc.psum_tensor(f"bank{b}", [P, 512], F32)) for b in range(8)]
        ps_x1, ps_qk, ps_v, ps_pq, ps_kvb, ps_sumb, ps_x2, ps_gate = banks
        ps_kv = ps_kvb[:, 0:G * KVW].rearrange("p (g n) -> p g n", g=G)
        ps_sums = ps_sumb[:, 0:G * NUMW].rearrange("p (g n) -> p g n", g=G)
        ps_rank = ps_x2
        ps_turn, ps_y = banks[0:2], banks[2:6]
        ps_o = banks[0:3]
        ps_heads, ps_score, ps_prob, ps_ao = banks[3:7]

        done = {s: sem(s) for s in P1_STEPS + P2_STEPS + DENSE_STEPS + P3_STEPS}
        rows_gathered = sems("rows_gathered", 4)
        special_gathered = sems("special_gathered", 4)
        scattered = sems("scattered", 4)
        h2_stored = sems("h2_stored", 2)
        qkv_loaded = sem("qkv_loaded")
        o_loaded = sem("o_loaded")
        weights_hi = sem("weights_hi")
        weights_lo = sem("weights_lo")
        small_loaded = sem("small_loaded")
        inputs_loaded = sem("inputs_loaded")
        attn_loaded = sem("attn_loaded")
        dummies_zeroed = sem("dummies_zeroed")
        consts_base = sem("consts_base")
        consts_ready = sem("consts_ready")
        setup_v = sem("setup_v")
        setup_own = sem("setup_own")
        setup_p = sem("setup_p")
        setup_a = sem("setup_a")
        setup_t = sem("setup_t")
        table_v = sem("table_v")
        table_t = sem("table_t")
        tables_ready = sem("tables_ready")
        regions_filled = sem("regions_filled")
        x_sorted = sem("x_sorted")
        pair_loaded = sems("pair_loaded", 4)
        y_stored = sems("y_stored", 4)
        y_ready = sem("y_ready")
        dense_loaded = sem("dense_loaded")
        dense_product = sem("dense_product")
        dense_added = sem("dense_added")
        dense_stored = sem("dense_stored")
        pairs_placed = sem("pairs_placed")
        y_filled = sem("y_filled")
        pairs_gathered = sems("pairs_gathered", 2)
        h2_loaded = sems("h2_loaded", 2)
        stored = sems("stored", 2)
        o_product = sem("o_product")
        o_scaled = sem("o_scaled")
        o_pooled = sem("o_pooled")
        o_added = sem("o_added")
        N_CONSTS = 17

        def after(eng, step, tile):
            if tile.exists:
                eng.wait_ge(done[step] if isinstance(step, str) else step, tile.t + 1)

        def landed_half(eng, by_parity, tile, dmas=1):
            if tile.exists:
                eng.wait_ge(by_parity[tile.p], tile.half * (16 * dmas) + 16 * dmas)

        def landed_quarter(eng, by_four, tile, dmas=1):
            if tile.exists:
                eng.wait_ge(by_four[tile.q], tile.quarter * (16 * dmas) + 16 * dmas)

        def product_done(eng, tile, s):
            if tile.exists:
                eng.wait_ge(o_product, tile.t * OSLOT + s + 1)

        def scaled_done(eng, tile, s):
            if tile.exists:
                eng.wait_ge(o_scaled, tile.t * len(POOL_SLOTS) + POOL_SLOTS.index(s) + 1)

        def pooled_done(eng, tile, s):
            if tile.exists:
                eng.wait_ge(o_pooled, tile.t * (2 * len(POOL_SLOTS) - 1) + 2 * POOL_SLOTS.index(s) + 1)

        def added_done(eng, tile, s, n=1):
            if tile.exists:
                eng.wait_ge(o_added, tile.t * (2 * len(DVE_SLOTS)) + 2 * DVE_SLOTS.index(s) + 1 + n)

        def run1(eng, step):
            run(eng, step, -6, B + 1, 3, B - 10)

        def run2(eng, step):
            run(eng, step, -5, PAIR_TILES, 4, PAIR_TILES - 9)

        def run3(eng, step):
            run(eng, step, -3, B - 1, 3, B - 6)

        def every_tile(eng, step):
            step(0, True)
            with eng.Fori(1, B) as t:
                step(t, False)

        def branch(eng, sorted_way, dense_way):
            eng.wait_ge(tables_ready, 1)
            flag = eng.value_load(flag_i[0:1, 0:1], min_val=0, max_val=1)
            with eng.If(flag < 1):
                sorted_way()
            with eng.Else():
                dense_way()

        def expert_of(tile):
            if tile.j is None:
                return tile.c if 0 <= tile.c < 3 else None
            return tile.j + 3 if tile.c == 3 else None

        block = ctx.enter_context(nc.Block())

        @block.sync
        def _(sp):
            row = 0
            sp.dma_start(ids_rows[:, :], x).then_inc(inputs_loaded, 16)
            sp.dma_start(sim[:, :, :], sim_matrix.rearrange("(c p) e -> p c e", p=P)).then_inc(inputs_loaded, 16)
            for tab_in in (op_table, var_table, const_table, struct_table):
                sp.dma_start(small[row:row + tab_in.shape[0], :], tab_in).then_inc(small_loaded, 16)
                row += tab_in.shape[0]
            sp.dma_start(bias_raw, b_qkv.unsqueeze(0)).then_inc(inputs_loaded, 16)
            sp.dma_start(gate_tmp[:, :], gates.partition_broadcast(P)).then_inc(inputs_loaded, 16)
            sp.dma_start(w_attn[:, :, :], W_qkv.rearrange("(c p) n -> p c n", p=P)).then_inc(attn_loaded, 16)
            sp.wait_ge(consts_ready, N_CONSTS)
            for n in range(E):
                sp.dma_start(sorted_x[E * REGION + n * P:E * REGION + (n + 1) * P, :], zeros[:, :]
                             ).then_inc(dummies_zeroed, 16)

            def step1(i):
                e = expert_of(i)
                if e is not None:
                    if isinstance(e, int) and e == 0:
                        sp.wait_ge(setup_v, 5)
                    else:
                        sp.wait_ge(weights_hi, e)
                        sp.wait_ge(weights_lo, e)
                    for m, w in enumerate((q_proj, k_proj, v_proj)):
                        src = w[bass.ds(e, 1)].rearrange("e (c p) h -> p (e c) h", p=P)
                        sp.dma_start(raw_qkv[:, :, m * HD:(m + 1) * HD], src).then_inc(qkv_loaded, 16)
                    sp.dma_start(raw_o[:, :], o_proj[bass.ds(e, 1)].rearrange("e h c -> h (e c)")
                                 ).then_inc(o_loaded, 16)
                tile = i.shift(2)
                if tile.inside(B):
                    after(sp, "h2", tile)
                    sp.dma_start(h2_rows[tile.t], h2[tile.p][:, :]).then_inc(h2_stored[tile.p], 16)

            run1(sp, step1)
            for p in range(2):
                sp.wait_ge(h2_stored[p], 16 * (B // 2))

            def sorted_way():
                for e in range(E):
                    at = sp.value_load(fill_i[0:1, e:e + 1], min_val=0, max_val=E * REGION - P)
                    sp.dma_start(sorted_x[bass.ds(at, P), :], zeros[:, :]).then_inc(regions_filled, 16)
                sp.wait_ge(regions_filled, 16 * E)
                sp.wait_ge(dummies_zeroed, 16 * E)
                for q in range(4):
                    sp.wait_ge(scattered[q], 32 * (B // 4))

                def rows_of(tile):
                    return bass.ds(sp.value_load(tab_i[0:1, 1, bass.ds(tile.t, 1)],
                                                 min_val=0, max_val=(E * REGION + E * P) - P), P)

                def step2(i):
                    tile = i.shift(5)
                    if tile.inside(PAIR_TILES):
                        rows = rows_of(tile)
                        after(sp, "pair_turned", tile.shift(-4))
                        sp.dma_start(row_x[:, tile.q, :], sorted_x[rows, :]
                                     ).then_inc(pair_loaded[tile.q], 16)
                    tile = i.shift(-1)
                    if tile.inside(PAIR_TILES):
                        after(sp, "pair_copied", tile)
                        sp.dma_start(sorted_y[bass.ds(tile.t * P, P), :], row_y[:, tile.q, :]
                                     ).then_inc(y_stored[tile.q], 16)

                run2(sp, step2)
                for q in range(4):
                    sp.wait_ge(y_stored[q], 16 * (PAIR_TILES // 4))
                sp.sem_inc(y_ready, 1)

            def dense_way():
                rest = sorted_y[B * P:PAIR_TILES * P, :].rearrange("r y -> (r y)").rearrange(
                    "(n p c) -> n p c", p=P, c=C)
                for n in range(rest.shape[0]):
                    sp.dma_start(rest[n], zeros[:, :]).then_inc(y_filled, 16)
                sp.wait_ge(y_filled, 16 * rest.shape[0])

                def token_tile(t, first):
                    if not first:
                        sp.wait_ge(done["dense_x2"], t)
                    sp.dma_start(row_x[:, 1, :], h2_rows[t]).then_inc(dense_loaded, 16)
                    sp.wait_ge(dense_added, t * E + E)
                    sp.dma_start(sorted_y[bass.ds(t * T, T), :], row_y[:, 0, :]).then_inc(dense_stored, 16)

                every_tile(sp, token_tile)
                sp.wait_ge(dense_stored, 16 * B)
                sp.sem_inc(y_ready, 1)

            branch(sp, sorted_way, dense_way)

            def step3(i):
                tile = i.shift(1)
                if tile.inside(B):
                    added_done(sp, tile.shift(-2), DVE_SLOTS[0], 0)
                    sp.dma_start(row_x[:, tile.p, :], h2_rows[tile.t]).then_inc(h2_loaded[tile.p], 16)
                tile = i
                if tile.inside(B):
                    after(sp, "out_sum", tile)
                    sp.dma_start(out[tile.t], row_x[:, 2 + tile.p, :]).then_inc(stored[tile.p], 16)

            run3(sp, step3)
            for p in range(2):
                sp.wait_ge(stored[p], 16 * (B // 2))

        @block.gpsimd
        def _(pool):
            pool.memset(ident[:, :], 0.0).then_inc(consts_base, 1)
            pool.memset(causal[:, :], 0.0).then_inc(consts_base, 1)
            pool.memset(head_mask[:, :], 1.0).then_inc(consts_base, 1)
            pool.memset(head_of_row[:, :], 1.0).then_inc(consts_base, 1)
            pool.memset(earlier[:, :], 1.0).then_inc(consts_base, 1)
            pool.memset(ones[:, :], 1.0).then_inc(consts_ready, 1)
            pool.memset(zeros[:, :], 0.0).then_inc(consts_ready, 1)
            pool.memset(minus_half[:, :], -0.5).then_inc(consts_ready, 1)
            pool.memset(vx[:, :, :], 1.0).then_inc(consts_ready, 1)
            pool.memset(eps[:, 0:2], LN_EPS).then_inc(consts_ready, 1)
            pool.memset(eps[:, 2:3], NORM_EPS).then_inc(consts_ready, 1)
            pool.memset(third[:, :], -4.0).then_inc(consts_ready, 1)
            for p in range(2):
                pool.memset(moments[p][:, :, :], 1.0).then_inc(consts_ready, 1)
            pool.iota(expert_no[:, :], pattern=[[1, E]], base=0, channel_multiplier=0,
                      allow_small_or_imprecise_dtypes=True).then_inc(consts_ready, 1)
            pool.iota(partition_no[:, :], pattern=[[0, 1]], base=0, channel_multiplier=1,
                      allow_small_or_imprecise_dtypes=True).then_inc(consts_ready, 1)
            pool.iota(region_start[:, :], pattern=[[REGION, E]], base=0, channel_multiplier=0,
                      allow_small_or_imprecise_dtypes=True).then_inc(consts_ready, 1)
            pool.wait_ge(consts_base, 5)
            pool.affine_select(out=ident[:, :], in_=ident[:, :], compare_op=ALU.not_equal, fill=1.0, base=0,
                               pattern=[[-1, P]], channel_multiplier=1).then_inc(consts_ready, 1)
            pool.affine_select(out=causal[:, :], in_=causal[:, :], compare_op=ALU.is_ge, fill=MASKED, base=0,
                               pattern=[[-1, P]], channel_multiplier=1).then_inc(consts_ready, 1)
            pool.affine_select(out=earlier[:, :], in_=earlier[:, :], compare_op=ALU.is_ge, fill=0.0, base=-1,
                               pattern=[[1, P]], channel_multiplier=-1).then_inc(consts_ready, 1)
            hm = head_mask[:, :].rearrange("p (h d) -> p h d", d=D)
            pool.affine_select(out=hm, in_=hm, compare_op=ALU.is_ge, fill=0.0, base=0,
                               pattern=[[-D, HG], [0, D]], channel_multiplier=1).then_inc(consts_base, 1)
            pool.affine_select(out=head_of_row[:, :], in_=head_of_row[:, :], compare_op=ALU.is_ge, fill=0.0,
                               base=0, pattern=[[-D, HG]], channel_multiplier=1).then_inc(consts_base, 1)
            pool.wait_ge(consts_base, 7)
            pool.affine_select(out=hm, in_=hm, compare_op=ALU.is_ge, fill=0.0, base=D - 1,
                               pattern=[[D, HG], [0, D]], channel_multiplier=-1).then_inc(consts_ready, 1)
            pool.affine_select(out=head_of_row[:, :], in_=head_of_row[:, :], compare_op=ALU.is_ge, fill=0.0,
                               base=D - 1, pattern=[[D, HG]], channel_multiplier=-1).then_inc(consts_ready, 1)

            pool.wait_ge(consts_ready, N_CONSTS)
            pool.wait_ge(setup_v, 3)
            pool.tensor_tensor(sim_inv[:, :], sim_norm[:, :], minus_half[:, :], ALU.pow).then_inc(setup_p, 1)
            pool.wait_ge(setup_v, 4)
            pool.wait_ge(small_loaded, 64)

            waits_taken = [0]

            def take_wait():
                n = waits_taken[0] % 8
                waits_taken[0] += 1
                pool.tensor_tensor(waiter[:, n:n + 1], ones[:, 0:1], ones[:, 0:1], ALU.add)

            def offsets(index):
                return bass.IndirectOffsetOnAxis(ap=index, axis=0)

            def step1(i):
                ln1, ln2, norm = i.shift(4), i.shift(1), i
                if ln1.inside(B) or ln2.inside(B) or norm.inside(B):
                    for t, step in ((ln1, "ln1_moments"), (ln2, "ln2_moments"), (norm, "x2_energy")):
                        if t.inside(B):
                            after(pool, step, t)
                    pool.tensor_tensor(roots_eps[i.p][:, :], moments[i.p][:, :, 1], eps[:, :], ALU.add
                                       ).then_inc(done["roots_eps"], 1)
                    after(pool, "roots_eps", i.shift(4))
                    pool.tensor_tensor(roots[i.p][:, :], roots_eps[i.p][:, :], minus_half[:, 0:3], ALU.pow
                                       ).then_inc(done["roots"], 1)
                gather = i.shift(6)
                if gather.inside(B):
                    after(pool, "h2", gather.shift(-4))
                    take_wait()
                    pool.tensor_copy(ids_now[gather.q][:, :],
                                     ids[:, bass.ds(gather.t, 1), :].rearrange("p o n -> p (o n)")
                                     ).then_inc(done["ids_picked"], 1)
                    after(pool, "ids_picked", gather)
                small_rows = i.shift(5)
                scatter = i.shift(-1)
                if small_rows.inside(B):
                    landed_quarter(pool, special_gathered, small_rows)
                if scatter.inside(B):
                    after(pool, "position_index", scatter)
                if small_rows.inside(B) or scatter.inside(B):
                    take_wait()
                if scatter.inside(B):
                    for n in range(2):
                        pool.indirect_dma_start(out=sorted_x, out_offset=offsets(position_u[scatter.q][:, n:n + 1]),
                                                in_=x2[scatter.q][:, :], in_offset=None
                                                ).then_inc(scattered[scatter.q], 16)
                if small_rows.inside(B):
                    q = small_rows.q
                    pool.indirect_dma_start(out=h4[:, q, HALF:C], out_offset=None, in_=small,
                                            in_offset=offsets(ids_now[q][:, 0:1]), bounds_check=N_SMALL - 1,
                                            oob_is_err=False).then_inc(rows_gathered[q], 16)
                if gather.inside(B):
                    q = gather.q
                    pool.indirect_dma_start(out=h4[:, q, 0:HALF], out_offset=None, in_=token_table,
                                            in_offset=offsets(ids_now[q][:, 0:1])
                                            ).then_inc(rows_gathered[q], 16)
                    pool.indirect_dma_start(out=h4[:, q, HALF:C], out_offset=None, in_=special_table,
                                            in_offset=offsets(ids_now[q][:, 1:2]), bounds_check=N_SPECIAL - 1,
                                            oob_is_err=False).then_inc(special_gathered[q], 16)

            run1(pool, step1)
            for q in range(4):
                pool.wait_ge(scattered[q], 32 * (B // 4))
            pool.sem_inc(x_sorted, 1)

            def sorted_way():
                rows = pair_in_x[:, :, :].rearrange("p b n -> p (b n)")
                term, total = [pqT[:, g, :] for g in range(2)], kvm[:, 0, 0:2 * B]
                count = 0
                for e in range(1, E):
                    if e > 2:
                        pool.wait_ge(pairs_placed, count - 1)
                    pool.tensor_scalar(term[e % 2], rows, float(e * REGION), y_step[:, e:e + 1],
                                       ALU.is_ge, ALU.mult).then_inc(pairs_placed, 1)
                    pool.wait_ge(pairs_placed, count + 1)
                    pool.tensor_tensor(total, rows if e == 1 else total, term[e % 2], ALU.add
                                       ).then_inc(pairs_placed, 1)
                    count += 2
                pool.wait_ge(pairs_placed, count)
                pool.tensor_copy(pair_at[:, :, :].rearrange("p b n -> p (b n)"), total).then_inc(pairs_placed, 1)
                pool.wait_ge(pairs_placed, count + 1)

            def dense_way():
                def token_tile(t, first):
                    pool.wait_ge(done["dense_moments"], t + 1)
                    pool.tensor_tensor(roots_eps[0][:, 0:1], moments[0][:, 0, 1:2], eps[:, 0:1], ALU.add
                                       ).then_inc(done["dense_eps"], 1)
                    pool.wait_ge(done["dense_eps"], t + 1)
                    pool.tensor_tensor(roots[0][:, 0:1], roots_eps[0][:, 0:1], minus_half[:, 0:1], ALU.pow
                                       ).then_inc(done["dense_root"], 1)

                every_tile(pool, token_tile)
                pool.memset(pair_w[:, :, 0], 1.0).then_inc(pairs_placed, 1)
                pool.memset(pair_w[:, :, 1], 0.0).then_inc(pairs_placed, 1)
                for n in range(2):
                    pool.iota(pair_at[:, :, n], pattern=[[T, B]], base=0, channel_multiplier=1,
                              allow_small_or_imprecise_dtypes=True).then_inc(pairs_placed, 1)
                pool.wait_ge(pairs_placed, 4)

            branch(pool, sorted_way, dense_way)
            pool.wait_ge(y_ready, 1)

            def add_part(tile, s):
                scaled_done(pool, tile, s)
                k = POOL_SLOTS.index(s)
                part = o_part[k % 2]
                if k:
                    pooled_done(pool, tile, POOL_SLOTS[k - 1])
                else:
                    after(pool, "out_sum", tile.shift(-1))
                if k == 0:
                    pool.tensor_tensor(acc_p[:, :], part[:, 0, :], part[:, 1, :], ALU.add
                                       ).then_inc(o_pooled, 1)
                    return
                pool.tensor_tensor(acc_p[:, :], part[:, 0, :], acc_p[:, :], ALU.add).then_inc(o_pooled, 1)
                if tile.exists:
                    pool.wait_ge(o_pooled, tile.t * (2 * len(POOL_SLOTS) - 1) + 2 * k)
                pool.tensor_tensor(acc_p[:, :], part[:, 1, :], acc_p[:, :], ALU.add).then_inc(o_pooled, 1)

            def step3(i):
                tile = i.shift(3)
                pick = tile.inside(B)
                if pick:
                    after(pool, "qkv_sum", tile.shift(-2))
                    take_wait()
                    pool.tensor_copy(pair_now[tile.p][:, :],
                                     pair_at[:, bass.ds(tile.t, 1), :].rearrange("p o n -> p (o n)")
                                     ).then_inc(done["pair_picked"], 1)
                    after(pool, "pair_picked", tile)
                if i.inside(B):
                    add_part(i, POOL_SLOTS[0])
                if pick:
                    for n in range(2):
                        pool.indirect_dma_start(out=row_y[:, 2 * tile.p + n, :], out_offset=None, in_=sorted_y,
                                                in_offset=offsets(pair_now[tile.p][:, n:n + 1])
                                                ).then_inc(pairs_gathered[tile.p], 16)
                if i.inside(B):
                    for s in POOL_SLOTS[1:]:
                        add_part(i, s)

            run3(pool, step3)

        @block.scalar
        def _(act):
            act.wait_ge(inputs_loaded, 64)
            act.activation(gate_bias[:, :], gate_tmp[:, :], ACT.Exp, scale=-1.0).then_inc(setup_a, 1)
            act.copy(bias[0][:, :], bias_raw).then_inc(setup_a, 1)
            act.wait_ge(consts_ready, N_CONSTS)
            act.copy(ones_r[:, :], ones[0:1, :]).then_inc(setup_a, 1)

            def step1(i):
                tile = i.shift(3)
                if tile.inside(B):
                    after(act, "qk_product", tile)
                    act.activation(qk_neg[:, :], ps_qk[:, :], ACT.Relu, scale=-1.0
                                   ).then_inc(done["qk_negative"], 1)
                    after(act, "qk_negative", tile)
                    act.activation(qk_e[:, :], qk_neg[:, :], ACT.Exp, scale=-1.0).then_inc(done["qk_exp"], 1)
                    after(act, "v_product", tile)
                    act.copy(vx[:, :, 0:P], ps_v[:, 0:C].rearrange("p (g n) -> p g n", g=G)
                             ).then_inc(done["v_copied"], 1)
                tile = i.shift(4)
                if tile.inside(B):
                    after(act, "x1_turned", tile)
                    act.copy(x1T[:, :], ps_x1[:, 0:C]).then_inc(done["x1_T"], 1)
                tile = i.shift(1)
                if tile.inside(B):
                    after(act, "x2_normed", tile)
                    act.activation(squares[:, :], x2[tile.q][:, :], ACT.Square, accum_out=moments[i.shift(1).p][:, 2, 1:2]
                                   ).then_inc(done["x2_energy"], 1)
                    after(act, "x2_turned", tile)
                    act.copy(x2T[:, :], ps_x2[:, 0:C]).then_inc(done["x2_T"], 1)
                tile = i
                if tile.inside(B):
                    after(act, "gate_negmax", tile)
                    act.activation(gexp[:, :], gated[:, :], ACT.Exp, bias=gneg[:, 0:1]
                                   ).then_inc(done["gate_exp"], 1)
                tile = i.shift(3)
                if tile.inside(B):
                    after(act, "phi_q_turned", tile)
                    act.copy(pqT[:, :, :].rearrange("p g t -> p (g t)"), ps_pq[:, 0:C]
                             ).then_inc(done["phi_q_T"], 1)
                e = expert_of(i)
                if e is not None:
                    act.wait_ge(qkv_loaded, e * 48 + 48)
                    act.wait_ge(o_loaded, e * 16 + 16)
                    act.copy(wq[0][:, bass.ds(e, 1), :, :].rearrange("p e c n -> p (e c n)"),
                             raw_qkv[:, :, :].rearrange("p c n -> p (c n)"))
                    act.copy(wo[0][:, bass.ds(e, 1), :].rearrange("p e n -> p (e n)"), raw_o[:, :]
                             ).then_inc(weights_hi, 1)

            run1(act, step1)

            def sorted_way():
                def step2(i):
                    tile = i.shift(2)
                    if tile.inside(PAIR_TILES):
                        after(act, "pair_product", tile.shift(-4))
                        after(act, "pair_turned", tile)
                        act.copy(split[tile.q][0][:, :, :].rearrange("p c t -> p (c t)"),
                                 ps_turn[tile.p][:, 0:C]).then_inc(done["pair_hi"], 1)
                    if i.inside(PAIR_TILES) and i.p:
                        landed_quarter(act, y_stored, i.shift(-4))
                        after(act, "pair_copied", i.shift(-1))
                        after(act, "pair_product", i)
                        act.copy(row_y[:, i.q, :], ps_y[i.q][:, 0:Y]).then_inc(done["pair_copied"], 1)

                run2(act, step2)

            def dense_way():
                def token_tile(t, first):
                    act.wait_ge(done["dense_turned"], t + 1)
                    act.copy(split[0][0][:, :, :].rearrange("p c t -> p (c t)"), ps_turn[0][:, 0:C]
                             ).then_inc(done["dense_hi"], 1)

                every_tile(act, token_tile)

            branch(act, sorted_way, dense_way)

            def scale_slot(tile, s):
                k = POOL_SLOTS.index(s)
                if k == 0:
                    after(act, "o_weights", tile)
                user, back = (k - 2, 0) if k >= 2 else (2 if k == 0 else 1, 1)
                pooled_done(act, tile.shift(-back), POOL_SLOTS[user])
                product_done(act, tile, s)
                part, ps = o_part[k % 2], ps_o[s % 3]
                for j in range(2):
                    e = 2 * s + j
                    last = act.mul(part[:, j, :], ps[:, j * C:(j + 1) * C], rwo[tile.p][:, e:e + 1])
                last.then_inc(o_scaled, 1)

            def step3(i):
                nxt = i.shift(1)
                if i.inside(B):
                    scale_slot(i, POOL_SLOTS[0])
                if nxt.inside(B):
                    after(act, "heads_turned", nxt)
                    act.copy(headsT[:, :, :].rearrange("p a t -> p (a t)"), ps_heads[:, 0:2 * P]
                             ).then_inc(done["heads_T"], 1)
                    after(act, "scores_negmax", nxt)
                    act.activation(pr[:, :], sc[:, :], ACT.Exp, bias=sneg[:, 0:1], accum_out=psumm[:, 0:1]
                                   ).then_inc(done["probs"], 1)
                if i.inside(B):
                    scale_slot(i, POOL_SLOTS[1])
                if nxt.inside(B):
                    after(act, "probs_turned", nxt)
                    act.copy(prT[:, :], ps_prob[:, 0:P]).then_inc(done["probs_T"], 1)
                    product_done(act, nxt.shift(-2), OSLOT - 1)
                    after(act, "ao_product", nxt)
                    act.copy(aoT[nxt.p][0], ps_ao[:, 0:P]).then_inc(done["aoT_hi"], 1)
                if i.inside(B):
                    scale_slot(i, POOL_SLOTS[2])

            run3(act, step3)

        @block.vector
        def _(dve):
            def ln_moments(tile, n, src, mv):
                dve.bn_stats(stats[:, n - 1, :], src).then_inc(done[f"ln{n}_stats"], 1)
                after(dve, f"ln{n}_stats", tile)

            dve.wait_ge(inputs_loaded, 64)
            dve.tensor_copy(ids_rows_f[:, :], ids_rows[:, :]).then_inc(setup_v, 1)
            dve.tensor_tensor(sim_sq[:, :, :], sim[:, :, :], sim[:, :, :], ALU.mult).then_inc(setup_v, 1)
            dve.wait_ge(setup_t, 1)
            dve.tensor_copy(ids_f[:, :], ps_x1[:, 0:B]).then_inc(setup_own, 1)
            dve.wait_ge(setup_t, 2)
            dve.tensor_scalar(sim_norm[:, :], ps_qk[:, 0:E], NORM_EPS, None, ALU.add).then_inc(setup_v, 1)
            dve.wait_ge(setup_own, 1)
            dve.tensor_scalar(ids_low[:, :], ids_f[:, :], float(N_SMALL), float(2 ** 22), ALU.is_lt, ALU.mult
                              ).then_inc(setup_own, 1)
            dve.wait_ge(setup_own, 2)
            dve.tensor_copy(ids[:, :, 0], ids_f[:, :])
            dve.scalar_tensor_tensor(ids[:, :, 1], ids_f[:, :], float(N_SMALL), ids_low[:, :],
                                     ALU.subtract, ALU.add).then_inc(setup_v, 1)
            dve.wait_ge(setup_a, 2)
            dve.tensor_tensor(bias[1][:, :], bias_raw, bias[0][:, :].bitcast(F32), ALU.subtract
                              ).then_inc(setup_v, 1)
            dve.tensor_scalar(gate_tmp[:, :], gate_bias[:, :], 1.0, None, ALU.add).then_inc(setup_own, 1)
            dve.wait_ge(setup_own, 3)
            dve.reciprocal(gate_bias[:, :], gate_tmp[:, :]).then_inc(setup_own, 1)
            dve.wait_ge(consts_ready, N_CONSTS)
            dve.tensor_copy(next_row[:, :], region_start[:, :]).then_inc(setup_own, 1)
            dve.wait_ge(setup_p, 1)
            dve.tensor_tensor(simn[:, :, :], sim[:, :, :], sim_inv[:, :].unsqueeze(1).broadcast_to([P, CH, E]),
                              ALU.mult).then_inc(setup_v, 1)
            dve.wait_ge(setup_own, 5)

            def step1(i):
                tile = i.shift(2)
                if tile.inside(B):
                    after(dve, "attn_sums", tile)
                    dve.tensor_scalar(den[:, :, :], ps_sums[:, :, P:NUMW], DEN_EPS, None, ALU.add
                                      ).then_inc(done["attn_den"], 1)
                    after(dve, "attn_den", tile)
                    dve.reciprocal(zden[:, :, :], den[:, :, :]).then_inc(done["attn_z"], 1)
                    after(dve, "attn_z", tile)
                    dve.tensor_tensor(attn[:, :].rearrange("p (g h d) -> p g h d", g=G, d=D),
                                      ps_sums[:, :, 0:P].rearrange("p g (h d) -> p g h d", d=D),
                                      zden[:, :, :].unsqueeze(3).broadcast_to([P, G, HG, D]), ALU.mult
                                      ).then_inc(done["attn"], 1)
                    after(dve, "attn", tile)
                    landed_half(dve, h2_stored, tile.shift(-2))
                    dve.tensor_tensor(h2[tile.p][:, :], h4[:, tile.q, :], attn[:, :], ALU.add
                                      ).then_inc(done["h2"], 1)
                    after(dve, "h2", tile)
                    dve.bn_stats(stats[:, 1, :], h2[tile.p][:, :]).then_inc(done["ln2_stats"], 1)
                roots_ready = i.shift(4)
                x1_tile, x2_tile = i.shift(4), i.shift(1)
                if x1_tile.inside(B):
                    after(dve, "x1_turned", x1_tile.shift(-1))
                if x1_tile.inside(B) or x2_tile.inside(B) or i.inside(B):
                    after(dve, "roots", roots_ready)
                if x1_tile.inside(B):
                    dve.tensor_scalar(x1[:, :], h4[:, x1_tile.q, :], moments[i.p][:, 0, 0:1], roots[i.p][:, 0:1],
                                      ALU.subtract, ALU.mult).then_inc(done["x1_normed"], 1)
                if tile.inside(B):
                    after(dve, "ln2_stats", tile)
                if i.inside(B):
                    after(dve, "logits_product", i)
                    dve.scalar_tensor_tensor(logits[:, :], ps_gate[:, 0:E], roots[i.p][:, 2:3], gate_bias[:, :],
                                             ALU.mult, ALU.subtract).then_inc(done["logits"], 1)
                elif tile.inside(B):
                    dve.tensor_copy(idle[:, :], ones[:, 0:1])
                if tile.inside(B):
                    dve.bn_aggr(moments[i.shift(1).p][:, 1, :], stats[:, 1, :]).then_inc(done["ln2_moments"], 1)
                if x2_tile.inside(B):
                    landed_quarter(dve, scattered, x2_tile.shift(-4), dmas=2)
                    dve.tensor_scalar(x2[x2_tile.q][:, :], h2[x2_tile.p][:, :], moments[i.p][:, 1, 0:1],
                                      roots[i.p][:, 1:2], ALU.subtract, ALU.mult
                                      ).then_inc(done["x2_normed"], 1)
                if i.inside(B):
                    after(dve, "logits", i)
                    dve.tensor_scalar(gated[:, :], logits[:, :], 0.0, None, ALU.max)
                    dve.max(top[:, :], logits[:, :]).then_inc(done["top_values"], 1)
                    dve.tensor_scalar(active[:, :], logits[:, :], 0.0, None, ALU.is_gt)
                    after(dve, "top_values", i)
                    dve.tensor_scalar(gneg[:, :], top[:, 0:1], 0.0, -1.0, ALU.max, ALU.mult
                                      ).then_inc(done["gate_negmax"], 1)
                    dve.max_index(top_at[:, :], top[:, :], logits[:, :]).then_inc(done["top_indices"], 1)
                    dve.tensor_scalar(idle[:, :], top[:, 0:1], 0.0, None, ALU.is_le)
                    dve.tensor_tensor(third[:, :], third[:, :], top[:, 2:3], ALU.max)
                tile = i.shift(3)
                if tile.inside(B):
                    after(dve, "qk_exp", tile)
                    dve.scalar_tensor_tensor(phi[:, :], ps_qk[:, :], 0.0, qk_e[:, :], ALU.max, ALU.add
                                             ).then_inc(done["phi"], 1)
                if i.inside(B):
                    after(dve, "top_indices", i)
                    dve.tensor_scalar(is_one[:, :], expert_no[:, :], top_at[:, 0:1], None, ALU.is_equal)
                    dve.tensor_scalar(is_two[:, :], expert_no[:, :], top_at[:, 1:2], None, ALU.is_equal
                                      ).then_inc(done["is_two"], 1)
                    after(dve, "is_two", i)
                    dve.tensor_tensor(top_two[:, :], is_one[:, :], is_two[:, :], ALU.add
                                      ).then_inc(done["top_two"], 1)
                    after(dve, "top_two", i)
                    dve.scalar_tensor_tensor(gmask[:, :], top_two[:, :], idle[:, 0:1], active[:, :],
                                             ALU.mult, ALU.max).then_inc(done["gate_mask"], 1)
                    after(dve, "gate_mask", i)
                    after(dve, "gate_exp", i)
                    dve.scalar_tensor_tensor(gsel[:, :], gexp[:, :], 1.0, gmask[:, :], ALU.mult, ALU.mult,
                                             accum_out=gsum[:, 0:1]).then_inc(done["gate_sum"], 1)
                    after(dve, "gate_sum", i)
                    dve.reciprocal(gsum[:, 1:2], gsum[:, 0:1]).then_inc(done["gate_rsum"], 1)
                if tile.inside(B):
                    after(dve, "kv_product", tile)
                    dve.tensor_tensor(kvm[:, :, 0:P], ps_kv[:, :, 0:P],
                                      head_mask[:, :].unsqueeze(1).broadcast_to([P, G, P]), ALU.mult)
                    dve.tensor_tensor(kvm[:, :, P:NUMW], ps_kv[:, :, P:P + 1].broadcast_to([P, G, HG]),
                                      head_of_row[:, :].unsqueeze(1).broadcast_to([P, G, HG]), ALU.mult
                                      ).then_inc(done["kv_masked"], 1)
                if i.inside(B):
                    now = routing[:, bass.ds(i.t, 1), :].rearrange("p o e -> p (o e)")
                    after(dve, "gate_rsum", i)
                    dve.tensor_scalar(now, gsel[:, :], gsum[:, 1:2], None, ALU.mult).then_inc(done["routing"], 1)
                    after(dve, "rank_product", i)
                    dve.tensor_tensor(ranks[:, :], ps_rank[:, 0:E], next_row[:, :], ALU.add
                                      ).then_inc(done["ranks"], 1)
                    after(dve, "ranks", i)
                    dve.tensor_tensor(next_row[:, :], ps_rank[:, E:2 * E], next_row[:, :], ALU.add
                                      ).then_inc(done["count"], 1)
                    for n, mine in enumerate((is_one, is_two)):
                        last = dve.scalar_tensor_tensor(picked[:, n, :], ranks[:, :], 1.0, mine[:, :], ALU.mult,
                                                        ALU.mult, accum_out=position[:, n:n + 1])
                    last.then_inc(done["position"], 1)
                    after(dve, "routing", i)
                    for n, mine in enumerate((is_one, is_two)):
                        last = dve.scalar_tensor_tensor(
                            picked[:, 2 + n, :], now, 1.0, mine[:, :], ALU.mult, ALU.mult,
                            accum_out=pair_w[:, bass.ds(i.t, 1), n:n + 1].rearrange("p o n -> p (o n)"))
                    last.then_inc(done["pair_weights"], 1)
                    after(dve, "position", i)
                    dve.tensor_copy(position_u[i.q][:, :], position[:, :]).then_inc(done["position_index"], 1)
                    dve.tensor_copy(pair_in_x[:, bass.ds(i.t, 1), :].rearrange("p o n -> p (o n)"), position[:, :]
                                    ).then_inc(done["position_kept"], 1)
                tile = i.shift(5)
                if tile.inside(B):
                    landed_quarter(dve, rows_gathered, tile, dmas=2)
                    dve.bn_stats(stats[:, 0, :], h4[:, tile.q, :]).then_inc(done["ln1_stats"], 1)
                e = expert_of(i)
                if tile.inside(B):
                    after(dve, "ln1_stats", tile)
                    dve.tensor_copy(tab_tmp[:, 0:1], ones[:, 0:1])
                    dve.bn_aggr(moments[i.shift(1).p][:, 0, :], stats[:, 0, :]).then_inc(done["ln1_moments"], 1)
                if e is not None:
                    dve.wait_ge(weights_hi, e + 1)
                    dve.tensor_tensor(wq[1][:, bass.ds(e, 1), :, :].rearrange("p e c n -> p (e c n)"),
                                      raw_qkv[:, :, :].rearrange("p c n -> p (c n)"),
                                      wq[0][:, bass.ds(e, 1), :, :].rearrange("p e c n -> p (e c n)").bitcast(F32),
                                      ALU.subtract)
                    dve.tensor_tensor(wo[1][:, bass.ds(e, 1), :].rearrange("p e n -> p (e n)"), raw_o[:, :],
                                      wo[0][:, bass.ds(e, 1), :].rearrange("p e n -> p (e n)").bitcast(F32),
                                      ALU.subtract).then_inc(weights_lo, 1)

            run1(dve, step1)

            chain = [0]

            def link(ins):
                chain[0] += 1
                ins.then_inc(table_v, 1)
                dve.wait_ge(table_v, chain[0])

            dve.wait_ge(done["count"], B)
            link(dve.tensor_tensor(ranks[:, :], next_row[:, :], region_start[:, :], ALU.subtract))
            link(dve.tensor_scalar(tiles_i[:, :], ranks[:, :], float(P - 1), None, ALU.add))
            link(dve.tensor_scalar(tiles_i[:, :], tiles_i[:, :], P.bit_length() - 1, None,
                                   ALU.arith_shift_right))
            link(dve.tensor_copy(tiles_f[:, :], tiles_i[:, :]))
            link(dve.tensor_tensor_scan(tiles_cum[:, :], ones[:, 0:E], tiles_f[:, :], 0.0, ALU.mult, ALU.add))
            link(dve.tensor_tensor(before[:, :], tiles_cum[:, :], tiles_f[:, :], ALU.subtract))
            link(dve.scalar_tensor_tensor(y_shift[:, :], before[:, :], float(P), region_start[:, :], ALU.mult,
                                          ALU.subtract))
            link(dve.tensor_tensor(y_step[:, 1:E], y_shift[:, 1:E], y_shift[:, 0:E - 1], ALU.subtract))
            for g in range(2):
                number, count, earlier_tiles, within = [tab_tmp[:, k:k + 1] for k in range(4)]
                link(dve.tensor_scalar(number, partition_no[:, :], float(g * P), None, ALU.add))
                link(dve.tensor_scalar(before[:, :], tiles_cum[:, :], number, None, ALU.is_le))
                link(dve.tensor_reduce(count, before[:, :], AX_X, ALU.add))
                link(dve.scalar_tensor_tensor(picked[:, 0, :], before[:, :], 1.0, tiles_f[:, :], ALU.mult,
                                              ALU.mult, accum_out=earlier_tiles))
                link(dve.scalar_tensor_tensor(within, number, earlier_tiles, number, ALU.subtract, ALU.bypass))
                link(dve.tensor_scalar(within, within, float(P), None, ALU.mult))
                link(dve.tensor_scalar(tab[:, g, 0:1], count, float(E - 1), None, ALU.min))
                link(dve.scalar_tensor_tensor(tab[:, g, 1:2], count, float(REGION), within, ALU.mult, ALU.add))
            dve.wait_ge(table_t, 1)
            dve.tensor_copy(tab_i[0:1, :, :].rearrange("p n t -> p (n t)"), ps_x1[0:1, 0:4 * P])
            dve.tensor_copy(fill_i[:, :], next_row[0:1, :])
            link(dve.tensor_reduce(flag_f[:, :], ps_qk[0:1, 0:P], AX_X, ALU.max))
            link(dve.tensor_scalar(flag_i[:, :], flag_f[:, :], 0.0, None, ALU.is_gt))
            dve.sem_inc(tables_ready, 1)

            def sorted_way():
                def step2(i):
                    tile = i.shift(2)
                    if tile.inside(PAIR_TILES):
                        after(dve, "pair_hi", tile)
                        hi, lo = [w[:, :, :].rearrange("p c t -> p (c t)") for w in split[tile.q]]
                        dve.tensor_tensor(lo, ps_turn[tile.p][:, 0:C], hi.bitcast(F32), ALU.subtract
                                          ).then_inc(done["pair_lo"], 1)
                    if i.inside(PAIR_TILES) and not i.p:
                        landed_quarter(dve, y_stored, i.shift(-4))
                        after(dve, "pair_copied", i.shift(-1))
                        after(dve, "pair_product", i)
                        dve.tensor_copy(row_y[:, i.q, :], ps_y[i.q][:, 0:Y]).then_inc(done["pair_copied"], 1)

                run2(dve, step2)

            def dense_way():
                def token_tile(t, first):
                    now = routing[:, bass.ds(t, 1), :].rearrange("p o e -> p (o e)")
                    if not first:
                        dve.wait_ge(dense_stored, t * 16)
                    dve.wait_ge(dense_loaded, t * 16 + 16)
                    dve.bn_stats(stats[:, 0, :], row_x[:, 1, :]).then_inc(done["dense_stats"], 1)
                    dve.wait_ge(done["dense_stats"], t + 1)
                    dve.tensor_copy(tab_tmp[:, 0:1], ones[:, 0:1])
                    dve.bn_aggr(moments[0][:, 0, :], stats[:, 0, :]).then_inc(done["dense_moments"], 1)
                    dve.wait_ge(done["dense_root"], t + 1)
                    dve.tensor_scalar(row_x[:, 0, :], row_x[:, 1, :], moments[0][:, 0, 0:1], roots[0][:, 0:1],
                                      ALU.subtract, ALU.mult).then_inc(done["dense_x2"], 1)
                    dve.tensor_copy(rwo[0][:, :], now)
                    dve.wait_ge(done["dense_hi"], t + 1)
                    hi, lo = [w[:, :, :].rearrange("p c t -> p (c t)") for w in split[0]]
                    dve.tensor_tensor(lo, ps_turn[0][:, 0:C], hi.bitcast(F32), ALU.subtract
                                      ).then_inc(done["dense_lo"], 1)
                    for e in range(E):
                        if e:
                            dve.wait_ge(dense_added, t * E + e)
                        dve.wait_ge(dense_product, t * E + e + 1)
                        src, acc = ps_y[e % 4][:, 0:Y], row_y[:, 0, :]
                        if e == 0:
                            dve.wait_ge(done["dense_lo"], t + 1)
                            ins = dve.tensor_scalar(acc, src, rwo[0][:, 0:1], None, ALU.mult)
                        else:
                            ins = dve.scalar_tensor_tensor(acc, src, rwo[0][:, e:e + 1], acc, ALU.mult, ALU.add)
                        ins.then_inc(dense_added, 1)

                every_tile(dve, token_tile)

            branch(dve, sorted_way, dense_way)

            def add_slot(tile, s):
                k = DVE_SLOTS.index(s)
                if k == 0:
                    landed_half(dve, h2_loaded, tile)
                    after(dve, "out_sum", tile.shift(-1))
                else:
                    added_done(dve, tile, DVE_SLOTS[k - 1])
                product_done(dve, tile, s)
                for j in range(2):
                    if j:
                        added_done(dve, tile, s, 0)
                    e = 2 * s + j
                    base = row_x[:, tile.p, :] if k == 0 and j == 0 else acc_v[:, :]
                    dve.scalar_tensor_tensor(acc_v[:, :], ps_o[s % 3][:, j * C:(j + 1) * C],
                                             rwo[tile.p][:, e:e + 1], base, ALU.mult, ALU.add
                                             ).then_inc(o_added, 1)

            def step3(i):
                nxt, after_nxt = i.shift(1), i.shift(2)
                if i.inside(B):
                    add_slot(i, DVE_SLOTS[0])
                if after_nxt.inside(B):
                    p = after_nxt.p
                    w = [pair_w[:, bass.ds(after_nxt.t, 1), n:n + 1].rearrange("p o n -> p (o n)")
                         for n in range(2)]
                    landed_half(dve, pairs_gathered, after_nxt, dmas=2)
                    after(dve, "ao_product", after_nxt.shift(-2))
                    dve.tensor_scalar(qkv[p][:, :], row_y[:, 2 * p, :], w[0], None, ALU.mult
                                      ).then_inc(done["first_row"], 1)
                if i.inside(B):
                    add_slot(i, DVE_SLOTS[1])
                if after_nxt.inside(B):
                    after(dve, "first_row", after_nxt)
                    dve.scalar_tensor_tensor(qkv[p][:, :], row_y[:, 2 * p + 1, :], w[1], qkv[p][:, :],
                                             ALU.mult, ALU.add).then_inc(done["qkv_sum"], 1)
                if nxt.inside(B):
                    after(dve, "scores", nxt)
                    dve.scalar_tensor_tensor(sc[:, :], ps_score[:, 0:P], SCALE, causal[:, :], ALU.mult,
                                             ALU.add).then_inc(done["scores_masked"], 1)
                    after(dve, "scores_masked", nxt)
                    dve.tensor_reduce(sneg[:, :], sc[:, :], AX_X, ALU.max, negate=True
                                      ).then_inc(done["scores_negmax"], 1)
                if i.inside(B):
                    add_slot(i, DVE_SLOTS[2])
                if nxt.inside(B):
                    after(dve, "probs", nxt)
                    dve.reciprocal(psumm[:, 1:2], psumm[:, 0:1]).then_inc(done["probs_rsum"], 1)
                    after(dve, "probs_rsum", nxt)
                    dve.tensor_scalar(rwo[nxt.p][:, :], routing[:, bass.ds(nxt.t, 1), :].rearrange(
                        "p o e -> p (o e)"), psumm[:, 1:2], None, ALU.mult).then_inc(done["o_weights"], 1)
                if i.inside(B):
                    add_slot(i, DVE_SLOTS[3])
                    if len(DVE_SLOTS) > 5:
                        add_slot(i, DVE_SLOTS[4])
                if nxt.inside(B):
                    after(dve, "aoT_hi", nxt)
                    dve.tensor_tensor(aoT[nxt.p][1], ps_ao[:, 0:P], aoT[nxt.p][0].bitcast(F32), ALU.subtract
                                      ).then_inc(done["aoT_lo"], 1)
                if i.inside(B):
                    add_slot(i, DVE_SLOTS[-1])
                    added_done(dve, i, DVE_SLOTS[-1])
                    pooled_done(dve, i, POOL_SLOTS[-1])
                    landed_half(dve, stored, i.shift(-2))
                    dve.tensor_tensor(row_x[:, 2 + i.p, :], acc_v[:, :], acc_p[:, :], ALU.add
                                      ).then_inc(done["out_sum"], 1)

            run3(dve, step3)

        @block.tensor
        def _(pe):
            def product(ps, left, right):
                n = len(left[0])
                for c in range(n):
                    pe.matmul(ps, left[1][c], right[0][c], start=(c == 0), stop=False)
                    pe.matmul(ps, left[0][c], right[1][c], start=False, stop=False)
                    last = pe.matmul(ps, left[0][c], right[0][c], start=False, stop=(c == n - 1))
                return last

            def turn(ps, *pieces):
                for n, piece in enumerate(pieces):
                    last = pe.transpose(ps[:, n * P:(n + 1) * P], piece, ident[:, :])
                return last

            def halves(t):
                return [t[:, c * P:(c + 1) * P] for c in range(2)]

            pe.wait_ge(consts_ready, N_CONSTS)
            pe.wait_ge(setup_v, 1)
            pe.transpose(ps_x1[:, 0:B], ids_rows_f[:, :], ident[0:B, 0:B]).then_inc(setup_t, 1)
            pe.wait_ge(setup_v, 2)
            for c in range(CH):
                last = pe.matmul(ps_qk[:, 0:E], ones[:, :], sim_sq[:, c, :], start=(c == 0), stop=(c == CH - 1))
            last.then_inc(setup_t, 1)
            pe.wait_ge(attn_loaded, 16)
            pe.wait_ge(setup_a, 3)
            pe.wait_ge(setup_v, 6)

            def step1(i):
                tile = i.shift(4)
                if tile.inside(B):
                    after(pe, "x1_T", tile.shift(-1))
                    after(pe, "x1_normed", tile)
                    turn(ps_x1, *halves(x1)).then_inc(done["x1_turned"], 1)
                tile = i.shift(1)
                if tile.inside(B):
                    after(pe, "ranks", tile.shift(-2))
                    after(pe, "count", tile.shift(-2))
                    after(pe, "x2_normed", tile)
                    turn(ps_x2, *halves(x2[tile.q])).then_inc(done["x2_turned"], 1)
                tile = i.shift(3)
                if tile.inside(B):
                    after(pe, "v_copied", tile)
                    after(pe, "phi_q_T", tile.shift(-1))
                    after(pe, "kv_masked", tile.shift(-1))
                    after(pe, "phi", tile)
                    turn(ps_pq, *halves(phi)).then_inc(done["phi_q_turned"], 1)
                    for g in range(G):
                        last = pe.matmul(ps_kv[:, g, :], phi[:, C + g * P:C + (g + 1) * P], vx[:, g, :],
                                         start=True, stop=True)
                    last.then_inc(done["kv_product"], 1)
                tile = i.shift(1)
                if tile.inside(B):
                    after(pe, "logits", tile.shift(-1))
                    after(pe, "x2_T", tile)
                    for c in range(CH):
                        last = pe.matmul(ps_gate[:, 0:E], halves(x2T)[c], simn[:, c, :], start=(c == 0),
                                         stop=(c == CH - 1))
                    last.then_inc(done["logits_product"], 1)
                if i.inside(B):
                    after(pe, "x2_T", i.shift(1) if i.shift(1).inside(B) else i)
                    after(pe, "top_two", i)
                    pe.matmul(ps_rank[:, 0:E], earlier[:, :], top_two[:, :], start=True, stop=True)
                    pe.matmul(ps_rank[:, E:2 * E], ones[:, :], top_two[:, :], start=True, stop=True
                              ).then_inc(done["rank_product"], 1)
                tile = i.shift(3)
                if tile.inside(B):
                    after(pe, "attn", tile.shift(-1))
                    after(pe, "phi_q_T", tile)
                    after(pe, "kv_masked", tile)
                    for g in range(G):
                        last = pe.matmul(ps_sums[:, g, :], pqT[:, g, :], kvm[:, g, :], start=True, stop=True)
                    last.then_inc(done["attn_sums"], 1)
                tile = i.shift(4)
                if tile.inside(B):
                    after(pe, "phi", tile.shift(-1))
                    after(pe, "v_copied", tile.shift(-1))
                    after(pe, "x1_T", tile)
                    for ps, lo, hi, name in ((ps_qk, 0, 2 * C, "qk_product"), (ps_v, 2 * C, 3 * C, "v_product")):
                        for n in range(2):
                            pe.matmul(ps[:, 0:hi - lo], ones_r[:, :], bias[n][:, lo:hi], start=(n == 0), stop=False)
                        for c in range(CH):
                            last = pe.matmul(ps[:, 0:hi - lo], halves(x1T)[c], w_attn[:, c, lo:hi], start=False,
                                             stop=(c == CH - 1))
                        last.then_inc(done[name], 1)

            run1(pe, step1)

            pe.wait_ge(table_v, 8 + 2 * 8)
            for n in range(2):
                for g in range(2):
                    pe.transpose(ps_x1[0:1, (2 * n + g) * P:(2 * n + g + 1) * P], tab[:, g, n:n + 1], ident[:, :])
            pe.transpose(ps_qk[0:1, 0:P], third[:, :], ident[:, :]).then_inc(table_t, 1)

            def sorted_way():
                pe.wait_ge(weights_lo, E)

                def step2(i):
                    tile = i.shift(2)
                    if tile.inside(PAIR_TILES):
                        after(pe, "pair_lo", tile.shift(-2))
                        landed_quarter(pe, pair_loaded, tile)
                        turn(ps_turn[tile.p], *halves(row_x[:, tile.q, :])).then_inc(done["pair_turned"], 1)
                    if i.inside(PAIR_TILES):
                        e = pe.value_load(tab_i[0:1, 0, bass.ds(i.t, 1)], min_val=0, max_val=E - 1)
                        after(pe, "pair_copied", i.shift(-4))
                        after(pe, "pair_lo", i)
                        product(ps_y[i.q][:, 0:Y], [[w[:, c, :] for c in range(CH)] for w in split[i.q]],
                                [[w[:, bass.ds(e, 1), c, :].rearrange("p e n -> p (e n)") for c in range(CH)]
                                 for w in wq]).then_inc(done["pair_product"], 1)

                run2(pe, step2)

            def dense_way():
                pe.wait_ge(weights_lo, E)
                def token_tile(t, first):
                    if not first:
                        pe.wait_ge(dense_added, t * E)
                    pe.wait_ge(done["dense_x2"], t + 1)
                    turn(ps_turn[0], *halves(row_x[:, 0, :])).then_inc(done["dense_turned"], 1)
                    for e in range(E):
                        if e >= 4:
                            pe.wait_ge(dense_added, t * E + e - 3)
                        if e == 0:
                            pe.wait_ge(done["dense_lo"], t + 1)
                        product(ps_y[e % 4][:, 0:Y], [[w[:, c, :] for c in range(CH)] for w in split[0]],
                                [[w[:, e, c, :] for c in range(CH)] for w in wq]).then_inc(dense_product, 1)

                every_tile(pe, token_tile)

            branch(pe, sorted_way, dense_way)
            pe.wait_ge(y_ready, 1)

            def bank_before(s):
                n = max(k for k in range(s - OSLOT, s) if k % OSLOT % 3 == s % 3)
                return n % OSLOT, 0 if n >= 0 else 1

            def o_slot(tile, s):
                user, back = bank_before(s)
                (scaled_done if user in POOL_SLOTS else added_done)(pe, tile.shift(-back), user)
                if s == 0:
                    after(pe, "aoT_lo", tile)
                for j in range(2):
                    last = product(ps_o[s % 3][:, j * C:(j + 1) * C], [[a] for a in aoT[tile.p]],
                                   [[w[:, 2 * s + j, :]] for w in wo])
                last.then_inc(o_product, 1)

            def step3(i):
                nxt = i.shift(1)

                def slots(*ss):
                    if i.inside(B):
                        for s in ss:
                            o_slot(i, s)

                slots(0)
                if nxt.inside(B):
                    after(pe, "heads_T", nxt.shift(-1))
                    after(pe, "qkv_sum", nxt)
                    turn(ps_heads, *halves(qkv[nxt.p])).then_inc(done["heads_turned"], 1)
                slots(1)
                if nxt.inside(B):
                    after(pe, "scores_masked", nxt.shift(-1))
                    after(pe, "heads_T", nxt)
                    pe.matmul(ps_score[:, 0:P], headsT[:, 0, :], headsT[:, 1, :], start=True, stop=True
                              ).then_inc(done["scores"], 1)
                slots(2, 3)
                if nxt.inside(B):
                    after(pe, "probs_T", nxt.shift(-1))
                    after(pe, "probs", nxt)
                    turn(ps_prob, pr[:, :]).then_inc(done["probs_turned"], 1)
                slots(4)
                if nxt.inside(B):
                    after(pe, "aoT_lo", nxt.shift(-1))
                    after(pe, "probs_T", nxt)
                    pe.matmul(ps_ao[:, 0:P], qkv[nxt.p][:, 2 * HD:3 * HD], prT[:, :], start=True, stop=True
                              ).then_inc(done["ao_product"], 1)
                slots(5, 6, 7)

            run3(pe, step3)


_INS = ["x", "L0_tok_token_table", "L0_tok_op_table", "L0_tok_var_table", "L0_tok_const_table",
        "L0_tok_struct_table", "L0_tok_special_table", "L0_attn_W_qkv", "L0_attn_b_qkv", "L0_attn_W_proj",
        "L0_attn_b_proj", "L0_ffn_sim_matrix", "L0_ffn_gates", "L0_ffn_q_proj", "L0_ffn_k_proj",
        "L0_ffn_v_proj", "L0_ffn_o_proj"]


def kernel(**inputs):
    import numpy as _np
    import concourse.bacc as _bacc
    from concourse import mybir as _mybir
    from concourse.bass_utils import run_bass_kernel_spmd as _run

    nc = _bacc.Bacc("TRN2", target_bir_lowering=False, num_devices=1)
    arrays, args = {}, []
    for name in _INS:
        a = _np.ascontiguousarray(inputs[name])
        arrays[f"in_{name}"] = a
        args.append(nc.dram_tensor(f"in_{name}", a.shape, _mybir.dt.from_np(a.dtype), kind="ExternalInput").ap())
    b, t = inputs["x"].shape
    c = 2 * inputs["L0_tok_token_table"].shape[1]
    args.append(nc.dram_tensor("out_h", (b, t, c), _mybir.dt.float32, kind="ExternalOutput").ap())
    build(nc, *args)
    r = _run(nc, [arrays], core_ids=[0])
    return r.results[0]["out_h"]
```

```python
from contextlib import ExitStack

import concourse.bass as bass
from concourse import mybir

F32 = mybir.dt.float32
F32R = mybir.dt.float32r
I32 = mybir.dt.int32
U32 = mybir.dt.uint32
ALU = mybir.AluOpType
ACT = mybir.ActivationFunctionType
AX_X = mybir.AxisListType.X

P = 128
LN_EPS = 1e-5
NORM_EPS = 1e-12
DEN_EPS = 1e-6
MASKED = -1.0e30

P1_STEPS = ["ids_picked", "ln1_stats", "ln1_moments", "ln2_stats", "ln2_moments", "roots_eps", "roots",
            "x1_normed", "x1_turned", "x1_T", "qk_product", "v_product", "qk_negative", "qk_exp", "v_copied",
            "phi", "phi_q_turned", "kv_product", "phi_q_T", "kv_masked", "attn_sums", "attn_den", "attn_z",
            "attn", "h2", "x2_normed", "x2_energy", "x2_turned", "x2_T", "logits_product", "logits",
            "top_values", "top_indices", "is_two", "top_two", "gate_mask", "gate_negmax", "gate_exp",
            "gate_sum", "gate_rsum", "routing", "pair_weights", "rank_product", "ranks", "position",
            "position_index", "count"]
P2_STEPS = ["pair_turned", "pair_hi", "pair_lo", "pair_product", "pair_copied"]
DENSE_STEPS = ["dense_stats", "dense_moments", "dense_eps", "dense_root", "dense_x2", "dense_turned", "dense_hi",
               "dense_lo"]
P3_STEPS = ["pair_picked", "first_row", "qkv_sum", "heads_turned", "heads_T", "scores",
            "scores_negmax", "probs", "probs_rsum", "o_weights", "probs_turned", "probs_T", "ao_product",
            "aoT_hi", "aoT_lo", "v_sum", "out_sum"]


class Tile:

    def __init__(self, c, j=None, turns=None):
        self.c, self.j = c, j
        self.p, self.q = c % 2, c % 4
        self.t = c if j is None else j * 4 + c
        self.half = c // 2 if j is None else j * 2 + c // 2
        self.quarter = c // 4 if j is None else j + c // 4
        self.turns, self.eighth = turns, None
        if turns is not None or j is None:
            self.eighth = c // 8 if j is None else turns + c // 8

    def shift(self, k):
        return Tile(self.c + k, self.j, self.turns)

    @property
    def exists(self):
        return self.j is not None or self.c >= 0

    def inside(self, n):
        return self.j is not None or 0 <= self.c < n


def run(eng, step, first, last, low, high, turn=4):
    for c in range(first, low):
        step(Tile(c))
    with eng.Fori(0, (high + 1 - low) // turn) as j:
        for k in range(turn):
            step(Tile(low + k, j) if turn == 4 else Tile(low + k, j * 2, j))
    for c in range(high + 1, last + 1):
        step(Tile(c))


def build(nc, x, token_table, op_table, var_table, const_table, struct_table, special_table,
          W_qkv, b_qkv, W_proj, b_proj, sim_matrix, gates, q_proj, k_proj, v_proj, o_proj, out):
    B, T = x.shape
    HALF = token_table.shape[1]
    C = 2 * HALF
    CH = C // P
    E = gates.shape[0]
    HD = q_proj.shape[2]
    Y = 3 * HD
    D = 16
    HG = P // D
    G = C // P
    KVW = P + 2
    NUMW = P + HG
    N_SMALL = sum(t.shape[0] for t in (op_table, var_table, const_table, struct_table))
    N_SPECIAL = special_table.shape[0]
    HALF_SCALE = float(HD) ** -0.25
    REGION = (B + 1) * T
    PAIR_TILES = 2 * B + E
    COPIES, COPY_FROM = 10, -4
    WHOLE_FROM = 14
    BIAS_ROWS = 33
    OSLOT = E // 2
    POOL_SLOTS = (0, 3, 6)
    DVE_SLOTS = [s for s in range(OSLOT) if s not in POOL_SLOTS]
    assert T == P and HD == P and C == 2 * P and E == 16 and B == 4 * E and PAIR_TILES % 8 == 0

    category = nc.dram_tensor("category_table", [N_SMALL + N_SPECIAL, HALF], F32, kind="Internal").ap()
    sorted_x = nc.dram_tensor("sorted_x", [E * REGION + E * P, C], F32, kind="Internal").ap()
    sorted_y = nc.dram_tensor("sorted_y", [PAIR_TILES * P, Y], F32, kind="Internal").ap()
    h2_rows = nc.dram_tensor("h2_rows", [B, T, C], F32, kind="Internal").ap()

    with ExitStack() as ctx:
        def sb(name, shape, dt=F32):
            return ctx.enter_context(nc.sbuf_tensor(name, shape, dt))

        def sem(name):
            return ctx.enter_context(nc.semaphore(name))

        def sems(name, n):
            return [sem(f"{name}{i}") for i in range(n)]

        ident = sb("ident", [P, P])
        causal = sb("causal", [P, P])
        head_mask = sb("head_mask", [P, P])
        head_of_row = sb("head_of_row", [P, HG])
        earlier = sb("earlier", [P, P])
        ones = sb("ones", [P, P])
        ones_r = sb("ones_r", [P, P], F32R)
        earlier_r = sb("earlier_r", [P, P], F32R)
        ident_r = sb("ident_r", [P, P], F32R)
        causal_r = sb("causal_r", [P, P], F32R)
        zeros = sb("zeros", [P, C])
        minus_half = sb("minus_half", [P, E])
        eps = sb("eps", [P, 3])
        expert_no = sb("expert_no", [P, E])
        region_start = sb("region_start", [P, E])
        tile_no = sb("tile_no", [P, 2])
        tile_row = sb("tile_row", [P, 2])
        waiter = sb("waiter", [P, 8])
        bias = sb("bias", [BIAS_ROWS, 3 * C], F32R)
        gate_bias = sb("gate_bias", [P, E])
        gate_tmp = sb("gate_tmp", [P, E])
        ids_rows = sb("ids_rows", [B, T], I32)
        ids_rows_f = sb("ids_rows_f", [B, T])
        ids_f = sb("ids_f", [P, B])
        ids_low = sb("ids_low", [P, B])
        ids = sb("ids", [P, B, 2], U32)
        ids_now = [sb(f"ids_now{q}", [P, 2], U32) for q in range(4)]
        w_attn = sb("w_attn", [P, CH, 3 * C])
        raw = [sb(f"raw{p}", [P, C]) for p in range(2)]
        wq = [sb(f"wq_{n}", [P, E, CH, Y], F32R) for n in ("hi", "lo")]
        wo = [sb(f"wo_{n}", [P, E, C], F32R) for n in ("hi", "lo")]
        sim = sb("sim", [P, CH, E])
        sim_sq = sb("sim_sq", [P, CH, E])
        sim_norm = sb("sim_norm", [P, E])
        sim_inv = sb("sim_inv", [P, E])
        simn = sb("simn", [P, CH, E])
        h4 = sb("h4", [P, 4, C])
        h2 = [sb(f"h2_{p}", [P, C]) for p in range(2)]
        stats = sb("stats", [P, 4, 6])
        moments = [sb(f"moments{p}", [P, 3, 2]) for p in range(2)]
        roots_eps = [sb(f"roots_eps{p}", [P, 3]) for p in range(2)]
        roots = [sb(f"roots{p}", [P, 3]) for p in range(2)]
        x1 = sb("x1", [P, C])
        x1T = sb("x1T", [P, C])
        x2 = [sb(f"x2_{q}", [P, C]) for q in range(4)]
        x2T = sb("x2T", [P, C])
        qk_neg = sb("qk_neg", [P, 2 * C])
        qk_e = sb("qk_e", [P, 2 * C])
        phi = sb("phi", [P, 2 * C])
        vx = sb("vx", [P, G, KVW])
        pqT = sb("pqT", [P, G, P])
        kvm = sb("kvm", [P, G, NUMW])
        den = sb("den", [P, G, HG])
        zden = sb("zden", [P, G, HG])
        attn = sb("attn", [P, C])
        squares = sb("squares", [P, C])
        logits = sb("logits", [P, E])
        top = sb("top", [P, 8])
        top_at = sb("top_at", [P, 8], U32)
        is_one = sb("is_one", [P, E])
        is_two = sb("is_two", [P, E])
        top_two = sb("top_two", [P, E], F32R)
        idle = sb("idle", [P, 1])
        active = sb("active", [P, E])
        gated = sb("gated", [P, E])
        gmask = sb("gmask", [P, E])
        gneg = sb("gneg", [P, 1])
        gexp = sb("gexp", [P, E])
        gsel = sb("gsel", [P, E])
        gsum = sb("gsum", [P, 2])
        picked = sb("picked", [P, 4, E])
        ranks = sb("ranks", [P, E])
        next_row = sb("next_row", [P, E])
        third = sb("third", [P, 1])
        position = sb("position", [P, 2])
        position_u = [sb(f"position_u{q}", [P, 2], U32) for q in range(4)]
        routing = sb("routing", [P, B, E])
        bias_raw = routing[0:BIAS_ROWS, :, :].rearrange("p b e -> p (b e)")[:, 0:3 * C]
        pair_w = sb("pair_w", [P, B, 2])
        pair_in_x = sb("pair_in_x", [P, B, 2])
        pair_at = sb("pair_at", [P, B, 2], U32)
        tab = sb("tab", [P, 2, 2])
        tiles_i = sb("tiles_i", [P, E], I32)
        tiles_f = sb("tiles_f", [P, E])
        tiles_cum = sb("tiles_cum", [P, E])
        before = sb("before", [P, E])
        full = sb("full", [P, 2, 2, E])
        n_full = sb("n_full", [P, 2, 2])
        y_shift = sb("y_shift", [P, E])
        y_step = sb("y_step", [P, E])
        tab_tmp = sb("tab_tmp", [P, 4])
        tab_i = sb("tab_i", [1, 2, 2 * P], I32)
        fill_i = sb("fill_i", [1, E], I32)
        flag_f = sb("flag_f", [1, 1])
        flag_i = sb("flag_i", [1, 1], I32)
        row_x = sb("row_x", [P, 4, C])
        row_y = sb("row_y", [P, 4, Y])
        split = [[sb(f"split_{n}{q}", [P, CH, P], F32R) for n in ("hi", "lo")] for q in range(4)]
        h = [h4[:, q, :] for q in range(4)] + [row_x[:, q, :] for q in range(4)]
        x_buf = [row_x[:, q, :] for q in range(4)] + [b[:, c * C:(c + 1) * C] for b in (phi, qk_neg) for c in range(2)]
        y_buf = row_y, w_attn[:, :, :].rearrange("p c n -> p (c n)").rearrange("p (q y) -> p q y", y=Y)
        qkv = [w_attn[:, :, :].rearrange("p c n -> p (c n)")[:, q * Y:(q + 1) * Y] for q in range(4)]
        pair_now = [sb(f"pair_now{q}", [P, 2], U32) for q in range(4)]
        headsT = x1T[:, :].rearrange("p (a t) -> p a t", a=2)
        pr = attn[:, P:2 * P]
        prT = pqT[:, 0, :]
        acc_v = [[x1, squares], [qk_e[:, 0:C], qk_e[:, C:2 * C]]]
        acc_p = [x2T, qk_neg[:, 0:C]]
        sneg = sb("sneg", [P, 1])
        psumm = sb("psumm", [P, 2])
        rwo = [sb(f"rwo{p}", [P, E]) for p in range(2)]
        o_part = [h4[:, 0:2, :], h4[:, 2:4, :],
                  phi[:, :].rearrange("p (j c) -> p j c", j=2)]
        aoT = [[w[:, 0, :] for w in split[p]] for p in range(2)]

        banks = [ctx.enter_context(nc.psum_tensor(f"bank{b}", [P, 512], F32)) for b in range(8)]
        ps_x1, ps_qk, ps_v, ps_pq, ps_kvb, ps_sumb, ps_x2, ps_gate = banks
        ps_kv = ps_kvb[:, 0:G * KVW].rearrange("p (g n) -> p g n", g=G)
        ps_sums = ps_sumb[:, 0:G * NUMW].rearrange("p (g n) -> p g n", g=G)
        ps_rank = ps_gate[:, E:3 * E]
        ps_turn, ps_y = banks[0:2], banks[2:6]
        ps_o = banks[0:4]
        ps_heads, ps_score, ps_prob, ps_ao = banks[4:8]

        done = {s: sem(s) for s in P1_STEPS + P2_STEPS + DENSE_STEPS + P3_STEPS}
        rows_gathered = sems("rows_gathered", 4)
        special_gathered = sems("special_gathered", 4)
        scattered = sems("scattered", 4)
        h2_stored = sems("h2_stored", 2)
        raw_loaded = sems("raw_loaded", 2)
        weights_hi = sem("weights_hi")
        weights_lo = sem("weights_lo")
        small_loaded = sem("small_loaded")
        special_copied = sem("special_copied")
        bias_cleared = sem("bias_cleared")
        ids_loaded = sem("ids_loaded")
        inputs_loaded = sem("inputs_loaded")
        attn_loaded = sem("attn_loaded")
        dummies_zeroed = sem("dummies_zeroed")
        ident_ready = sem("ident_ready")
        consts_base = sem("consts_base")
        consts_ready = sem("consts_ready")
        setup_v = sem("setup_v")
        setup_own = sem("setup_own")
        setup_p = sem("setup_p")
        setup_a = sem("setup_a")
        setup_t = sem("setup_t")
        table_v = sem("table_v")
        table_t = sem("table_t")
        tables_ready = sem("tables_ready")
        fill_ready = sem("fill_ready")
        regions_filled = sem("regions_filled")
        pair_loaded = sems("pair_loaded", 8)
        y_stored = sems("y_stored", 4)
        y_ready = sem("y_ready")
        dense_loaded = sem("dense_loaded")
        dense_product = sem("dense_product")
        dense_added = sem("dense_added")
        dense_stored = sem("dense_stored")
        pairs_placed = sem("pairs_placed")
        y_filled = sem("y_filled")
        pairs_gathered = sems("pairs_gathered", 2)
        h2_loaded = sems("h2_loaded", 2)
        stored = sems("stored", 2)
        o_product = sem("o_product")
        o_scaled = sem("o_scaled")
        o_pooled = sem("o_pooled")
        o_added = sem("o_added")
        N_CONSTS = 17

        def after(eng, step, tile):
            if tile.exists:
                eng.wait_ge(done[step] if isinstance(step, str) else step, tile.t + 1)

        def landed_half(eng, by_parity, tile, dmas=1):
            if tile.exists:
                eng.wait_ge(by_parity[tile.p], tile.half * (16 * dmas) + 16 * dmas)

        def landed_quarter(eng, by_four, tile, dmas=1):
            if tile.exists:
                eng.wait_ge(by_four[tile.q], tile.quarter * (16 * dmas) + 16 * dmas)

        def product_done(eng, tile, s):
            if tile.exists:
                eng.wait_ge(o_product, tile.t * OSLOT + s + 1)

        def scaled_done(eng, tile, s):
            if tile.exists:
                eng.wait_ge(o_scaled, tile.t * len(POOL_SLOTS) + POOL_SLOTS.index(s) + 1)

        def pooled_done(eng, tile, s):
            if tile.exists:
                eng.wait_ge(o_pooled, tile.t * (2 * len(POOL_SLOTS) - 1) + 2 * POOL_SLOTS.index(s) + 1)

        def added_done(eng, tile, s, n=1):
            if tile.exists:
                eng.wait_ge(o_added, tile.t * (2 * len(DVE_SLOTS)) + 2 * DVE_SLOTS.index(s) + 1 + n)

        def y_landed(eng, tile):
            if tile.exists:
                eng.wait_ge(y_stored[tile.c % 8 // 2], tile.eighth * 16 + 16)

        def run1(eng, step):
            run(eng, step, -7, B, 8, B - 9, turn=8)

        def run2(eng, step):
            run(eng, step, -8, PAIR_TILES, 8, PAIR_TILES - 9, turn=8)

        def run3(eng, step):
            run(eng, step, -4, B, 4, B - 5)

        def fill_regions(eng, half):
            eng.wait_ge(fill_ready, 1)
            n = E // 2
            at = nc.values_load_multi_w_load_instructions(
                fill_i[0:1, half * n:(half + 1) * n], engines=(eng.engine,), min_val=0, max_val=E * REGION - P)[1]
            for row in at:
                eng.dma_start(sorted_x[bass.ds(row, P), :], zeros[:, :]).then_inc(regions_filled, 16)

        def every_tile(eng, step):
            step(0, True)
            with eng.Fori(1, B) as t:
                step(t, False)

        def branch(eng, sorted_way, dense_way):
            eng.wait_ge(tables_ready, 1)
            flag = eng.value_load(flag_i[0:1, 0:1], min_val=0, max_val=1)
            with eng.If(flag < 1):
                sorted_way()
            with eng.Else():
                dense_way()

        def quarter_of(split_weights, tile):
            one = bass.ds(tile.quarter, 1)
            if tile.q == 3:
                return split_weights[1][:, one, :].rearrange("p e n -> p (e n)")
            return split_weights[0][:, one, :, tile.q * HD:(tile.q + 1) * HD].rearrange("p e c n -> p (e c) n")

        def split_by_vector(tile):
            return tile.j is None and 0 <= tile.c < 7

        def like(tile, raw_buf):
            return raw_buf[:, :] if tile.q == 3 else raw_buf[:, :].rearrange("p (c n) -> p c n", c=CH)

        block = ctx.enter_context(nc.Block())

        @block.sync
        def _(sp):
            row = 0
            sp.dma_start(ids_rows[:, :], x).then_inc(ids_loaded, 16)
            sp.dma_start(sim[:, :, :], sim_matrix.rearrange("(c p) e -> p c e", p=P)).then_inc(inputs_loaded, 16)
            for tab_in in (op_table, var_table, const_table, struct_table):
                sp.dma_start(category[row:row + tab_in.shape[0], :], tab_in).then_inc(small_loaded, 16)
                row += tab_in.shape[0]
            sp.wait_ge(bias_cleared, 1)
            for n in (0, BIAS_ROWS - 1):
                sp.dma_start(bias_raw[n:n + 1, :], b_qkv.unsqueeze(0)).then_inc(inputs_loaded, 16)
            sp.dma_start(gate_tmp[:, :], gates.partition_broadcast(P)).then_inc(inputs_loaded, 16)
            sp.dma_start(w_attn[:, :, :], W_qkv.rearrange("(c p) n -> p c n", p=P)).then_inc(attn_loaded, 16)
            sp.wait_ge(consts_ready, N_CONSTS)
            for n in range(E):
                sp.dma_start(sorted_x[E * REGION + n * P:E * REGION + (n + 1) * P, :], zeros[:, :]
                             ).then_inc(dummies_zeroed, 16)

            def step1(i):
                if i.j is None and 0 <= i.c - COPY_FROM < COPIES:
                    n = -(-N_SPECIAL // COPIES)
                    lo, hi = n * (i.c - COPY_FROM), min(n * (i.c - COPY_FROM + 1), N_SPECIAL)
                    sp.dma_start(category[N_SMALL + lo:N_SMALL + hi, :], special_table[lo:hi, :]
                                 ).then_inc(special_copied, 16)
                tile = i.shift(1)
                if tile.inside(B):
                    after(sp, weights_lo, tile.shift(-2))
                    one = bass.ds(tile.quarter, 1)
                    if tile.q == 3:
                        src = o_proj[one].rearrange("e h c -> h (e c)")
                    else:
                        src = (q_proj, k_proj, v_proj)[tile.q][one].rearrange("e (c p) h -> p (e c) h", p=P)
                    sp.dma_start(like(tile, raw[tile.p]), src).then_inc(raw_loaded[tile.p], 16)
                tile = i.shift(2)
                if tile.inside(B):
                    after(sp, "h2", tile)
                    sp.dma_start(h2_rows[tile.t], h2[tile.p][:, :]).then_inc(h2_stored[tile.p], 16)

            run1(sp, step1)
            for p in range(2):
                sp.wait_ge(h2_stored[p], 16 * (B // 2))
            fill_regions(sp, 0)
            sp.wait_ge(regions_filled, 16 * E)
            sp.wait_ge(dummies_zeroed, 16 * E)
            for q in range(4):
                sp.wait_ge(scattered[q], 32 * (B // 4))

            def sorted_way():
                rows = {}

                def step2(i):
                    tile = i.shift(8)
                    if tile.inside(PAIR_TILES):
                        if tile.q == 0:
                            loaded = nc.values_load_multi_w_load_instructions(
                                tab_i[0:1, 1, bass.ds(tile.t, 4)], engines=(sp.engine,), min_val=0,
                                max_val=(E * REGION + E * P) - P)[1]
                            rows.update(enumerate(loaded))
                        after(sp, "pair_turned", tile.shift(-8))
                        sp.dma_start(x_buf[tile.c % 8], sorted_x[bass.ds(rows[tile.q], P), :]
                                     ).then_inc(pair_loaded[tile.c % 8], 16)
                    tile = i.shift(-1)
                    if tile.inside(PAIR_TILES) and tile.p:
                        after(sp, "pair_copied", tile)
                        first, buf = tile.shift(-1), y_buf[tile.c % 8 // 4]
                        sp.dma_start(sorted_y[bass.ds(first.t * P, 2 * P), :].rearrange("(n p) y -> p n y", p=P),
                                     buf[:, first.q:first.q + 2, :]).then_inc(y_stored[tile.c % 8 // 2], 16)

                run2(sp, step2)
                for q in range(4):
                    sp.wait_ge(y_stored[q], 16 * (PAIR_TILES // 8))
                sp.sem_inc(y_ready, 1)

            def dense_way():
                rest = sorted_y[B * P:PAIR_TILES * P, :].rearrange("r y -> (r y)").rearrange(
                    "(n p c) -> n p c", p=P, c=C)
                for n in range(rest.shape[0]):
                    sp.dma_start(rest[n], zeros[:, :]).then_inc(y_filled, 16)
                sp.wait_ge(y_filled, 16 * rest.shape[0])

                def token_tile(t, first):
                    if not first:
                        sp.wait_ge(done["dense_x2"], t)
                    sp.dma_start(row_x[:, 1, :], h2_rows[t]).then_inc(dense_loaded, 16)
                    sp.wait_ge(dense_added, t * E + E)
                    sp.dma_start(sorted_y[bass.ds(t * T, T), :], row_y[:, 0, :]).then_inc(dense_stored, 16)

                every_tile(sp, token_tile)
                sp.wait_ge(dense_stored, 16 * B)
                sp.sem_inc(y_ready, 1)

            branch(sp, sorted_way, dense_way)

            def step3(i):
                tile = i.shift(1)
                if tile.inside(B):
                    added_done(sp, tile.shift(-2), DVE_SLOTS[0], 0)
                    sp.dma_start(row_x[:, tile.p, :], h2_rows[tile.t]).then_inc(h2_loaded[tile.p], 16)
                tile = i.shift(-1)
                if tile.inside(B):
                    after(sp, "out_sum", tile)
                    sp.dma_start(out[tile.t], row_x[:, 2 + tile.p, :]).then_inc(stored[tile.p], 16)

            run3(sp, step3)
            for p in range(2):
                sp.wait_ge(stored[p], 16 * (B // 2))

        @block.gpsimd
        def _(pool):
            pool.memset(ident[:, :], 0.0).then_inc(ident_ready, 1)
            pool.memset(bias_raw, 0.0).then_inc(bias_cleared, 1)
            pool.wait_ge(ident_ready, 1)
            pool.affine_select(out=ident[:, :], in_=ident[:, :], compare_op=ALU.not_equal, fill=1.0, base=0,
                               pattern=[[-1, P]], channel_multiplier=1).then_inc(ident_ready, 1)
            pool.memset(causal[:, :], 0.0).then_inc(consts_base, 1)
            pool.memset(head_mask[:, :], 1.0).then_inc(consts_base, 1)
            pool.memset(head_of_row[:, :], 1.0).then_inc(consts_base, 1)
            pool.memset(earlier[:, :], 1.0).then_inc(consts_base, 1)
            pool.memset(ones[:, :], 1.0).then_inc(consts_ready, 1)
            pool.memset(zeros[:, :], 0.0).then_inc(consts_ready, 1)
            pool.memset(minus_half[:, :], -0.5).then_inc(consts_ready, 1)
            pool.memset(vx[:, :, :], 1.0).then_inc(consts_ready, 1)
            pool.memset(eps[:, 0:2], LN_EPS).then_inc(consts_ready, 1)
            pool.memset(eps[:, 2:3], NORM_EPS).then_inc(consts_ready, 1)
            pool.memset(third[:, :], -4.0).then_inc(consts_ready, 1)
            for p in range(2):
                pool.memset(moments[p][:, :, :], 1.0).then_inc(consts_ready, 1)
            pool.iota(expert_no[:, :], pattern=[[1, E]], base=0, channel_multiplier=0,
                      allow_small_or_imprecise_dtypes=True).then_inc(consts_ready, 1)
            pool.iota(tile_no[:, :], pattern=[[P, 2]], base=0, channel_multiplier=1,
                      allow_small_or_imprecise_dtypes=True).then_inc(consts_ready, 1)
            pool.iota(tile_row[:, :], pattern=[[P * P, 2]], base=0, channel_multiplier=P,
                      allow_small_or_imprecise_dtypes=True).then_inc(consts_ready, 1)
            pool.iota(region_start[:, :], pattern=[[REGION, E]], base=0, channel_multiplier=0,
                      allow_small_or_imprecise_dtypes=True).then_inc(consts_ready, 1)
            pool.wait_ge(consts_base, 4)
            pool.affine_select(out=causal[:, :], in_=causal[:, :], compare_op=ALU.is_ge, fill=MASKED, base=0,
                               pattern=[[-1, P]], channel_multiplier=1).then_inc(consts_ready, 1)
            pool.affine_select(out=earlier[:, :], in_=earlier[:, :], compare_op=ALU.is_ge, fill=0.0, base=-1,
                               pattern=[[1, P]], channel_multiplier=-1).then_inc(consts_ready, 1)
            hm = head_mask[:, :].rearrange("p (h d) -> p h d", d=D)
            pool.affine_select(out=hm, in_=hm, compare_op=ALU.is_ge, fill=0.0, base=0,
                               pattern=[[-D, HG], [0, D]], channel_multiplier=1).then_inc(consts_base, 1)
            pool.affine_select(out=head_of_row[:, :], in_=head_of_row[:, :], compare_op=ALU.is_ge, fill=0.0,
                               base=0, pattern=[[-D, HG]], channel_multiplier=1).then_inc(consts_base, 1)
            pool.wait_ge(consts_base, 6)
            pool.affine_select(out=hm, in_=hm, compare_op=ALU.is_ge, fill=0.0, base=D - 1,
                               pattern=[[D, HG], [0, D]], channel_multiplier=-1).then_inc(consts_ready, 1)
            pool.affine_select(out=head_of_row[:, :], in_=head_of_row[:, :], compare_op=ALU.is_ge, fill=0.0,
                               base=D - 1, pattern=[[D, HG]], channel_multiplier=-1).then_inc(consts_ready, 1)

            pool.wait_ge(consts_ready, N_CONSTS)
            pool.wait_ge(setup_v, 2)
            pool.wait_ge(small_loaded, 64)

            waits_taken = [0]

            def take_wait():
                n = waits_taken[0] % 8
                waits_taken[0] += 1
                pool.tensor_tensor(waiter[:, n:n + 1], ones[:, 0:1], ones[:, 0:1], ALU.add)

            def in_parts(tile):
                return tile.j is None and 0 <= tile.c < WHOLE_FROM

            def offsets(index):
                return bass.IndirectOffsetOnAxis(ap=index, axis=0)

            def step1(i):
                if i.j is None and i.c == -5:
                    pool.wait_ge(setup_v, 4)
                    pool.tensor_tensor(sim_inv[:, :], sim_norm[:, :], minus_half[:, :], ALU.pow
                                       ).then_inc(setup_p, 1)
                gather, small_rows, scatter = i.shift(7), i.shift(6), i.shift(-1)
                ln1, ln2, norm = i.shift(4), i.shift(1), i
                rooted = ln1.inside(B) or ln2.inside(B) or norm.inside(B)
                if rooted:
                    if in_parts(small_rows):
                        landed_quarter(pool, special_gathered, small_rows)
                    for t, step in ((ln1, "ln1_moments"), (ln2, "ln2_moments"), (norm, "x2_energy")):
                        if t.inside(B):
                            after(pool, step, t)
                    pool.tensor_tensor(roots_eps[i.p][:, :], moments[i.p][:, :, 1], eps[:, :], ALU.add
                                       ).then_inc(done["roots_eps"], 1)
                if gather.inside(B):
                    pool.tensor_copy(ids_now[gather.q][:, :],
                                     ids[:, bass.ds(gather.t, 1), :].rearrange("p o n -> p (o n)")
                                     ).then_inc(done["ids_picked"], 1)
                    after(pool, "ids_picked", gather)
                if rooted:
                    after(pool, "roots_eps", i.shift(4))
                    pool.tensor_tensor(roots[i.p][:, :], roots_eps[i.p][:, :], minus_half[:, 0:3], ALU.pow
                                       ).then_inc(done["roots"], 1)
                elif in_parts(small_rows):
                    landed_quarter(pool, special_gathered, small_rows)
                if in_parts(small_rows):
                    pool.indirect_dma_start(out=h[small_rows.c % 8][:, HALF:C], out_offset=None,
                                            in_=category[0:N_SMALL, :],
                                            in_offset=offsets(ids_now[small_rows.q][:, 0:1]),
                                            bounds_check=N_SMALL - 1, oob_is_err=False
                                            ).then_inc(rows_gathered[small_rows.q], 16)
                if gather.inside(B) and not in_parts(gather):
                    if i.j is None and gather.c == WHOLE_FROM:
                        pool.wait_ge(special_copied, 16 * COPIES)
                        take_wait()
                    pool.indirect_dma_start(out=h[gather.c % 8][:, HALF:C], out_offset=None, in_=category,
                                            in_offset=offsets(ids_now[gather.q][:, 0:1])
                                            ).then_inc(rows_gathered[gather.q], 16)
                if in_parts(gather):
                    pool.indirect_dma_start(out=h[gather.c % 8][:, HALF:C], out_offset=None, in_=special_table,
                                            in_offset=offsets(ids_now[gather.q][:, 1:2]),
                                            bounds_check=N_SPECIAL - 1, oob_is_err=False
                                            ).then_inc(special_gathered[gather.q], 16)
                if gather.inside(B):
                    pool.indirect_dma_start(out=h[gather.c % 8][:, 0:HALF], out_offset=None, in_=token_table,
                                            in_offset=offsets(ids_now[gather.q][:, 0:1])
                                            ).then_inc(rows_gathered[gather.q], 16)
                if scatter.inside(B):
                    after(pool, "position_index", scatter)
                    take_wait()
                    for n in range(2):
                        pool.indirect_dma_start(out=sorted_x, out_offset=offsets(position_u[scatter.q][:, n:n + 1]),
                                                in_=x2[scatter.q][:, :], in_offset=None
                                                ).then_inc(scattered[scatter.q], 16)
                if scatter.inside(B) and not split_by_vector(scatter):
                    after(pool, weights_hi, scatter)
                    after(pool, weights_lo, scatter.shift(-1))
                    pool.tensor_tensor(quarter_of((wq[1], wo[1]), scatter), like(scatter, raw[scatter.p]),
                                       quarter_of((wq[0], wo[0]), scatter).bitcast(F32), ALU.subtract
                                       ).then_inc(weights_lo, 1)

            run1(pool, step1)

            def sorted_way():
                rows = pair_in_x[:, :, :].rearrange("p b n -> p (b n)")
                term, total = [pqT[:, g, :] for g in range(2)], kvm[:, 0, 0:2 * B]
                count = 0
                for e in range(1, E):
                    if e > 2:
                        pool.wait_ge(pairs_placed, count - 1)
                    pool.tensor_scalar(term[e % 2], rows, float(e * REGION), y_step[:, e:e + 1],
                                       ALU.is_ge, ALU.mult).then_inc(pairs_placed, 1)
                    pool.wait_ge(pairs_placed, count + 1)
                    pool.tensor_tensor(total, rows if e == 1 else total, term[e % 2], ALU.add
                                       ).then_inc(pairs_placed, 1)
                    count += 2
                pool.wait_ge(pairs_placed, count)
                pool.tensor_copy(pair_at[:, :, :].rearrange("p b n -> p (b n)"), total).then_inc(pairs_placed, 1)
                pool.wait_ge(pairs_placed, count + 1)

            def dense_way():
                def token_tile(t, first):
                    pool.wait_ge(done["dense_moments"], t + 1)
                    pool.tensor_tensor(roots_eps[0][:, 0:1], moments[0][:, 0, 1:2], eps[:, 0:1], ALU.add
                                       ).then_inc(done["dense_eps"], 1)
                    pool.wait_ge(done["dense_eps"], t + 1)
                    pool.tensor_tensor(roots[0][:, 0:1], roots_eps[0][:, 0:1], minus_half[:, 0:1], ALU.pow
                                       ).then_inc(done["dense_root"], 1)

                every_tile(pool, token_tile)
                pool.memset(pair_w[:, :, 0], 1.0).then_inc(pairs_placed, 1)
                pool.memset(pair_w[:, :, 1], 0.0).then_inc(pairs_placed, 1)
                for n in range(2):
                    pool.iota(pair_at[:, :, n], pattern=[[T, B]], base=0, channel_multiplier=1,
                              allow_small_or_imprecise_dtypes=True).then_inc(pairs_placed, 1)
                pool.wait_ge(pairs_placed, 4)

            branch(pool, sorted_way, dense_way)
            pool.wait_ge(y_ready, 1)

            def add_part(tile, s):
                k = POOL_SLOTS.index(s)
                part, acc = o_part[k], acc_p[tile.p]
                if k == 0:
                    after(pool, "out_sum", tile.shift(-2))
                    scaled_done(pool, tile, s)
                    pool.tensor_tensor(acc[:, :], part[:, 0, :], part[:, 1, :], ALU.add).then_inc(o_pooled, 1)
                    return
                pooled_done(pool, tile, POOL_SLOTS[k - 1])
                scaled_done(pool, tile, s)
                pool.tensor_tensor(acc[:, :], part[:, 0, :], acc[:, :], ALU.add).then_inc(o_pooled, 1)
                pool.wait_ge(o_pooled, tile.t * (2 * len(POOL_SLOTS) - 1) + 2 * k)
                pool.tensor_tensor(acc[:, :], part[:, 1, :], acc[:, :], ALU.add).then_inc(o_pooled, 1)

            def step3(i):
                tile = i.shift(4)
                if tile.inside(B):
                    pool.tensor_copy(pair_now[tile.q][:, :],
                                     pair_at[:, bass.ds(tile.t, 1), :].rearrange("p o n -> p (o n)")
                                     ).then_inc(done["pair_picked"], 1)
                    after(pool, "pair_picked", tile)
                    after(pool, "qkv_sum", tile.shift(-2))
                    take_wait()
                    for n in range(2):
                        pool.indirect_dma_start(out=row_y[:, 2 * tile.p + n, :], out_offset=None, in_=sorted_y,
                                                in_offset=offsets(pair_now[tile.q][:, n:n + 1])
                                                ).then_inc(pairs_gathered[tile.p], 16)
                if i.inside(B):
                    for s in POOL_SLOTS:
                        add_part(i, s)

            run3(pool, step3)

        @block.scalar
        def _(act):
            act.wait_ge(inputs_loaded, 64)
            act.activation(gate_bias[:, :], gate_tmp[:, :], ACT.Exp, scale=-1.0).then_inc(setup_a, 1)
            act.copy(bias[:, :], bias_raw).then_inc(setup_a, 1)
            act.wait_ge(consts_ready, N_CONSTS)
            act.copy(earlier_r[:, :], earlier[:, :])
            act.copy(ident_r[:, :], ident[:, :])
            act.copy(causal_r[:, :], causal[:, :])
            act.copy(ones_r[:, :], ones[:, :]).then_inc(setup_a, 1)

            def step1(i):
                tile = i.shift(3)
                if tile.inside(B):
                    after(act, "qk_product", tile)
                    act.activation(qk_neg[:, :], ps_qk[:, :], ACT.Relu, scale=-1.0
                                   ).then_inc(done["qk_negative"], 1)
                    after(act, "qk_negative", tile)
                    act.activation(qk_e[:, :], qk_neg[:, :], ACT.Exp, scale=-1.0).then_inc(done["qk_exp"], 1)
                tile = i.shift(4)
                if tile.inside(B):
                    after(act, "x1_turned", tile)
                    act.copy(x1T[:, :], ps_x1[:, 0:C]).then_inc(done["x1_T"], 1)
                tile = i.shift(1)
                if tile.inside(B):
                    after(act, "x2_normed", tile)
                    act.activation(squares[:, :], x2[tile.q][:, :], ACT.Square,
                                   accum_out=moments[i.shift(1).p][:, 2, 1:2]).then_inc(done["x2_energy"], 1)
                tile = i.shift(3)
                if tile.inside(B):
                    after(act, "v_product", tile)
                    act.copy(vx[:, :, 0:P], ps_v[:, 0:C].rearrange("p (g n) -> p g n", g=G)
                             ).then_inc(done["v_copied"], 1)
                tile = i.shift(1)
                if tile.inside(B):
                    after(act, "x2_turned", tile)
                    act.copy(x2T[:, :], ps_x2[:, 0:C]).then_inc(done["x2_T"], 1)
                tile = i.shift(3)
                if tile.inside(B):
                    after(act, "phi_q_turned", tile)
                    act.copy(pqT[:, :, :].rearrange("p g t -> p (g t)"), ps_pq[:, 0:C]
                             ).then_inc(done["phi_q_T"], 1)
                tile = i
                if tile.inside(B):
                    after(act, "gate_negmax", tile)
                    act.activation(gexp[:, :], gated[:, :], ACT.Exp, bias=gneg[:, 0:1]
                                   ).then_inc(done["gate_exp"], 1)
                if i.inside(B):
                    landed_half(act, raw_loaded, i)
                    act.copy(quarter_of((wq[0], wo[0]), i), like(i, raw[i.p])).then_inc(weights_hi, 1)

            run1(act, step1)
            fill_regions(act, 1)

            def sorted_way():
                def step2(i):
                    tile = i.shift(2)
                    if tile.inside(PAIR_TILES):
                        after(act, "pair_product", tile.shift(-4))
                        after(act, "pair_turned", tile)
                        act.copy(split[tile.q][0][:, :, :].rearrange("p c t -> p (c t)"),
                                 ps_turn[tile.p][:, 0:C]).then_inc(done["pair_hi"], 1)
                    if i.inside(PAIR_TILES) and i.p:
                        y_landed(act, i.shift(-8))
                        after(act, "pair_copied", i.shift(-1))
                        after(act, "pair_product", i)
                        act.copy(y_buf[i.c % 8 // 4][:, i.q, :], ps_y[i.q][:, 0:Y]
                                 ).then_inc(done["pair_copied"], 1)

                run2(act, step2)

            def dense_way():
                def token_tile(t, first):
                    act.wait_ge(done["dense_turned"], t + 1)
                    act.copy(split[0][0][:, :, :].rearrange("p c t -> p (c t)"), ps_turn[0][:, 0:C]
                             ).then_inc(done["dense_hi"], 1)

                every_tile(act, token_tile)

            branch(act, sorted_way, dense_way)

            def scale_slot(tile, s):
                k = POOL_SLOTS.index(s)
                if k == 0:
                    after(act, "o_weights", tile)
                pooled_done(act, tile.shift(-1), s)
                product_done(act, tile, s)
                part, ps = o_part[k], ps_o[s % len(ps_o)]
                for j in range(2):
                    e = 2 * s + j
                    last = act.mul(part[:, j, :], ps[:, j * C:(j + 1) * C], rwo[tile.p][:, e:e + 1])
                last.then_inc(o_scaled, 1)

            def step3(i):
                tile = i.shift(1)
                if tile.inside(B):
                    after(act, "scores_negmax", tile)
                    act.activation(pr[:, :], ps_score[:, 0:P], ACT.Exp, bias=sneg[:, 0:1], accum_out=psumm[:, 0:1]
                                   ).then_inc(done["probs"], 1)
                if i.inside(B):
                    scale_slot(i, POOL_SLOTS[0])
                tile = i.shift(1)
                if tile.inside(B):
                    after(act, "probs_turned", tile)
                    act.copy(prT[:, :], ps_prob[:, 0:P]).then_inc(done["probs_T"], 1)
                if tile.shift(1).inside(B):
                    after(act, "heads_turned", tile.shift(1))
                    act.mul(headsT[:, :, :].rearrange("p a t -> p (a t)"), ps_heads[:, 0:2 * P], HALF_SCALE
                            ).then_inc(done["heads_T"], 1)
                if tile.inside(B):
                    product_done(act, tile.shift(-2), OSLOT - 1)
                    after(act, "ao_product", tile)
                    act.copy(aoT[tile.p][0], ps_ao[:, 0:P]).then_inc(done["aoT_hi"], 1)
                if i.inside(B):
                    scale_slot(i, POOL_SLOTS[1])
                tile = i.shift(3)
                if tile.inside(B):
                    landed_half(act, pairs_gathered, tile, dmas=2)
                    act.mul(qkv[tile.q][:, :], row_y[:, 2 * tile.p, :],
                            pair_w[:, bass.ds(tile.t, 1), 0:1].rearrange("p o n -> p (o n)")
                            ).then_inc(done["first_row"], 1)
                if i.inside(B):
                    scale_slot(i, POOL_SLOTS[2])

            run3(act, step3)

        @block.vector
        def _(dve):
            def ln_moments(tile, n, src, mv):
                dve.bn_stats(stats[:, n - 1, :], src).then_inc(done[f"ln{n}_stats"], 1)
                after(dve, f"ln{n}_stats", tile)

            dve.wait_ge(ids_loaded, 16)
            dve.tensor_copy(ids_rows_f[:, :], ids_rows[:, :]).then_inc(setup_v, 1)
            dve.wait_ge(setup_t, 1)
            dve.tensor_copy(ids_f[:, :], ps_x1[:, 0:B]).then_inc(setup_own, 1)
            dve.wait_ge(setup_own, 1)
            dve.tensor_scalar(ids_low[:, :], ids_f[:, :], float(N_SMALL), float(2 ** 22), ALU.is_lt, ALU.mult
                              ).then_inc(setup_own, 1)
            dve.wait_ge(setup_own, 2)
            dve.tensor_copy(ids[:, :, 0], ids_f[:, :])
            dve.scalar_tensor_tensor(ids[:, :, 1], ids_f[:, :], float(N_SMALL), ids_low[:, :],
                                     ALU.subtract, ALU.add).then_inc(setup_v, 1)
            dve.wait_ge(inputs_loaded, 64)
            dve.tensor_tensor(sim_sq[:, :, :], sim[:, :, :], sim[:, :, :], ALU.mult).then_inc(setup_v, 1)
            dve.wait_ge(setup_t, 2)
            dve.tensor_scalar(sim_norm[:, :], ps_qk[:, 0:E], NORM_EPS, None, ALU.add).then_inc(setup_v, 1)
            dve.wait_ge(setup_a, 2)
            last_row = slice(BIAS_ROWS - 1, BIAS_ROWS)
            dve.tensor_tensor(bias[last_row, :], bias_raw[last_row, :], bias[last_row, :].bitcast(F32),
                              ALU.subtract).then_inc(setup_v, 1)
            dve.tensor_scalar(gate_tmp[:, :], gate_bias[:, :], 1.0, None, ALU.add).then_inc(setup_own, 1)
            dve.wait_ge(setup_own, 3)
            dve.reciprocal(gate_bias[:, :], gate_tmp[:, :]).then_inc(setup_own, 1)
            dve.wait_ge(consts_ready, N_CONSTS)
            dve.tensor_copy(next_row[:, :], region_start[:, :]).then_inc(setup_own, 1)
            dve.wait_ge(setup_own, 5)

            def carry():
                dve.tensor_copy(tab_tmp[:, 0:1], ones[:, 0:1])

            def step1(i):
                if i.j is None and i.c == -4:
                    dve.wait_ge(setup_p, 1)
                    dve.tensor_tensor(simn[:, :, :], sim[:, :, :],
                                      sim_inv[:, :].unsqueeze(1).broadcast_to([P, CH, E]), ALU.mult
                                      ).then_inc(setup_v, 1)
                x1_tile, x2_tile, attn_tile, phi_tile, ln1_tile = [i.shift(k) for k in (4, 1, 2, 3, 5)]
                last_tile = i.shift(-1)
                if x1_tile.inside(B):
                    after(dve, "x1_turned", x1_tile.shift(-1))
                if x1_tile.inside(B) or x2_tile.inside(B) or i.inside(B):
                    after(dve, "roots", i.shift(4))
                if x1_tile.inside(B):
                    dve.tensor_scalar(x1[:, :], h[x1_tile.c % 8], moments[i.p][:, 0, 0:1], roots[i.p][:, 0:1],
                                      ALU.subtract, ALU.mult).then_inc(done["x1_normed"], 1)
                if last_tile.inside(B):
                    after(dve, "rank_product", last_tile)
                    dve.tensor_tensor(ranks[:, :], ps_rank[:, 0:E], next_row[:, :], ALU.add
                                      ).then_inc(done["ranks"], 1)
                    after(dve, "routing", last_tile)
                    now = routing[:, bass.ds(last_tile.t, 1), :].rearrange("p o e -> p (o e)")
                    for n, mine in enumerate((is_one, is_two)):
                        last = dve.scalar_tensor_tensor(
                            picked[:, 2 + n, :], now, 1.0, mine[:, :], ALU.mult, ALU.mult,
                            accum_out=pair_w[:, bass.ds(last_tile.t, 1), n:n + 1].rearrange("p o n -> p (o n)"))
                    last.then_inc(done["pair_weights"], 1)
                    after(dve, "ranks", last_tile)
                    dve.tensor_tensor(next_row[:, :], ps_rank[:, E:2 * E], next_row[:, :], ALU.add
                                      ).then_inc(done["count"], 1)
                    for n, mine in enumerate((is_one, is_two)):
                        last = dve.scalar_tensor_tensor(picked[:, n, :], ranks[:, :], 1.0, mine[:, :], ALU.mult,
                                                        ALU.mult, accum_out=position[:, n:n + 1])
                    last.then_inc(done["position"], 1)
                if x2_tile.inside(B):
                    landed_quarter(dve, scattered, x2_tile.shift(-4), dmas=2)
                    dve.tensor_scalar(x2[x2_tile.q][:, :], h2[x2_tile.p][:, :], moments[i.p][:, 1, 0:1],
                                      roots[i.p][:, 1:2], ALU.subtract, ALU.mult
                                      ).then_inc(done["x2_normed"], 1)
                if last_tile.inside(B):
                    after(dve, "position", last_tile)
                    dve.tensor_copy(position_u[last_tile.q][:, :], position[:, :]
                                    ).then_inc(done["position_index"], 1)
                if ln1_tile.inside(B):
                    after(dve, "ln1_stats", ln1_tile)
                if i.inside(B):
                    after(dve, "logits_product", i)
                    dve.scalar_tensor_tensor(logits[:, :], ps_gate[:, 0:E], roots[i.p][:, 2:3], gate_bias[:, :],
                                             ALU.mult, ALU.subtract).then_inc(done["logits"], 1)
                elif ln1_tile.inside(B):
                    carry()
                if ln1_tile.inside(B):
                    dve.bn_aggr(moments[i.shift(1).p][:, 0, :], stats[:, 2 * i.p, :]).then_inc(done["ln1_moments"], 1)
                if phi_tile.inside(B):
                    after(dve, "qk_exp", phi_tile)
                    dve.scalar_tensor_tensor(phi[:, :], ps_qk[:, :], 0.0, qk_e[:, :], ALU.max, ALU.add
                                             ).then_inc(done["phi"], 1)
                if attn_tile.inside(B):
                    after(dve, "attn_sums", attn_tile)
                    dve.tensor_scalar(den[:, :, :], ps_sums[:, :, P:NUMW], DEN_EPS, None, ALU.add
                                      ).then_inc(done["attn_den"], 1)
                if i.inside(B):
                    after(dve, "logits", i)
                    dve.tensor_scalar(gated[:, :], logits[:, :], 0.0, None, ALU.max)
                    dve.max(top[:, :], logits[:, :]).then_inc(done["top_values"], 1)
                if attn_tile.inside(B):
                    after(dve, "attn_den", attn_tile)
                    dve.reciprocal(zden[:, :, :], den[:, :, :]).then_inc(done["attn_z"], 1)
                if i.inside(B):
                    dve.tensor_scalar(active[:, :], logits[:, :], 0.0, None, ALU.is_gt)
                    after(dve, "top_values", i)
                    dve.tensor_scalar(gneg[:, :], top[:, 0:1], 0.0, -1.0, ALU.max, ALU.mult
                                      ).then_inc(done["gate_negmax"], 1)
                if attn_tile.inside(B):
                    after(dve, "attn_z", attn_tile)
                    dve.tensor_tensor(attn[:, :].rearrange("p (g h d) -> p g h d", g=G, d=D),
                                      ps_sums[:, :, 0:P].rearrange("p g (h d) -> p g h d", d=D),
                                      zden[:, :, :].unsqueeze(3).broadcast_to([P, G, HG, D]), ALU.mult
                                      ).then_inc(done["attn"], 1)
                if i.inside(B):
                    dve.max_index(top_at[:, :], top[:, :], logits[:, :]).then_inc(done["top_indices"], 1)
                    dve.tensor_scalar(idle[:, :], top[:, 0:1], 0.0, None, ALU.is_le)
                if attn_tile.inside(B):
                    after(dve, "attn", attn_tile)
                    landed_half(dve, h2_stored, attn_tile.shift(-2))
                    dve.tensor_tensor(h2[attn_tile.p][:, :], h[attn_tile.c % 8], attn[:, :], ALU.add
                                      ).then_inc(done["h2"], 1)
                if i.inside(B):
                    after(dve, "top_indices", i)
                    dve.tensor_scalar(is_one[:, :], expert_no[:, :], top_at[:, 0:1], None, ALU.is_equal)
                    dve.tensor_scalar(is_two[:, :], expert_no[:, :], top_at[:, 1:2], None, ALU.is_equal
                                      ).then_inc(done["is_two"], 1)
                if attn_tile.inside(B):
                    after(dve, "h2", attn_tile)
                    dve.bn_stats(stats[:, 2 * i.p + 1, :], h2[attn_tile.p][:, :]).then_inc(done["ln2_stats"], 1)
                if last_tile.inside(B):
                    dve.tensor_copy(pair_in_x[:, bass.ds(last_tile.t, 1), :].rearrange("p o n -> p (o n)"),
                                    position[:, :])
                if attn_tile.inside(B):
                    after(dve, "ln2_stats", attn_tile)
                    if not i.inside(B):
                        carry()
                if i.inside(B):
                    after(dve, "is_two", i)
                    dve.tensor_tensor(top_two[:, :], is_one[:, :], is_two[:, :], ALU.add
                                      ).then_inc(done["top_two"], 1)
                if attn_tile.inside(B):
                    dve.bn_aggr(moments[i.shift(1).p][:, 1, :], stats[:, 2 * i.p + 1, :]
                                ).then_inc(done["ln2_moments"], 1)
                if i.inside(B):
                    after(dve, "top_two", i)
                    dve.scalar_tensor_tensor(gmask[:, :], top_two[:, :].bitcast(F32), idle[:, 0:1], active[:, :],
                                             ALU.mult, ALU.max).then_inc(done["gate_mask"], 1)
                    dve.tensor_tensor(third[:, :], third[:, :], top[:, 2:3], ALU.max)
                    after(dve, "gate_mask", i)
                    after(dve, "gate_exp", i)
                    dve.scalar_tensor_tensor(gsel[:, :], gexp[:, :], 1.0, gmask[:, :], ALU.mult, ALU.mult,
                                             accum_out=gsum[:, 0:1]).then_inc(done["gate_sum"], 1)
                if phi_tile.inside(B):
                    after(dve, "kv_product", phi_tile)
                    dve.tensor_tensor(kvm[:, :, 0:P], ps_kv[:, :, 0:P],
                                      head_mask[:, :].unsqueeze(1).broadcast_to([P, G, P]), ALU.mult)
                    dve.tensor_tensor(kvm[:, :, P:NUMW], ps_kv[:, :, P:P + 1].broadcast_to([P, G, HG]),
                                      head_of_row[:, :].unsqueeze(1).broadcast_to([P, G, HG]), ALU.mult
                                      ).then_inc(done["kv_masked"], 1)
                stats_tile = i.shift(6)
                if i.inside(B):
                    after(dve, "gate_sum", i)
                    dve.reciprocal(gsum[:, 1:2], gsum[:, 0:1]).then_inc(done["gate_rsum"], 1)
                if split_by_vector(i):
                    after(dve, weights_hi, i)
                    dve.tensor_tensor(quarter_of((wq[1], wo[1]), i), like(i, raw[i.p]),
                                      quarter_of((wq[0], wo[0]), i).bitcast(F32), ALU.subtract
                                      ).then_inc(weights_lo, 1)
                if stats_tile.inside(B):
                    landed_quarter(dve, rows_gathered, stats_tile, dmas=2)
                    dve.bn_stats(stats[:, 2 * i.shift(1).p, :], h[stats_tile.c % 8]).then_inc(done["ln1_stats"], 1)
                if i.inside(B):
                    now = routing[:, bass.ds(i.t, 1), :].rearrange("p o e -> p (o e)")
                    after(dve, "gate_rsum", i)
                    dve.tensor_scalar(now, gsel[:, :], gsum[:, 1:2], None, ALU.mult).then_inc(done["routing"], 1)

            run1(dve, step1)

            chain = [0]

            def link(ins):
                chain[0] += 1
                ins.then_inc(table_v, 1)
                dve.wait_ge(table_v, chain[0])

            dve.wait_ge(done["count"], B)
            dve.tensor_copy(fill_i[:, :], next_row[0:1, :]).then_inc(fill_ready, 1)
            link(dve.tensor_tensor(ranks[:, :], next_row[:, :], region_start[:, :], ALU.subtract))
            link(dve.tensor_scalar(tiles_i[:, :], ranks[:, :], float(P - 1), None, ALU.add))
            link(dve.tensor_scalar(tiles_i[:, :], tiles_i[:, :], P.bit_length() - 1, None,
                                   ALU.arith_shift_right))
            link(dve.tensor_copy(tiles_f[:, :], tiles_i[:, :]))
            link(dve.tensor_tensor_scan(tiles_cum[:, :], ones[:, 0:E], tiles_f[:, :], 0.0, ALU.mult, ALU.add))

            def over_tiles(t):
                return t[:, :].unsqueeze(1).broadcast_to([P, 2, E])

            link(dve.tensor_tensor(full[:, 0, :, :], over_tiles(tiles_cum),
                                   tile_no[:, :].unsqueeze(2).broadcast_to([P, 2, E]), ALU.is_le))
            link(dve.tensor_tensor(full[:, 1, :, :], full[:, 0, :, :], over_tiles(tiles_f), ALU.mult))
            link(dve.tensor_reduce(n_full[:, :, :], full[:, :, :, :], AX_X, ALU.add))
            link(dve.scalar_tensor_tensor(tab_tmp[:, 0:2], n_full[:, 1, :], float(-P), tile_row[:, :],
                                          ALU.mult, ALU.add))
            dve.tensor_scalar(tab[:, :, 0], n_full[:, 0, :], float(E - 1), None, ALU.min)
            link(dve.scalar_tensor_tensor(tab[:, :, 1], n_full[:, 0, :], float(REGION), tab_tmp[:, 0:2],
                                          ALU.mult, ALU.add))
            link(dve.tensor_tensor(before[:, :], tiles_cum[:, :], tiles_f[:, :], ALU.subtract))
            link(dve.scalar_tensor_tensor(y_shift[:, :], before[:, :], float(P), region_start[:, :], ALU.mult,
                                          ALU.subtract))
            link(dve.tensor_tensor(y_step[:, 1:E], y_shift[:, 1:E], y_shift[:, 0:E - 1], ALU.subtract))
            dve.wait_ge(table_t, 1)
            link(dve.tensor_reduce(flag_f[:, :], ps_qk[0:1, 0:P], AX_X, ALU.max))
            link(dve.tensor_scalar(flag_i[:, :], flag_f[:, :], 0.0, None, ALU.is_gt))
            dve.wait_ge(table_t, 2)
            link(dve.tensor_copy(tab_i[0:1, :, :].rearrange("p n t -> p (n t)"), ps_x1[0:1, 0:4 * P]))
            dve.sem_inc(tables_ready, 1)

            def sorted_way():
                def step2(i):
                    tile = i.shift(2)
                    if tile.inside(PAIR_TILES):
                        after(dve, "pair_hi", tile)
                        hi, lo = [w[:, :, :].rearrange("p c t -> p (c t)") for w in split[tile.q]]
                        dve.tensor_tensor(lo, ps_turn[tile.p][:, 0:C], hi.bitcast(F32), ALU.subtract
                                          ).then_inc(done["pair_lo"], 1)
                    if i.inside(PAIR_TILES) and not i.p:
                        y_landed(dve, i.shift(-8))
                        after(dve, "pair_copied", i.shift(-1))
                        after(dve, "pair_product", i)
                        dve.tensor_copy(y_buf[i.c % 8 // 4][:, i.q, :], ps_y[i.q][:, 0:Y]
                                        ).then_inc(done["pair_copied"], 1)

                run2(dve, step2)

            def dense_way():
                def token_tile(t, first):
                    now = routing[:, bass.ds(t, 1), :].rearrange("p o e -> p (o e)")
                    if not first:
                        dve.wait_ge(dense_stored, t * 16)
                    dve.wait_ge(dense_loaded, t * 16 + 16)
                    dve.bn_stats(stats[:, 0, :], row_x[:, 1, :]).then_inc(done["dense_stats"], 1)
                    dve.wait_ge(done["dense_stats"], t + 1)
                    dve.tensor_copy(tab_tmp[:, 0:1], ones[:, 0:1])
                    dve.bn_aggr(moments[0][:, 0, :], stats[:, 0, :]).then_inc(done["dense_moments"], 1)
                    dve.wait_ge(done["dense_root"], t + 1)
                    dve.tensor_scalar(row_x[:, 0, :], row_x[:, 1, :], moments[0][:, 0, 0:1], roots[0][:, 0:1],
                                      ALU.subtract, ALU.mult).then_inc(done["dense_x2"], 1)
                    dve.tensor_copy(rwo[0][:, :], now)
                    dve.wait_ge(done["dense_hi"], t + 1)
                    hi, lo = [w[:, :, :].rearrange("p c t -> p (c t)") for w in split[0]]
                    dve.tensor_tensor(lo, ps_turn[0][:, 0:C], hi.bitcast(F32), ALU.subtract
                                      ).then_inc(done["dense_lo"], 1)
                    for e in range(E):
                        if e:
                            dve.wait_ge(dense_added, t * E + e)
                        dve.wait_ge(dense_product, t * E + e + 1)
                        src, acc = ps_y[e % 4][:, 0:Y], row_y[:, 0, :]
                        if e == 0:
                            dve.wait_ge(done["dense_lo"], t + 1)
                            ins = dve.tensor_scalar(acc, src, rwo[0][:, 0:1], None, ALU.mult)
                        else:
                            ins = dve.scalar_tensor_tensor(acc, src, rwo[0][:, e:e + 1], acc, ALU.mult, ALU.add)
                        ins.then_inc(dense_added, 1)

                every_tile(dve, token_tile)

            branch(dve, sorted_way, dense_way)

            def add_slot(tile, s):
                k = DVE_SLOTS.index(s)
                acc = acc_v[tile.p]
                if k == 0:
                    landed_half(dve, h2_loaded, tile)
                product_done(dve, tile, s)
                for j in range(2):
                    if k:
                        added_done(dve, tile, DVE_SLOTS[k - 1], j)
                    src, weight = ps_o[s % len(ps_o)][:, j * C:(j + 1) * C], rwo[tile.p][:, 2 * s + j:2 * s + j + 1]
                    if k == 0 and j == 1:
                        ins = dve.tensor_scalar(acc[1][:, :], src, weight, None, ALU.mult)
                    else:
                        base = acc[j] if k else row_x[:, tile.p, :]
                        ins = dve.scalar_tensor_tensor(acc[j][:, :], src, weight, base[:, :], ALU.mult, ALU.add)
                    ins.then_inc(o_added, 1)

            def step3(i):
                if i.inside(B):
                    add_slot(i, DVE_SLOTS[0])
                tile = i.shift(1)
                if tile.inside(B):
                    after(dve, "probs", tile)
                    dve.reciprocal(psumm[:, 1:2], psumm[:, 0:1]).then_inc(done["probs_rsum"], 1)
                last = i.shift(-1)
                if last.inside(B):
                    added_done(dve, last, DVE_SLOTS[-1])
                    a, b = acc_v[last.p]
                    dve.tensor_tensor(a[:, :], a[:, :], b[:, :], ALU.add).then_inc(done["v_sum"], 1)
                tile = i.shift(1)
                if tile.inside(B):
                    after(dve, "probs_rsum", tile)
                    dve.tensor_scalar(rwo[tile.p][:, :], routing[:, bass.ds(tile.t, 1), :].rearrange(
                        "p o e -> p (o e)"), psumm[:, 1:2], None, ALU.mult).then_inc(done["o_weights"], 1)
                if i.inside(B):
                    add_slot(i, DVE_SLOTS[1])
                tile = i.shift(2)
                if tile.inside(B):
                    after(dve, "probs", tile.shift(-1))
                    after(dve, "scores", tile)
                    dve.tensor_reduce(sneg[:, :], ps_score[:, 0:P], AX_X, ALU.max, negate=True
                                      ).then_inc(done["scores_negmax"], 1)
                tile = i.shift(1)
                if tile.inside(B):
                    after(dve, "aoT_hi", tile)
                    dve.tensor_tensor(aoT[tile.p][1], ps_ao[:, 0:P], aoT[tile.p][0].bitcast(F32), ALU.subtract
                                      ).then_inc(done["aoT_lo"], 1)
                if i.inside(B):
                    add_slot(i, DVE_SLOTS[2])
                if last.inside(B):
                    after(dve, "v_sum", last)
                    pooled_done(dve, last, POOL_SLOTS[-1])
                    landed_half(dve, stored, last.shift(-2))
                    dve.tensor_tensor(row_x[:, 2 + last.p, :], acc_v[last.p][0][:, :], acc_p[last.p][:, :], ALU.add
                                      ).then_inc(done["out_sum"], 1)
                tile = i.shift(3)
                if tile.inside(B):
                    after(dve, "first_row", tile)
                    dve.scalar_tensor_tensor(qkv[tile.q][:, :], row_y[:, 2 * tile.p + 1, :],
                                             pair_w[:, bass.ds(tile.t, 1), 1:2].rearrange("p o n -> p (o n)"),
                                             qkv[tile.q][:, :], ALU.mult, ALU.add).then_inc(done["qkv_sum"], 1)
                if i.inside(B):
                    add_slot(i, DVE_SLOTS[3])
                if i.inside(B):
                    add_slot(i, DVE_SLOTS[4])

            run3(dve, step3)

        @block.tensor
        def _(pe):
            def product(ps, left, right):
                n = len(left[0])
                for c in range(n):
                    pe.matmul(ps, left[1][c], right[0][c], start=(c == 0), stop=False)
                    pe.matmul(ps, left[0][c], right[1][c], start=False, stop=False)
                    last = pe.matmul(ps, left[0][c], right[0][c], start=False, stop=(c == n - 1))
                return last

            def turn(ps, *pieces):
                for n, piece in enumerate(pieces):
                    last = pe.transpose(ps[:, n * P:(n + 1) * P], piece, ident[:, :])
                return last

            def halves(t):
                return [t[:, c * P:(c + 1) * P] for c in range(2)]

            pe.wait_ge(ident_ready, 2)
            pe.wait_ge(setup_v, 1)
            pe.transpose(ps_x1[:, 0:B], ids_rows_f[:, :], ident[0:B, 0:B]).then_inc(setup_t, 1)
            pe.wait_ge(consts_ready, N_CONSTS)
            pe.wait_ge(setup_v, 3)
            for c in range(CH):
                last = pe.matmul(ps_qk[:, 0:E], ones[:, :], sim_sq[:, c, :], start=(c == 0), stop=(c == CH - 1))
            last.then_inc(setup_t, 1)
            pe.wait_ge(attn_loaded, 16)
            pe.wait_ge(setup_a, 3)
            pe.wait_ge(setup_v, 5)

            def step1(i):
                tile = i.shift(2)
                if tile.inside(B):
                    after(pe, "attn", tile.shift(-1))
                    after(pe, "phi_q_T", tile)
                    after(pe, "kv_masked", tile)
                    for g in range(G):
                        last = pe.matmul(ps_sums[:, g, :], pqT[:, g, :], kvm[:, g, :], start=True, stop=True)
                    last.then_inc(done["attn_sums"], 1)
                tile = i.shift(4)
                if tile.inside(B):
                    after(pe, "x1_T", tile.shift(-1))
                    after(pe, "x1_normed", tile)
                    turn(ps_x1, *halves(x1)).then_inc(done["x1_turned"], 1)
                tile = i.shift(1)
                if tile.inside(B):
                    after(pe, "x2_T", tile.shift(-1))
                    after(pe, "x2_normed", tile)
                    turn(ps_x2, *halves(x2[tile.q])).then_inc(done["x2_turned"], 1)
                tile = i.shift(3)
                if tile.inside(B):
                    after(pe, "v_copied", tile)
                    after(pe, "phi_q_T", tile.shift(-1))
                    after(pe, "kv_masked", tile.shift(-1))
                    after(pe, "phi", tile)
                    turn(ps_pq, *halves(phi)).then_inc(done["phi_q_turned"], 1)
                    for g in range(G):
                        last = pe.matmul(ps_kv[:, g, :], phi[:, C + g * P:C + (g + 1) * P], vx[:, g, :],
                                         start=True, stop=True)
                    last.then_inc(done["kv_product"], 1)
                tile = i.shift(1)
                if tile.inside(B):
                    after(pe, "logits", tile.shift(-1))
                    after(pe, "x2_T", tile)
                    if i.j is None and i.c == -1:
                        pe.wait_ge(setup_v, 6)
                    for c in range(CH):
                        last = pe.matmul(ps_gate[:, 0:E], halves(x2T)[c], simn[:, c, :], start=(c == 0),
                                         stop=(c == CH - 1))
                    last.then_inc(done["logits_product"], 1)
                tile = i.shift(4)

                def attn_product(ps, lo, hi, name):
                    pe.matmul(ps[:, 0:hi - lo], ones_r[0:BIAS_ROWS, :], bias[:, lo:hi], start=True, stop=False)
                    for c in range(CH):
                        last = pe.matmul(ps[:, 0:hi - lo], halves(x1T)[c], w_attn[:, c, lo:hi], start=False,
                                         stop=(c == CH - 1))
                    last.then_inc(done[name], 1)

                if tile.inside(B):
                    after(pe, "phi", tile.shift(-1))
                    after(pe, "x1_T", tile)
                    attn_product(ps_qk, 0, 2 * C, "qk_product")
                if i.inside(B):
                    after(pe, "count", i.shift(-1))
                    after(pe, "top_two", i)
                    pe.matmul(ps_rank[:, 0:E], earlier_r[:, :], top_two[:, :], start=True, stop=True)
                    pe.matmul(ps_rank[:, E:2 * E], ones_r[:, :], top_two[:, :], start=True, stop=True
                              ).then_inc(done["rank_product"], 1)
                tile = i.shift(4)
                if tile.inside(B):
                    after(pe, "v_copied", tile.shift(-1))
                    attn_product(ps_v, 2 * C, 3 * C, "v_product")

            run1(pe, step1)

            pe.wait_ge(done["gate_sum"], B)
            pe.transpose(ps_qk[0:1, 0:P], third[:, :], ident[:, :]).then_inc(table_t, 1)
            pe.wait_ge(table_v, 10)
            for n in range(2):
                for g in range(2):
                    last = pe.transpose(ps_x1[0:1, (2 * n + g) * P:(2 * n + g + 1) * P], tab[:, g, n:n + 1],
                                        ident[:, :])
            last.then_inc(table_t, 1)

            def sorted_way():
                pe.wait_ge(weights_lo, 4 * E)
                experts = {}

                def step2(i):
                    if i.inside(PAIR_TILES) and i.q == 0:
                        loaded = nc.values_load_multi_w_load_instructions(
                            tab_i[0:1, 0, bass.ds(i.t, 4)], engines=(pe.engine,), min_val=0, max_val=E - 1)[1]
                        experts.update(enumerate(loaded))
                    tile = i.shift(2)
                    if tile.inside(PAIR_TILES):
                        after(pe, "pair_lo", tile.shift(-2))
                        pe.wait_ge(pair_loaded[tile.c % 8], tile.eighth * 16 + 16)
                        turn(ps_turn[tile.p], *halves(x_buf[tile.c % 8])).then_inc(done["pair_turned"], 1)
                    if i.inside(PAIR_TILES):
                        e = experts[i.q]
                        after(pe, "pair_copied", i.shift(-4))
                        after(pe, "pair_lo", i)
                        product(ps_y[i.q][:, 0:Y], [[w[:, c, :] for c in range(CH)] for w in split[i.q]],
                                [[w[:, bass.ds(e, 1), c, :].rearrange("p e n -> p (e n)") for c in range(CH)]
                                 for w in wq]).then_inc(done["pair_product"], 1)

                run2(pe, step2)

            def dense_way():
                pe.wait_ge(weights_lo, 4 * E)

                def token_tile(t, first):
                    if not first:
                        pe.wait_ge(dense_added, t * E)
                    pe.wait_ge(done["dense_x2"], t + 1)
                    turn(ps_turn[0], *halves(row_x[:, 0, :])).then_inc(done["dense_turned"], 1)
                    for e in range(E):
                        if e >= 4:
                            pe.wait_ge(dense_added, t * E + e - 3)
                        if e == 0:
                            pe.wait_ge(done["dense_lo"], t + 1)
                        product(ps_y[e % 4][:, 0:Y], [[w[:, c, :] for c in range(CH)] for w in split[0]],
                                [[w[:, e, c, :] for c in range(CH)] for w in wq]).then_inc(dense_product, 1)

                every_tile(pe, token_tile)

            branch(pe, sorted_way, dense_way)
            pe.wait_ge(y_ready, 1)

            def bank_before(s):
                n = s - len(ps_o)
                return n % OSLOT, 0 if n >= 0 else 1

            def o_slot(tile, s):
                user, back = bank_before(s)
                (scaled_done if user in POOL_SLOTS else added_done)(pe, tile.shift(-back), user)
                if s == 0:
                    after(pe, "aoT_lo", tile)
                for j in range(2):
                    last = product(ps_o[s % len(ps_o)][:, j * C:(j + 1) * C], [[a] for a in aoT[tile.p]],
                                   [[w[:, 2 * s + j, :]] for w in wo])
                last.then_inc(o_product, 1)

            def step3(i):
                def slots(*numbers):
                    if i.inside(B):
                        for s in numbers:
                            o_slot(i, s)

                slots(0)
                tile = i.shift(2)
                if tile.inside(B):
                    after(pe, "heads_T", tile.shift(-1))
                    after(pe, "qkv_sum", tile)
                    turn(ps_heads, *halves(qkv[tile.q])).then_inc(done["heads_turned"], 1)
                tile = i.shift(1)
                if tile.inside(B):
                    after(pe, "probs_T", tile.shift(-1))
                    after(pe, "probs", tile)
                    turn(ps_prob, pr[:, :]).then_inc(done["probs_turned"], 1)
                slots(1)
                tile = i.shift(1)
                if tile.inside(B):
                    after(pe, "aoT_lo", tile.shift(-1))
                    after(pe, "probs_T", tile)
                    pe.matmul(ps_ao[:, 0:P], qkv[tile.q][:, 2 * HD:3 * HD], prT[:, :], start=True, stop=True
                              ).then_inc(done["ao_product"], 1)
                slots(2)
                tile = i.shift(2)
                if tile.inside(B):
                    after(pe, "probs", tile.shift(-1))
                    after(pe, "heads_T", tile)
                    pe.matmul(ps_score[:, 0:P], headsT[:, 0, :], headsT[:, 1, :], start=True, stop=False)
                    pe.matmul(ps_score[:, 0:P], ident_r[:, :], causal_r[:, :], start=False, stop=True
                              ).then_inc(done["scores"], 1)
                slots(3, 4, 5, 6, 7)

            run3(pe, step3)


_INS = ["x", "L0_tok_token_table", "L0_tok_op_table", "L0_tok_var_table", "L0_tok_const_table",
        "L0_tok_struct_table", "L0_tok_special_table", "L0_attn_W_qkv", "L0_attn_b_qkv", "L0_attn_W_proj",
        "L0_attn_b_proj", "L0_ffn_sim_matrix", "L0_ffn_gates", "L0_ffn_q_proj", "L0_ffn_k_proj",
        "L0_ffn_v_proj", "L0_ffn_o_proj"]


def kernel(**inputs):
    import numpy as _np
    import concourse.bacc as _bacc
    from concourse import mybir as _mybir
    from concourse.bass_utils import run_bass_kernel_spmd as _run

    nc = _bacc.Bacc("TRN2", target_bir_lowering=False, num_devices=1)
    arrays, args = {}, []
    for name in _INS:
        a = _np.ascontiguousarray(inputs[name])
        arrays[f"in_{name}"] = a
        args.append(nc.dram_tensor(f"in_{name}", a.shape, _mybir.dt.from_np(a.dtype), kind="ExternalInput").ap())
    b, t = inputs["x"].shape
    c = 2 * inputs["L0_tok_token_table"].shape[1]
    args.append(nc.dram_tensor("out_h", (b, t, c), _mybir.dt.float32, kind="ExternalOutput").ap())
    build(nc, *args)
    r = _run(nc, [arrays], core_ids=[0])
    return r.results[0]["out_h"]
```
